# Optimizing a Trainium2 kernel written in Bass

```python
import numpy as np
import jax
import jax.numpy as jnp

def _softmax(x, axis=-1):
    return jax.nn.softmax(x, axis=axis)

def _gelu(x):
    return jax.nn.gelu(x, approximate=True)

def _silu(x):
    return jax.nn.silu(x)

def _sigmoid(x):
    return jax.nn.sigmoid(x)

def _layernorm(x, axis=-1, eps=1e-05):
    m = jnp.mean(x, axis=axis, keepdims=True)
    v = jnp.var(x, axis=axis, keepdims=True)
    return (x - m) / jnp.sqrt(v + eps)

def _scatter_add(tgt, idx, src, axis=0):
    return tgt.at[idx].add(src)

def _segment_sum(src, seg, n):
    return jax.ops.segment_sum(src, seg, n)
kernel_name = 'mk_vit_tower_cls_d2_tok_img1024_r4_d2a70d'

def setup_inputs(seed: int=0):
    np.random.seed(seed)
    _w = jnp.asarray

    def _rec_inputs():
        import jax
        import jax.numpy as jnp
        _rk = jax.random.key(seed)
        x = -0.000348323 + 0.999952 * jax.random.normal(jax.random.fold_in(_rk, 1), (32, 3, 84, 84), jnp.float32)
        cls_tok = 0.02 * jax.random.normal(jax.random.fold_in(_rk, 5), (1, 1, 256), jnp.float32)
        return (x, cls_tok)
    x, cls_tok = _rec_inputs()

    def _L0_tok_setup():
        import jax, jax.numpy as jnp
        import numpy as np
        from jax import lax
        PATCH = 16
        key = jax.random.key(seed)
        k1, k2 = jax.random.split(key)
        B, C, IMG, HID = (32, 3, 96, 256)
        inputs = jax.random.normal(k1, (B, C, IMG, IMG), dtype=jnp.float32)
        flat = C * PATCH * PATCH
        W = jax.random.normal(k2, (flat, HID), dtype=jnp.float32) / np.sqrt(flat)
        return {'inputs': inputs, 'W': W}
    _L0_tok_all = _L0_tok_setup()
    _L0_tok_in = {k: v for k, v in _L0_tok_all.items() if k in ('W',)}
    del _L0_tok_all

    def _L0_attn_setup():
        import jax, jax.numpy as jnp
        import numpy as np
        D = 256
        key = jax.random.key(seed)
        ks = jax.random.split(key, 9)
        s = 1.0 / np.sqrt(D)
        x = jax.random.normal(ks[0], (1024, 8, D), dtype=jnp.float32)
        Wq = jax.random.uniform(ks[1], (D, D), jnp.float32, -s, s)
        bq = jax.random.uniform(ks[2], (D,), jnp.float32, -s, s)
        Wk = jax.random.uniform(ks[3], (D, D), jnp.float32, -s, s)
        bk = jax.random.uniform(ks[4], (D,), jnp.float32, -s, s)
        Wv = jax.random.uniform(ks[5], (D, D), jnp.float32, -s, s)
        bv = jax.random.uniform(ks[6], (D,), jnp.float32, -s, s)
        Wo = jax.random.uniform(ks[7], (D, D), jnp.float32, -s, s)
        bo = jax.random.uniform(ks[8], (D,), jnp.float32, -s, s)
        return {'x': x, 'Wq': Wq, 'bq': bq, 'Wk': Wk, 'bk': bk, 'Wv': Wv, 'bv': bv, 'Wo': Wo, 'bo': bo}
    _L0_attn_all = _L0_attn_setup()
    _L0_attn_in = {k: v for k, v in _L0_attn_all.items() if k in ('Wq', 'bq', 'Wk', 'bk', 'Wv', 'bv', 'Wo', 'bo')}
    del _L0_attn_all

    def _L0_ffn_setup():
        import jax, jax.numpy as jnp
        import numpy as np
        MICRO_BATCHES = 2
        TOP_K = 2
        NUM_EXPERTS = 8
        B, S, D = (4, 1024, 256)
        H = 4 * D
        key = jax.random.key(seed)
        ks = jax.random.split(key, 8)
        s = 0.02
        return {'x': jax.random.normal(ks[0], (B, S, D), jnp.float32), 'ln_scale': jnp.ones((D,), jnp.float32), 'ln_bias': jnp.zeros((D,), jnp.float32), 'attn_w': jax.random.normal(ks[1], (D, D), jnp.float32) * s, 'attn_b': jnp.zeros((D,), jnp.float32), 'gate_w': jax.random.normal(ks[2], (NUM_EXPERTS, D), jnp.float32) * s, 'w1': jax.random.normal(ks[3], (NUM_EXPERTS, D, H), jnp.float32) * s, 'b1': jnp.zeros((NUM_EXPERTS, H), jnp.float32), 'w2': jax.random.normal(ks[4], (NUM_EXPERTS, H, D), jnp.float32) * s, 'b2': jnp.zeros((NUM_EXPERTS, D), jnp.float32), 'next_w': jax.random.normal(ks[5], (D, D), jnp.float32) * s, 'next_b': jnp.zeros((D,), jnp.float32)}
    _L0_ffn_all = _L0_ffn_setup()
    _L0_ffn_in = {k: v for k, v in _L0_ffn_all.items() if k in ('ln_scale', 'ln_bias', 'attn_w', 'attn_b', 'gate_w', 'w1', 'b1', 'w2', 'b2', 'next_w', 'next_b')}
    del _L0_ffn_all

    def _L1_attn_setup():
        import jax, jax.numpy as jnp
        import numpy as np
        NUM_HEADS = 16
        EMBED_DIM = 256

        def _linear_attention(x, Wq, bq, Wk, bk, Wv, bv, Wo, bo):
            B, S, D = x.shape
            H = NUM_HEADS
            hd = D // H
            v = (x @ Wv + bv).reshape(B, S, H, hd)
            q = (x @ Wq + bq).reshape(B, S, H, hd)
            k = (x @ Wk + bk).reshape(B, S, H, hd)
            q = jax.nn.elu(q) + 1.0
            k = jax.nn.elu(k) + 1.0
            qT = q.transpose(1, 0, 2, 3)
            kT = k.transpose(1, 0, 2, 3)
            vT = v.transpose(1, 0, 2, 3)
            s0 = jnp.zeros((B, H, hd, hd), dtype=x.dtype)
            z0 = jnp.zeros((B, H, hd), dtype=x.dtype)

            def step(carry, qkv):
                s, z = carry
                q_i, k_i, v_i = qkv
                s = s + jnp.einsum('bhd,bhm->bhdm', k_i, v_i)
                z = z + k_i
                qs = jnp.einsum('bhd,bhdm->bhm', q_i, s)
                qz = jnp.einsum('bhd,bhd->bh', q_i, z)[..., None]
                return ((s, z), qs / (qz + 1e-06))
            (_, _), values = jax.lax.scan(step, (s0, z0), (qT, kT, vT))
            values = values.transpose(1, 0, 2, 3).reshape(B, S, D)
            return values @ Wo + bo
        key = jax.random.key(seed)
        ks = jax.random.split(key, 6)
        B, S, D = (4, 512, EMBED_DIM)
        sc = 1.0 / np.sqrt(D)
        return {'x': jax.random.normal(ks[0], (B, S, D), dtype=jnp.float32), 'mask': jnp.ones((B, S), dtype=jnp.int32), 'Wq': jax.random.normal(ks[1], (D, D), dtype=jnp.float32) * sc, 'bq': jnp.zeros((D,), dtype=jnp.float32), 'Wk': jax.random.normal(ks[2], (D, D), dtype=jnp.float32) * sc, 'bk': jnp.zeros((D,), dtype=jnp.float32), 'Wv': jax.random.normal(ks[3], (D, D), dtype=jnp.float32) * sc, 'bv': jnp.zeros((D,), dtype=jnp.float32), 'Wo': jax.random.normal(ks[4], (D, D), dtype=jnp.float32) * sc, 'bo': jnp.zeros((D,), dtype=jnp.float32)}
    _L1_attn_all = _L1_attn_setup()
    _L1_attn_in = {k: v for k, v in _L1_attn_all.items() if k in ('mask', 'Wq', 'bq', 'Wk', 'bk', 'Wv', 'bv', 'Wo', 'bo')}
    del _L1_attn_all

    def _L1_ffn_setup():
        import jax, jax.numpy as jnp
        import numpy as np
        H = 256
        I = 512
        E = 32
        B, S = (4, 512)

        def _grouped_mm(a, w, group_sizes):
            return jax.lax.ragged_dot(a, w, group_sizes)

        def _swiglu(x, gw, uw, dw):
            return jax.nn.silu(x @ gw) * (x @ uw) @ dw
        key = jax.random.key(seed)
        ks = jax.random.split(key, 8)
        scale = 0.02
        inp = {'hidden_states': jax.random.normal(ks[0], (B, S, H), dtype=jnp.float32), 'gate_w': jax.random.normal(ks[1], (H, E), dtype=jnp.float32) * scale, 'shared_gate_w': jax.random.normal(ks[2], (H, I), dtype=jnp.float32) * scale, 'shared_up_w': jax.random.normal(ks[3], (H, I), dtype=jnp.float32) * scale, 'shared_down_w': jax.random.normal(ks[4], (I, H), dtype=jnp.float32) * scale, 'routed_gate_w': jax.random.normal(ks[5], (E, H, I), dtype=jnp.float32) * scale, 'routed_up_w': jax.random.normal(ks[6], (E, H, I), dtype=jnp.float32) * scale, 'routed_down_w': jax.random.normal(ks[7], (E, I, H), dtype=jnp.float32) * scale}
        return inp
    _L1_ffn_all = _L1_ffn_setup()
    _L1_ffn_in = {k: v for k, v in _L1_ffn_all.items() if k in ('gate_w', 'shared_gate_w', 'shared_up_w', 'shared_down_w', 'routed_gate_w', 'routed_up_w', 'routed_down_w')}
    del _L1_ffn_all
    return {'x': x, 'cls_tok': cls_tok, 'L0_tok_W': _L0_tok_in['W'], 'L0_attn_Wq': _L0_attn_in['Wq'], 'L0_attn_bq': _L0_attn_in['bq'], 'L0_attn_Wk': _L0_attn_in['Wk'], 'L0_attn_bk': _L0_attn_in['bk'], 'L0_attn_Wv': _L0_attn_in['Wv'], 'L0_attn_bv': _L0_attn_in['bv'], 'L0_attn_Wo': _L0_attn_in['Wo'], 'L0_attn_bo': _L0_attn_in['bo'], 'L0_ffn_ln_scale': _L0_ffn_in['ln_scale'], 'L0_ffn_ln_bias': _L0_ffn_in['ln_bias'], 'L0_ffn_attn_w': _L0_ffn_in['attn_w'], 'L0_ffn_attn_b': _L0_ffn_in['attn_b'], 'L0_ffn_gate_w': _L0_ffn_in['gate_w'], 'L0_ffn_w1': _L0_ffn_in['w1'], 'L0_ffn_b1': _L0_ffn_in['b1'], 'L0_ffn_w2': _L0_ffn_in['w2'], 'L0_ffn_b2': _L0_ffn_in['b2'], 'L0_ffn_next_w': _L0_ffn_in['next_w'], 'L0_ffn_next_b': _L0_ffn_in['next_b'], 'L1_attn_mask': _L1_attn_in['mask'], 'L1_attn_Wq': _L1_attn_in['Wq'], 'L1_attn_bq': _L1_attn_in['bq'], 'L1_attn_Wk': _L1_attn_in['Wk'], 'L1_attn_bk': _L1_attn_in['bk'], 'L1_attn_Wv': _L1_attn_in['Wv'], 'L1_attn_bv': _L1_attn_in['bv'], 'L1_attn_Wo': _L1_attn_in['Wo'], 'L1_attn_bo': _L1_attn_in['bo'], 'L1_ffn_gate_w': _L1_ffn_in['gate_w'], 'L1_ffn_shared_gate_w': _L1_ffn_in['shared_gate_w'], 'L1_ffn_shared_up_w': _L1_ffn_in['shared_up_w'], 'L1_ffn_shared_down_w': _L1_ffn_in['shared_down_w'], 'L1_ffn_routed_gate_w': _L1_ffn_in['routed_gate_w'], 'L1_ffn_routed_up_w': _L1_ffn_in['routed_up_w'], 'L1_ffn_routed_down_w': _L1_ffn_in['routed_down_w']}

def reference(x, cls_tok, L0_tok_W, L0_attn_Wq, L0_attn_bq, L0_attn_Wk, L0_attn_bk, L0_attn_Wv, L0_attn_bv, L0_attn_Wo, L0_attn_bo, L0_ffn_ln_scale, L0_ffn_ln_bias, L0_ffn_attn_w, L0_ffn_attn_b, L0_ffn_gate_w, L0_ffn_w1, L0_ffn_b1, L0_ffn_w2, L0_ffn_b2, L0_ffn_next_w, L0_ffn_next_b, L1_attn_mask, L1_attn_Wq, L1_attn_bq, L1_attn_Wk, L1_attn_bk, L1_attn_Wv, L1_attn_bv, L1_attn_Wo, L1_attn_bo, L1_ffn_gate_w, L1_ffn_shared_gate_w, L1_ffn_shared_up_w, L1_ffn_shared_down_w, L1_ffn_routed_gate_w, L1_ffn_routed_up_w, L1_ffn_routed_down_w):
    import jax
    import jax.numpy as jnp

    def _L0_tok_ref(inputs, W):
        import jax, jax.numpy as jnp
        import numpy as np
        from jax import lax
        PATCH = 16
        B, C, H, Wimg = inputs.shape
        patches = lax.conv_general_dilated_patches(inputs, filter_shape=[PATCH, PATCH], window_strides=[PATCH, PATCH], padding='VALID', dimension_numbers=('NCHW', 'HWIO', 'NCHW'))
        patches = patches.reshape(B, -1, C * PATCH * PATCH)
        return jnp.einsum('bnf,fh->bnh', patches, W)

    def _L0_attn_ref(x, Wq, bq, Wk, bk, Wv, bv, Wo, bo):
        import jax, jax.numpy as jnp
        import numpy as np
        D = 256
        Q = jax.nn.elu(x @ Wq.T + bq) + 1.0
        K = jax.nn.elu(x @ Wk.T + bk) + 1.0
        V = x @ Wv.T + bv
        KV = jnp.einsum('sbd,sbe->bde', K, V)
        out = jnp.einsum('sbd,bde->sbe', Q, KV)
        return out @ Wo.T + bo

    def _L0_ffn_ref(x, ln_scale, ln_bias, attn_w, attn_b, gate_w, w1, b1, w2, b2, next_w, next_b):
        import jax, jax.numpy as jnp
        import numpy as np
        MICRO_BATCHES = 2
        TOP_K = 2
        NUM_EXPERTS = 8
        B, S, D = (4, 1024, 256)
        H = 4 * D
        b, s, d = x.shape
        flat = x.reshape(b * s, d)
        mu = jnp.mean(flat, axis=-1, keepdims=True)
        var = jnp.mean((flat - mu) ** 2, axis=-1, keepdims=True)
        xn = (flat - mu) * jax.lax.rsqrt(var + 1e-05) * ln_scale + ln_bias
        x_attn = xn @ attn_w.T + attn_b + flat
        logits = x_attn @ gate_w.T
        _vals, _idx = jax.lax.top_k(logits, TOP_K)
        e = w1.shape[0]
        n = b * s // (MICRO_BATCHES * e)
        xe = x_attn.reshape(MICRO_BATCHES, e, n, d)
        h = jax.nn.gelu(jnp.einsum('mend,edh->menh', xe, w1) + b1[None, :, None, :], approximate=False)
        eo = jnp.einsum('menh,ehd->mend', h, w2) + b2[None, :, None, :]
        eo = eo.reshape(b * s, d)
        out = jax.nn.gelu(eo @ next_w.T + next_b, approximate=False)
        return out.reshape(b, s, d)

    def _L1_attn_ref(x, mask, Wq, bq, Wk, bk, Wv, bv, Wo, bo):
        import jax, jax.numpy as jnp
        import numpy as np
        NUM_HEADS = 16
        EMBED_DIM = 256

        def _linear_attention(x, Wq, bq, Wk, bk, Wv, bv, Wo, bo):
            B, S, D = x.shape
            H = NUM_HEADS
            hd = D // H
            v = (x @ Wv + bv).reshape(B, S, H, hd)
            q = (x @ Wq + bq).reshape(B, S, H, hd)
            k = (x @ Wk + bk).reshape(B, S, H, hd)
            q = jax.nn.elu(q) + 1.0
            k = jax.nn.elu(k) + 1.0
            qT = q.transpose(1, 0, 2, 3)
            kT = k.transpose(1, 0, 2, 3)
            vT = v.transpose(1, 0, 2, 3)
            s0 = jnp.zeros((B, H, hd, hd), dtype=x.dtype)
            z0 = jnp.zeros((B, H, hd), dtype=x.dtype)

            def step(carry, qkv):
                s, z = carry
                q_i, k_i, v_i = qkv
                s = s + jnp.einsum('bhd,bhm->bhdm', k_i, v_i)
                z = z + k_i
                qs = jnp.einsum('bhd,bhdm->bhm', q_i, s)
                qz = jnp.einsum('bhd,bhd->bh', q_i, z)[..., None]
                return ((s, z), qs / (qz + 1e-06))
            (_, _), values = jax.lax.scan(step, (s0, z0), (qT, kT, vT))
            values = values.transpose(1, 0, 2, 3).reshape(B, S, D)
            return values @ Wo + bo
        return _linear_attention(x, Wq, bq, Wk, bk, Wv, bv, Wo, bo)

    def _L1_ffn_ref(hidden_states, gate_w, shared_gate_w, shared_up_w, shared_down_w, routed_gate_w, routed_up_w, routed_down_w):
        import jax, jax.numpy as jnp
        import numpy as np
        H = 256
        I = 512
        E = 32
        B, S = (4, 512)

        def _grouped_mm(a, w, group_sizes):
            return jax.lax.ragged_dot(a, w, group_sizes)

        def _swiglu(x, gw, uw, dw):
            return jax.nn.silu(x @ gw) * (x @ uw) @ dw
        b, s, h = hidden_states.shape
        x = hidden_states.reshape(-1, h)
        shared_out = _swiglu(x, shared_gate_w, shared_up_w, shared_down_w)
        logits = x @ gate_w
        topk_ids = jnp.argmax(logits, axis=-1)
        topk_val = jnp.max(logits, axis=-1)
        scores = jax.nn.sigmoid(topk_val)[:, None]
        xs = x * scores
        tokens_per_expert = jnp.zeros((E,), jnp.int32).at[topk_ids].add(1)
        order = jnp.argsort(topk_ids)
        sorted_x = xs[order]
        g = _grouped_mm(sorted_x, routed_gate_w, tokens_per_expert)
        u = _grouped_mm(sorted_x, routed_up_w, tokens_per_expert)
        d = _grouped_mm(jax.nn.silu(g) * u, routed_down_w, tokens_per_expert)
        inv = jnp.argsort(order)
        routed_out = d[inv]
        return (shared_out + routed_out).reshape(b, s, h)
    h = _L0_tok_ref(x, L0_tok_W)
    h = jnp.concatenate([jnp.broadcast_to(cls_tok, (h.shape[0], 1, h.shape[2])), h], axis=1)
    h = h + _L0_attn_ref(_layernorm(h, axis=-1), L0_attn_Wq, L0_attn_bq, L0_attn_Wk, L0_attn_bk, L0_attn_Wv, L0_attn_bv, L0_attn_Wo, L0_attn_bo)
    h = h + _L0_ffn_ref(_layernorm(h, axis=-1), L0_ffn_ln_scale, L0_ffn_ln_bias, L0_ffn_attn_w, L0_ffn_attn_b, L0_ffn_gate_w, L0_ffn_w1, L0_ffn_b1, L0_ffn_w2, L0_ffn_b2, L0_ffn_next_w, L0_ffn_next_b)
    h = h + _L1_attn_ref(_layernorm(h, axis=-1), L1_attn_mask, L1_attn_Wq, L1_attn_bq, L1_attn_Wk, L1_attn_bk, L1_attn_Wv, L1_attn_bv, L1_attn_Wo, L1_attn_bo)
    h = h + _L1_ffn_ref(_layernorm(h, axis=-1), L1_ffn_gate_w, L1_ffn_shared_gate_w, L1_ffn_shared_up_w, L1_ffn_shared_down_w, L1_ffn_routed_gate_w, L1_ffn_routed_up_w, L1_ffn_routed_down_w)
    return h

_drawn_inputs = setup_inputs


def setup_inputs(seed=0):
    import zlib

    import numpy as np

    out = dict(_drawn_inputs(seed))
    spreads = {'L0_ffn_ln_scale': (1.0, 0.6),
     'L0_ffn_ln_bias': (0.0, 0.8),
     'L0_ffn_attn_b': (0.0, 2.0),
     'L0_ffn_b1': (0.0, 2.0),
     'L0_ffn_b2': (0.0, 2.0),
     'L0_ffn_next_b': (0.0, 2.0),
     'L1_attn_bq': (0.0, 2.0),
     'L1_attn_bk': (0.0, 2.0),
     'L1_attn_bv': (0.0, 2.0),
     'L1_attn_bo': (0.0, 2.0)}
    factors = {'L0_attn_bq': 42.212,
     'L0_attn_bk': 64.0,
     'L0_attn_bo': 64.0,
     'L0_ffn_attn_w': 8.0,
     'L0_ffn_w1': 8.0,
     'L0_ffn_w2': 8.0,
     'L0_ffn_next_w': 8.0,
     'L1_attn_Wq': 55.3,
     'L1_attn_Wk': 43.517,
     'L1_attn_Wv': 8.0,
     'L1_attn_Wo': 8.0,
     'L1_ffn_gate_w': 29.301,
     'L1_ffn_shared_gate_w': 33.053,
     'L1_ffn_shared_up_w': 29.321,
     'L1_ffn_shared_down_w': 28.955,
     'L1_ffn_routed_gate_w': 33.053,
     'L1_ffn_routed_up_w': 28.785,
     'L1_ffn_routed_down_w': 29.312}
    for name, (base, spread) in spreads.items():
        noise = np.random.default_rng([zlib.crc32(name.encode()), seed]).standard_normal(out[name].shape)
        drawn = base * np.exp(spread * noise) if base else spread * noise
        out[name] = jnp.asarray(drawn.astype(out[name].dtype))
    for name, factor in factors.items():
        out[name] = (out[name] * factor).astype(out[name].dtype)
    return out
```

```python
from contextlib import ExitStack

import numpy as np
import concourse.bass as bass
from concourse import mybir

F32 = mybir.dt.float32
BF16 = mybir.dt.bfloat16
I32 = mybir.dt.int32
ALU = mybir.AluOpType
ACT = mybir.ActivationFunctionType
AX = mybir.AxisListType

IMAGES, POSITIONS, D = 32, 26, 256
TOKENS = IMAGES * POSITIONS
GROUPS = 8
GT = TOKENS // GROUPS
GI = IMAGES // GROUPS
DC = D // 128
FC = 6
HIDDEN = 1024
HC = HIDDEN // 128
INNER = 512
IC = INNER // 128
EXPERTS = 32
HEADS, HD = 16, 16
HPAD = 32
EPS = 1e-5
HALF = TOKENS // 2
PT = 4 * IMAGES
PTILES = 7
BLOCK = 128
UNROLL = 4
MAX_BLOCKS = 40
SORTED = TOKENS + BLOCK

BQ0, BK0, LNS, LNB, AB, BQ1, BK1, B2, B1 = 0, 2, 4, 6, 8, 10, 12, 14, 30
EVEN, ODD = B1 + GROUPS * HC, B1 + GROUPS * HC + 1
NBCOL = ODD + 1
BV0, BO0, NXB, BV1, BO1 = range(5)
C_IOTA, C_K, C_128, C_QUAD, C_128K = 0, 32, 32 + 1280, 32 + 1280 + 224, 32 + 1280 + 224 + 10
NROUTE = C_128K + MAX_BLOCKS


def tower(nc, patches, cls, tokw, w0, wx, w1a, w1o, gate, shared, experts0, experts1, bcol, brow,
          ident_in, masks_in, tri_in, route_in, out):
    sorted_x = nc.dram_tensor("sorted_x", (SORTED, D), F32, kind="Internal").ap()
    sorted_y = nc.dram_tensor("sorted_y", (SORTED, D), F32, kind="Internal").ap()

    with ExitStack() as ctx:
        def sb(name, shape, dt=F32):
            return ctx.enter_context(nc.sbuf_tensor(name, shape, dt))

        def sem(name):
            return ctx.enter_context(nc.semaphore(name))

        ring = sb("ring", [128, 4, 4096])
        pat = sb("pat", [128, GROUPS, FC * GT])
        vpad = pat[:, :, 0:HEADS * HPAD].rearrange("p g (h m) -> p g h m", m=HPAD)
        kz = sb("kz", [128, DC, TOKENS])
        tokw_s = kz[:, :, :].rearrange("p c t -> p (c t)")[:, 0:FC * D].rearrange("p (c n) -> p c n", c=FC)
        w0_s = sb("w0_s", [128, 4, DC, D])
        wx_s = sb("wx_s", [128, 2, DC, D])
        wl1 = sb("wl1", [128, 2 * MAX_BLOCKS * EXPERTS])
        w1_s = wl1[:, 0:3 * DC * D].rearrange("p (w c n) -> p w c n", w=3, c=DC)
        w1o_s = wl1[:, 3 * DC * D:3 * DC * D + 4 * D].rearrange("p (c n) -> p c n", c=4)
        tmat = wl1[0:1, :].rearrange("p (a n) -> p a n", a=2)
        gate_s = sb("gate_s", [128, DC, EXPERTS])
        shared_s = sb("shared_s", [128, 2 * DC * INNER + IC * D])
        sgw = shared_s[:, 0:DC * INNER].rearrange("p (c n) -> p c n", c=DC)
        suw = shared_s[:, DC * INNER:2 * DC * INNER].rearrange("p (c n) -> p c n", c=DC)
        sdw = shared_s[:, 2 * DC * INNER:].rearrange("p (c n) -> p c n", c=IC)
        bcol_s = sb("bcol_s", [128, NBCOL])
        brow_s = sb("brow_s", [128, 5, D])
        ident = sb("ident", [128, 128])
        masks = sb("masks", [128, 128 + GT])
        tri = sb("tri", [GT, GT + 128], BF16)
        route = w0_s[:, :, :, :].rearrange("p w c n -> p (w c n)")[:, 0:NROUTE]
        h = sb("h", [GT, GROUPS, D])
        xA = sb("xA", [128, DC, TOKENS])
        qT = sb("qT", [128, DC, TOKENS])
        kT = sb("kT", [128, DC, TOKENS])
        q1, kE, kO = qT, kT, xA
        vrow = sb("vrow", [128, GROUPS, D])
        x3 = vrow
        oT = sb("oT", [128, DC, TOKENS])
        x3T = oT
        eA = sb("eA", [128, 2, HALF])
        fhT = sb("fhT", [128, HC, GT])
        zA = fhT[:, :, :].rearrange("p c t -> p (c t)").rearrange("p (a n) -> p a n", a=2)
        S = sb("S", [128, 2, HEADS * GT])
        hidT = S[:, :, :].rearrange("p a n -> p (a n)").rearrange("p (c n) -> p c n", c=IC)
        attA = S[:, 0, 0:2 * PT].rearrange("p (a n) -> p a n", a=2)
        clsbuf = S[0:GT, 1, 0:D]
        zrow = S[:, 1, D:2 * D]
        xr = sb("xr", [GT, 2, D])
        xr2 = sb("xr2", [GT, 2, D])
        st = sb("st", [GT, 6])
        mv = sb("mv", [GT, 2])
        var = sb("var", [GT, 1])
        rstd = sb("rstd", [GT, 1])
        slot_seen = sb("slot_seen", [1, 1])
        mhalf = sb("mhalf", [GT, 1])
        cols5 = sb("cols5", [128, 5, DC, GT])
        nT, n2T, xaT, eoT, x2T = (cols5[:, i, :, :] for i in range(5))
        flat5 = cols5[:, :, :, :].rearrange("p a c t -> p (a c t)")
        rden = flat5[:, 0:HALF]
        valT = flat5[:, HALF:2 * HALF].rearrange("p (a t) -> p a t", a=4)
        nxr = sb("nxr", [GT, D])
        flate = eA[:, :, :].rearrange("p a n -> p (a n)")
        big = flate[0:GT, 0:256].rearrange("p (g e) -> p g e", e=EXPERTS)
        onehot = flate[0:GT, 256:512].rearrange("p (g e) -> p g e", e=EXPERTS)
        before = flate[:, 512:512 + (GROUPS + 1) * EXPERTS].rearrange("p (g e) -> p g e", e=EXPERTS)
        onehot_b = sb("onehot_b", [GT, GROUPS, EXPERTS], BF16)
        lgm = sb("lgm", [GT, 4 * GROUPS])
        slot_i = sb("slot_i", [GT, GROUPS], I32)
        rt = sb("rt", [128, 8, EXPERTS])
        ones32 = sb("ones32", [GT, 32])
        table = sb("table", [1, 2 * MAX_BLOCKS + 1], I32)
        tfl = sb("tfl", [1, 2, MAX_BLOCKS])
        xs = sb("xs", [GT, 2, D])
        xw = xA[:, :, :].rearrange("p c t -> p (c t)")[:, 0:UNROLL * D].rearrange("p (u d) -> p u d", u=UNROLL)
        xwT = kT[:, :, :].rearrange("p c t -> p (c t)")[:, 0:UNROLL * D].rearrange("p (u c t) -> p u c t", u=UNROLL, c=DC)
        sg = S[:, :, :].rearrange("p a n -> p (a n)")[:, 0:2 * INNER].rearrange("p (u n) -> p u n", u=2)
        hw = S[:, :, :].rearrange("p a n -> p (a n)")[:, 2 * INNER:4 * INNER].rearrange("p (u n) -> p u n", u=2)
        yw = qT[:, :, :].rearrange("p c t -> p (c t)")[:, 0:UNROLL * D].rearrange("p (u d) -> p u d", u=UNROLL)
        back = pat[:, :, :].rearrange("p g n -> p (g n)")[:, 0:GROUPS * D].rearrange("p (g d) -> p g d", d=D)

        P = [ctx.enter_context(nc.psum_tensor(f"P{i}", [128, 512], F32)) for i in range(8)]

        names = ("consts cls_in pat_in tokw_in w0_in wx_in w1_in gate_in shared_in bias_in brow_in route_in "
                 "zeroed cls_zero vpad_zero vec var_ready rstd_ready "
                 "tok_done h0_ready trA_done xA_ready "
                 "qk0_done z0_sum z0_ready exp0_done qk0_ready v0_done v0_ready att_done att_ready oT_done oT_ready "
                 "wo_done n_ready wo_read tr1_done nT_ready n2T_ready xa_done xaT_ready up_done gelu_done down_done eoT_ready "
                 "nx_done nx_sum nx_gelu x2_ready tr2_done x2T_ready qk1_done z1_ready v1_done v1_ready "
                 "m1_ready exp1_done q1_ready k1_ready sc_done sc_ready av_done val_ready wo1_done x3_ready tr3_done x3T_ready lg_done "
                 "onehot_ready prefix_done score_ready topv_ready slot_ready table_ready xs_ready scattered "
                 "sg_done silu0_done hid_ready sd_done h_final "
                 "xwt_done xwT_ready gu_done silu_done hw_ready dn_done yw_ready written all_written gathered out_ready stored").split()
        s = {n: sem(n) for n in names}
        ring_in = [sem(f"ring_in{i}") for i in range(4)]
        block_in = [sem(f"block_in{i}") for i in range(4)]
        window_in = [sem(f"window_in{i}") for i in range(4)]
        pat_in = [sem(f"pat_in{i}") for i in range(4)]
        xs_sent = [sem(f"xs_sent{i}") for i in range(2)]
        rows_back = [sem(f"rows_back{i}") for i in range(GROUPS)]

        def gcol(g):
            return slice(g * GT, (g + 1) * GT)

        def bank(b, *shape):
            n = int(np.prod(shape))
            if len(shape) == 1:
                return P[b][:, 0:n]
            return P[b][:, 0:n].rearrange("p (a n) -> p a n", a=shape[0])

        def ptile(i):
            n = min(PT, TOKENS - i * PT)
            return slice(i * PT, i * PT + n), n

        def lagged(steps, stages):
            for t in range(steps):
                for stage, lag in stages:
                    if 0 <= t - lag < GROUPS:
                        stage(t - lag)

        block = ctx.enter_context(nc.Block())

        @block.sync
        def _(sp):
            sp.dma_start(ident[:, :], ident_in).then_inc(s["consts"], 16)
            sp.dma_start(tokw_s[:, :, :], tokw).then_inc(s["tokw_in"], 16)
            for i in range(4):
                sp.dma_start(pat[:, 2 * i:2 * i + 2, :], patches[:, 2 * i:2 * i + 2, :]).then_inc(pat_in[i], 16)
            sp.dma_start(w0_s[:, :, :, :], w0).then_inc(s["w0_in"], 16)
            sp.dma_start(bcol_s[:, :], bcol).then_inc(s["bias_in"], 16)
            sp.dma_start(brow_s[:, :, :], brow.partition_broadcast(128)).then_inc(s["brow_in"], 16)
            sp.dma_start(masks[:, :], masks_in).then_inc(s["consts"], 16)
            sp.dma_start(wx_s[:, :, :, :], wx).then_inc(s["wx_in"], 16)
            for e in range(2):
                sp.dma_start(ring[:, e, :], experts0[e]).then_inc(ring_in[e], 16)
            sp.dma_start(w1_s[:, :, :, :], w1a).then_inc(s["w1_in"], 16)
            sp.dma_start(w1o_s[:, :, :], w1o).then_inc(s["w1_in"], 16)
            for e in range(2, 4):
                sp.dma_start(ring[:, e, :], experts0[e]).then_inc(ring_in[e], 16)
            sp.dma_start(gate_s[:, :, :], gate).then_inc(s["gate_in"], 16)
            sp.dma_start(shared_s[:, :], shared).then_inc(s["shared_in"], 16)
            sp.dma_start(tri[:, :], tri_in).then_inc(s["route_in"], 16)
            for e in range(4, GROUPS):
                sp.wait_ge(s["down_done"], e - 3)
                sp.dma_start(ring[:, e - 4, :], experts0[e]).then_inc(ring_in[e - 4], 16)
            sp.wait_ge(s["wo_done"], GROUPS)
            sp.dma_start(route[:, :], route_in).then_inc(s["route_in"], 16)
            sp.wait_ge(s["table_ready"], 1)
            sp.wait_ge(s["down_done"], GROUPS)
            sp.wait_ge(s["scattered"], 16 * GROUPS)
            sp.wait_ge(s["written"], 16)
            sp.wait_ge(s["sc_done"], GROUPS)
            rounds = sp.value_load(table[0:1, 2 * MAX_BLOCKS:2 * MAX_BLOCKS + 1], min_val=1, max_val=MAX_BLOCKS // UNROLL)
            with sp.Fori(0, rounds) as r:
                for u in range(UNROLL):
                    sp.wait_ge(s["dn_done"], r * UNROLL + 1)
                    e = sp.value_load(table[0:1, bass.ds(r * UNROLL + u, 1)], min_val=0, max_val=EXPERTS - 1)
                    at = sp.value_load(table[0:1, bass.ds(r * UNROLL + u + MAX_BLOCKS, 1)], min_val=0, max_val=TOKENS)
                    sp.dma_start(xw[:, u, :], sorted_x[bass.ds(at, BLOCK), :]).then_inc(window_in[u], 16)
                    sp.dma_start(ring[:, u, 0:3072], experts1[bass.ds(e, 1)].rearrange("e p n -> (e p) n")).then_inc(block_in[u], 16)
            for g in range(GROUPS):
                sp.wait_ge(s["out_ready"], g + 1)
                sp.dma_start(out[g], h[:, g, :]).then_inc(s["stored"], 16)
            sp.wait_ge(s["stored"], 16 * GROUPS)

        @block.tensor
        def _(pe):
            mm = nc.tensor.matmul

            def rows(b, lhs, rhs, chunks, col=0):
                for c in range(chunks):
                    a = lhs(c)
                    last = mm(P[b][0:a.shape[1], col:col + D], a, rhs(c), start=(c == 0), stop=(c == chunks - 1))
                return last

            def tok(g):
                if g % 2 == 0:
                    pe.wait_ge(pat_in[g // 2], 16)
                if g >= 2:
                    pe.wait_ge(s["h0_ready"], g - 1)
                rows(g % 2, lambda c: pat[:, g, c * GT:(c + 1) * GT], lambda c: tokw_s[:, c, :], FC).then_inc(s["tok_done"], 1)

            def trA(g):
                pe.wait_ge(s["n_ready"], g + 1)
                if g >= 2:
                    pe.wait_ge(s["xA_ready"], g - 1)
                for c in range(DC):
                    last = nc.tensor.transpose(bank(2 + g % 2, DC, GT)[:, c, :], xr[:, g % 2, c * 128:(c + 1) * 128], ident[0:GT, 0:GT])
                last.then_inc(s["trA_done"], 1)

            nc.tensor.nop().then_inc(s["dn_done"], 1)
            nc.tensor.nop().then_inc(s["gu_done"], 1)
            pe.wait_ge(s["consts"], 16)
            pe.wait_ge(s["tokw_in"], 16)
            lagged(GROUPS + 2, [(trA, 2), (tok, 0)])

            pe.wait_ge(s["w0_in"], 16)
            pe.wait_ge(s["xA_ready"], GROUPS)
            pe.wait_ge(s["h0_ready"], GROUPS)
            for n in range(8):
                w, m, half = n // 4, (n // 2) % 2, n % 2
                if n >= 4:
                    pe.wait_ge(s["z0_ready"], n - 3)
                for c in range(DC):
                    last = mm(bank(n % 4, HALF), w0_s[:, w, c, m * 128:(m + 1) * 128],
                              xA[:, c, half * HALF:(half + 1) * HALF], start=(c == 0), stop=(c == DC - 1))
                last.then_inc(s["qk0_done"], 1)
            for i in range(PTILES):
                cols, n = ptile(i)
                if i >= 2:
                    pe.wait_ge(s["v0_ready"], i - 1)
                rows(4 + i % 2, lambda c: xA[:, c, cols], lambda c: w0_s[:, 2, c, :], DC).then_inc(s["v0_done"], 1)
            pe.wait_ge(s["qk0_ready"], 8)

            def att(i):
                if i >= PTILES:
                    return
                cols, n = ptile(i)
                if i >= 2:
                    pe.wait_ge(s["att_ready"], i - 1)
                for c in range(DC):
                    last = mm(P[6 + i % 2][0:n, 0:n], kT[:, c, cols], qT[:, c, cols], start=(c == 0), stop=(c == DC - 1))
                last.then_inc(s["att_done"], 1)

            def att_v(i):
                if i >= PTILES:
                    return
                cols, n = ptile(i)
                pe.wait_ge(s["att_ready"], i + 1)
                pe.wait_ge(s["v0_ready"], i + 1)
                if i >= 2:
                    pe.wait_ge(s["oT_ready"], i - 1)
                for c in range(DC):
                    last = mm(bank(i % 2, DC, PT)[:, c, 0:n], vrow[0:n, i, c * 128:(c + 1) * 128], attA[0:n, i % 2, 0:n],
                              start=True, stop=True)
                last.then_inc(s["oT_done"], 1)

            lagged(GROUPS + 1, [(att, 0), (att_v, 1)])

            def wo(g):
                if g == 0:
                    pe.wait_ge(s["oT_ready"], PTILES)
                if g >= 3:
                    pe.wait_ge(s["x2T_ready"], g - 2)
                elif g >= 1:
                    pe.wait_ge(s["wo_read"], g)
                rows(0, lambda c: oT[:, c, gcol(g)], lambda c: w0_s[:, 3, c, :], DC).then_inc(s["wo_done"], 1)

            def tr1(g):
                pe.wait_ge(s["n_ready"], GROUPS + 2 * g + 2)
                if g >= 1:
                    pe.wait_ge(s["n2T_ready"], g)
                    pe.wait_ge(s["nT_ready"], g)
                for a, src in ((0, xr), (2, xr2)):
                    for c in range(DC):
                        last = nc.tensor.transpose(bank(1, 4, GT)[:, a + c, :], src[:, g % 2, c * 128:(c + 1) * 128], ident[0:GT, 0:GT])
                last.then_inc(s["tr1_done"], 1)

            def xa(g):
                pe.wait_ge(s["n2T_ready"], g + 1)
                if g >= 1:
                    pe.wait_ge(s["xaT_ready"], g)
                for m in range(DC):
                    for c in range(DC):
                        last = mm(bank(2, DC, GT)[:, m, :], wx_s[:, 0, c, m * 128:(m + 1) * 128], n2T[:, c, :],
                                  start=(c == 0), stop=(c == DC - 1))
                last.then_inc(s["xa_done"], 1)

            def up(g):
                pe.wait_ge(ring_in[g % 4], 16 * (g // 4 + 1))
                pe.wait_ge(s["xaT_ready"], g + 1)
                w = ring[:, g % 4, 0:DC * HIDDEN].rearrange("p (c n) -> p c n", c=DC)
                for m in range(HC):
                    if g >= 1 and m % 4 == 0:
                        pe.wait_ge(s["gelu_done"], HC * (g - 1) + m + 4)
                    for c in range(DC):
                        last = mm(bank(3 + m // 4, 4, GT)[:, m % 4, :], w[:, c, m * 128:(m + 1) * 128], xaT[:, c, :],
                                  start=(c == 0), stop=(c == DC - 1))
                    if m % 4 == 3:
                        last.then_inc(s["up_done"], 1)

            def down(g):
                if g >= 1:
                    pe.wait_ge(s["nx_sum"], g)
                w = ring[:, g % 4, DC * HIDDEN:].rearrange("p (c n) -> p c n", c=HC)
                pe.wait_ge(s["gelu_done"], HC * (g + 1))
                for m in range(DC):
                    for c in range(HC):
                        last = mm(P[5][:, m * GT:(m + 1) * GT], w[:, c, m * 128:(m + 1) * 128], fhT[:, c, :],
                                  start=(c == 0), stop=(c == HC - 1))
                last.then_inc(s["down_done"], 1)

            def nx(g):
                pe.wait_ge(s["eoT_ready"], g + 1)
                rows(5, lambda c: eoT[:, c, :], lambda c: wx_s[:, 1, c, :], DC, col=256).then_inc(s["nx_done"], 1)

            def tr2(g):
                pe.wait_ge(s["x2_ready"], g + 1)
                pe.wait_ge(s["wo_read"], min(g + 3, GROUPS))
                for c in range(DC):
                    last = nc.tensor.transpose(P[0][:, 256 + c * GT:256 + (c + 1) * GT], xs[:, g % 2, c * 128:(c + 1) * 128], ident[0:GT, 0:GT])
                last.then_inc(s["tr2_done"], 1)

            def qk1(g):
                pe.wait_ge(s["x2T_ready"], g + 1)
                if g == 0:
                    pe.wait_ge(s["w1_in"], 32)
                else:
                    pe.wait_ge(s["z1_ready"], g)
                for w in range(2):
                    for m in range(DC):
                        for c in range(DC):
                            last = mm(bank(6, 4, GT)[:, 2 * w + m, :], w1_s[:, w, c, m * 128:(m + 1) * 128], x2T[:, c, :],
                                      start=(c == 0), stop=(c == DC - 1))
                last.then_inc(s["qk1_done"], 1)

            def v1(g):
                if g >= 1:
                    pe.wait_ge(s["v1_ready"], g)
                rows(7, lambda c: x2T[:, c, :], lambda c: w1_s[:, 2, c, :], DC).then_inc(s["v1_done"], 1)

            pe.wait_ge(s["wx_in"], 16)
            lagged(GROUPS + 3, [(tr1, 1), (tr2, 3), (nx, 2), (xa, 1), (wo, 0), (up, 1), (qk1, 3), (v1, 3), (down, 1)])

            def scores(g):
                pe.wait_ge(s["k1_ready"], 2 * (g + 1))
                pe.wait_ge(s["q1_ready"], g + 1)
                if g >= 1:
                    pe.wait_ge(s["sc_ready"], 4 * g)
                for c in range(DC):
                    for odd, k in ((0, kE), (1, kO)):
                        for r in range(4):
                            last = mm(bank(r, 4, GT)[0:GT, 2 * c + odd, :], k[32 * r:32 * r + 32, c, gcol(g)],
                                      q1[32 * r:32 * r + 32, c, gcol(g)], start=True, stop=True, tile_position=(32 * r, 0))
                last.then_inc(s["sc_done"], 1)

            def av(g):
                pe.wait_ge(s["sc_ready"], 4 * (g + 1))
                if g == 0:
                    pe.wait_ge(s["v1_ready"], GROUPS)
                else:
                    pe.wait_ge(s["val_ready"], g)
                for b in range(4):
                    for r in range(4):
                        head = 8 * (b // 2) + 2 * r + b % 2
                        sc = S[0:GT, g % 2, (r * 4 + b) * GT:(r * 4 + b + 1) * GT]
                        mm(bank(4, 4, GT)[32 * r:32 * r + 32, b, :], vpad[0:GT, g, head, :], sc, start=True, stop=True,
                           tile_position=(0, 32 * r))
                for b in range(4):
                    for r in range(4):
                        sc = S[0:GT, g % 2, (r * 4 + b) * GT:(r * 4 + b + 1) * GT]
                        last = mm(bank(5, 4, GT)[32 * r:32 * r + 32, b, :], ones32[:, :], sc, start=True, stop=True,
                                  tile_position=(0, 32 * r))
                last.then_inc(s["av_done"], 1)

            def wo1(g):
                pe.wait_ge(s["val_ready"], g + 1)
                if g >= 1:
                    pe.wait_ge(s["h0_ready"], 2 * GROUPS + g)
                rows(6, lambda c: valT[:, c, :], lambda c: w1o_s[:, c, :], 4).then_inc(s["wo1_done"], 1)

            def tr3(g):
                pe.wait_ge(s["x3_ready"], g + 1)
                if g >= 1:
                    pe.wait_ge(s["x3T_ready"], g)
                for c in range(DC):
                    last = nc.tensor.transpose(bank(7, DC, GT)[:, c, :], x3[0:GT, g, c * 128:(c + 1) * 128], ident[0:GT, 0:GT])
                last.then_inc(s["tr3_done"], 1)

            pe.wait_ge(s["zeroed"], 2)
            lagged(GROUPS + 3, [(tr3, 3), (av, 1), (wo1, 2), (scores, 0)])

            pe.wait_ge(s["gate_in"], 16)
            pe.wait_ge(s["h0_ready"], 3 * GROUPS)
            for g in range(GROUPS):
                pe.wait_ge(s["x3T_ready"], g + 1)
                for c in range(DC):
                    last = mm(P[6][0:GT, g * EXPERTS:(g + 1) * EXPERTS], x3T[:, c, gcol(g)], gate_s[:, c, :],
                              start=(c == 0), stop=(c == DC - 1))
            last.then_inc(s["lg_done"], 1)

            pe.wait_ge(s["shared_in"], 16)

            def shared_up(n):
                m, half = n // 2, n % 2
                if n >= 2:
                    pe.wait_ge(s["hid_ready"], n - 1)
                for b, w in ((n % 2, sgw), (2 + n % 2, suw)):
                    for c in range(DC):
                        last = mm(bank(b, HALF), w[:, c, m * 128:(m + 1) * 128], x3T[:, c, half * HALF:(half + 1) * HALF],
                                  start=(c == 0), stop=(c == DC - 1))
                last.then_inc(s["sg_done"], 1)

            shared_up(0)
            shared_up(1)
            pe.wait_ge(s["onehot_ready"], 1)
            pe.wait_ge(s["route_in"], 32)
            mm(P[4][0:GT, 0:256], tri[:, 0:GT], onehot_b[:, :, :].rearrange("p g e -> p (g e)"), start=True, stop=True)
            mm(P[5][:, 0:256], tri[:, GT:GT + 128], onehot_b[:, :, :].rearrange("p g e -> p (g e)"), start=True, stop=True)\
                .then_inc(s["prefix_done"], 1)
            for n in range(2, 2 * IC):
                shared_up(n)
            pe.wait_ge(s["hid_ready"], 2 * IC)
            for g in range(GROUPS):
                if g >= 2:
                    pe.wait_ge(s["h_final"], g - 1)
                rows(6 + g % 2, lambda c: hidT[:, c, gcol(g)], lambda c: sdw[:, c, :], IC).then_inc(s["sd_done"], 1)

            pe.wait_ge(s["h_final"], GROUPS)
            pe.wait_ge(s["slot_ready"], 1)
            rounds = pe.value_load(table[0:1, 2 * MAX_BLOCKS:2 * MAX_BLOCKS + 1], min_val=1, max_val=MAX_BLOCKS // UNROLL)
            with pe.Fori(0, rounds) as r:
                for pair in range(UNROLL // 2):
                    for u in (2 * pair, 2 * pair + 1):
                        pe.wait_ge(window_in[u], 16 * (r + 1))
                        pe.wait_ge(s["xwT_ready"], r * UNROLL + u + 1)
                        for c in range(DC):
                            last = nc.tensor.transpose(bank(4, DC, BLOCK)[:, c, :], xw[:, u, c * 128:(c + 1) * 128], ident[:, :])
                        last.then_inc(s["xwt_done"], 1)
                    for u in (2 * pair, 2 * pair + 1):
                        gw = ring[:, u, 0:1024].rearrange("p (c n) -> p c n", c=DC)
                        uw = ring[:, u, 1024:2048].rearrange("p (c n) -> p c n", c=DC)
                        pe.wait_ge(block_in[u], 16 * (r + 1))
                        pe.wait_ge(s["xwT_ready"], r * UNROLL + u + 2)
                        if u >= 2:
                            pe.wait_ge(s["hw_ready"], r * UNROLL + u)
                        else:
                            pe.wait_ge(s["hw_ready"], r * UNROLL + 1)
                        for b, w in ((u % 2, gw), (2 + u % 2, uw)):
                            for m in range(IC):
                                for c in range(DC):
                                    last = mm(bank(b, IC, BLOCK)[:, m, :], w[:, c, m * 128:(m + 1) * 128], xwT[:, u, c, :],
                                              start=(c == 0), stop=(c == DC - 1))
                            last.then_inc(s["gu_done"], 1)
                    for u in (2 * pair, 2 * pair + 1):
                        dw = ring[:, u, 2048:3072].rearrange("p (c n) -> p c n", c=IC)
                        pe.wait_ge(s["hw_ready"], r * UNROLL + u + 2)
                        pe.wait_ge(s["yw_ready"], r * UNROLL + (u if u >= 2 else 1))
                        rows(5 + u % 2, lambda c: hw[:, u % 2, c * BLOCK:(c + 1) * BLOCK], lambda c: dw[:, c, :], IC)\
                            .then_inc(s["dn_done"], 1)

        @block.scalar
        def _(act):
            A = nc.scalar.activation

            for g in range(GROUPS):
                act.wait_ge(s["trA_done"], g + 1)
                for c in range(DC):
                    dst = xA[:, c, :].rearrange("p (b i) -> p i b", i=IMAGES)[:, GI * g:GI * (g + 1), :]
                    src = bank(2 + g % 2, DC, GT)[:, c, :].rearrange("p (i b) -> p i b", b=POSITIONS)
                    last = A(dst, src, ACT.Copy)
                last.then_inc(s["xA_ready"], 1)
            act.wait_ge(s["bias_in"], 16)
            for n in range(8):
                act.wait_ge(s["z0_ready"], n + 1)
                A(eA[:, n % 2, :], eA[:, n % 2, :], ACT.Exp).then_inc(s["exp0_done"], 1)
            for i in range(PTILES):
                cols, n = ptile(i)
                act.wait_ge(s["oT_done"], i + 1)
                for c in range(DC):
                    dst = oT[:, c, :].rearrange("p (i b) -> p b i", b=POSITIONS)[:, 4 * i:4 * i + n // IMAGES, :]
                    src = bank(i % 2, DC, PT)[:, c, 0:n].rearrange("p (b i) -> p b i", i=IMAGES)
                    last = A(dst, src, ACT.Copy)
                last.then_inc(s["oT_ready"], 1)

            def nT_evac(g):
                act.wait_ge(s["tr1_done"], g + 1)
                if g >= 1:
                    act.wait_ge(s["xa_done"], g)
                for c in range(DC):
                    last = A(n2T[:, c, :], bank(1, 4, GT)[:, 2 + c, :], ACT.Identity, bias=bcol_s[:, LNB + c:LNB + c + 1],
                             scale=bcol_s[:, LNS + c:LNS + c + 1])
                last.then_inc(s["n2T_ready"], 1)
                if g >= 1:
                    act.wait_ge(s["xaT_ready"], g)
                for c in range(DC):
                    last = A(nT[:, c, :], bank(1, 4, GT)[:, c, :], ACT.Identity, bias=bcol_s[:, AB + c:AB + c + 1])
                last.then_inc(s["nT_ready"], 1)

            def gelu_up(g):
                if g >= 1:
                    act.wait_ge(s["down_done"], g)
                for m in range(HC):
                    if m % 4 == 0:
                        act.wait_ge(s["up_done"], 2 * g + m // 4 + 1)
                    A(fhT[:, m, :], bank(3 + m // 4, 4, GT)[:, m % 4, :], ACT.Gelu, bias=bcol_s[:, B1 + HC * g + m:B1 + HC * g + m + 1])\
                        .then_inc(s["gelu_done"], 1)

            def gelu_nx(g):
                act.wait_ge(s["nx_sum"], g + 1)
                A(nxr[:, :], nxr[:, :], ACT.Gelu).then_inc(s["nx_gelu"], 1)

            def x2_evac(g):
                act.wait_ge(s["tr2_done"], g + 1)
                if g >= 1:
                    act.wait_ge(s["v1_done"], g)
                A(x2T[:, :, :].rearrange("p c t -> p (c t)"), P[0][:, 256:256 + DC * GT], ACT.Copy).then_inc(s["x2T_ready"], 1)

            lagged(GROUPS + 3, [(nT_evac, 1), (x2_evac, 3), (gelu_nx, 2), (gelu_up, 1)])

            def exp1(g):
                act.wait_ge(s["m1_ready"], g + 1)
                last = A(eA[:, g % 2, :], eA[:, g % 2, :], ACT.Exp)
                last.then_inc(s["exp1_done"], 1)

            def k_evac(g):
                act.wait_ge(s["q1_ready"], g + 1)
                for dst, m in ((kE, EVEN), (kO, ODD)):
                    A(dst[:, :, gcol(g)], kz[:, :, gcol(g)], ACT.Copy, scale=bcol_s[:, m:m + 1]).then_inc(s["k1_ready"], 1)

            def x3_evac(g):
                act.wait_ge(s["tr3_done"], g + 1)
                A(x3T[:, :, gcol(g)], bank(7, DC, GT), ACT.Copy).then_inc(s["x3T_ready"], 1)

            exp1(0)
            lagged(GROUPS + 3, [(x3_evac, 3), (k_evac, 0), (lambda g: g + 1 < GROUPS and exp1(g + 1), 0)])

            act.wait_ge(s["topv_ready"], 1)
            A(lgm[:, GROUPS:2 * GROUPS], lgm[:, 0:GROUPS], ACT.Sigmoid).then_inc(s["score_ready"], 1)
            for n in range(2 * IC):
                act.wait_ge(s["sg_done"], n + 1)
                if n >= 2:
                    act.wait_ge(s["hid_ready"], n - 1)
                A(zA[:, n % 2, :], bank(n % 2, HALF), ACT.Silu).then_inc(s["silu0_done"], 1)

            act.wait_ge(s["slot_ready"], 1)
            act.wait_ge(s["sd_done"], GROUPS)
            rounds = act.value_load(table[0:1, 2 * MAX_BLOCKS:2 * MAX_BLOCKS + 1], min_val=1, max_val=MAX_BLOCKS // UNROLL)
            with act.Fori(0, rounds) as r:
                for u in range(UNROLL):
                    act.wait_ge(s["gu_done"], 2 * (r * UNROLL + u) + 2)
                    act.wait_ge(s["hw_ready"], r * UNROLL + (u if u >= 2 else 1))
                    A(sg[:, u % 2, :], P[u % 2][:, :], ACT.Silu).then_inc(s["silu_done"], 1)

        @block.vector
        def _(dve):
            V = nc.vector
            chain = [0]

            def link(ins):
                chain[0] += 1
                ins.then_inc(s["vec"], 1)
                dve.wait_ge(s["vec"], chain[0])

            norms = [0]

            def norm(src, dst, done):
                link(V.bn_stats(st[:, :], src))
                link(V.bn_aggr(mv[:, :], st[:, :]))
                V.tensor_scalar_add(var[:, :], mv[:, 1:2], EPS).then_inc(s["var_ready"], 1)
                norms[0] += 1
                dve.wait_ge(s["rstd_ready"], norms[0])
                V.tensor_scalar(dst, src, mv[:, 0:1], rstd[:, :], ALU.subtract, ALU.mult).then_inc(s[done], 1)

            V.memset(mhalf[:, :], -0.5).then_inc(s["zeroed"], 1)
            V.memset(ones32[:, :], 1.0).then_inc(s["zeroed"], 1)

            dve.wait_ge(s["cls_in"], 16 * GI)
            for g in range(GROUPS):
                dve.wait_ge(s["tok_done"], g + 1)
                V.tensor_tensor(h[:, g, :], P[g % 2][0:GT, 0:D], clsbuf, ALU.add).then_inc(s["h0_ready"], 1)
                dve.wait_ge(s["h0_ready"], g + 1)
                if g >= 2:
                    dve.wait_ge(s["trA_done"], g - 1)
                norm(h[:, g, :], xr[:, g % 2, :], "n_ready")

            dve.wait_ge(s["bias_in"], 16)
            for n in range(9):
                if n < 8:
                    b = (BQ0, BK0)[n // 4] + (n // 2) % 2
                    dve.wait_ge(s["qk0_done"], n + 1)
                    if n >= 2:
                        dve.wait_ge(s["qk0_ready"], n - 1)
                    V.tensor_scalar(zA[:, n % 2, :], bank(n % 4, HALF), bcol_s[:, b:b + 1], None, ALU.add).then_inc(s["z0_sum"], 1)
                    dve.wait_ge(s["z0_sum"], n + 1)
                    V.tensor_scalar_min(eA[:, n % 2, :], zA[:, n % 2, :], 0.0).then_inc(s["z0_ready"], 1)
                if n == 0:
                    continue
                n -= 1
                w, m, half = n // 4, (n // 2) % 2, n % 2
                dve.wait_ge(s["exp0_done"], n + 1)
                V.scalar_tensor_tensor((qT, kT)[w][:, m, half * HALF:(half + 1) * HALF], zA[:, n % 2, :], 0.0, eA[:, n % 2, :],
                                       ALU.max, ALU.add).then_inc(s["qk0_ready"], 1)
            dve.wait_ge(s["brow_in"], 16)
            for i in range(PTILES):
                cols, n = ptile(i)
                dve.wait_ge(s["v0_done"], i + 1)
                V.tensor_tensor(vrow[0:n, i, :], P[4 + i % 2][0:n, 0:D], brow_s[0:n, BV0, :], ALU.add).then_inc(s["v0_ready"], 1)
            dve.wait_ge(s["consts"], 32)
            for i in range(PTILES):
                cols, n = ptile(i)
                dve.wait_ge(s["att_done"], i + 1)
                if i >= 2:
                    dve.wait_ge(s["oT_done"], i - 1)
                V.tensor_tensor(attA[0:n, i % 2, 0:n], P[6 + i % 2][0:n, 0:n], masks[0:n, 0:n], ALU.mult).then_inc(s["att_ready"], 1)

            def h1_norms(g):
                dve.wait_ge(s["wo_done"], g + 1)
                V.tensor_tensor(xr2[:, g % 2, :], P[0][0:GT, 0:D], brow_s[0:GT, BO0, :], ALU.add).then_inc(s["wo_read"], 1)
                dve.wait_ge(s["wo_read"], g + 1)
                V.tensor_tensor(h[:, g, :], h[:, g, :], xr2[:, g % 2, :], ALU.add).then_inc(s["h0_ready"], 1)
                dve.wait_ge(s["h0_ready"], GROUPS + g + 1)
                norm(h[:, g, :], xr[:, g % 2, :], "n_ready")
                dve.wait_ge(s["n_ready"], GROUPS + 2 * g + 1)
                norm(xr[:, g % 2, :], xr2[:, g % 2, :], "n_ready")

            def xa_evac(g):
                dve.wait_ge(s["xa_done"], g + 1)
                dve.wait_ge(s["nT_ready"], g + 1)
                if g >= 1:
                    dve.wait_ge(s["up_done"], 2 * g)
                V.tensor_tensor(xaT[:, :, :], bank(2, DC, GT), nT[:, :, :], ALU.add).then_inc(s["xaT_ready"], 1)

            def eo_evac(g):
                dve.wait_ge(s["down_done"], g + 1)
                if g >= 1:
                    dve.wait_ge(s["nx_done"], g)
                for c in range(DC):
                    last = V.tensor_scalar(eoT[:, c, :], P[5][:, c * GT:(c + 1) * GT], bcol_s[:, B2 + DC * g + c:B2 + DC * g + c + 1], None, ALU.add)
                last.then_inc(s["eoT_ready"], 1)

            def nx_evac(g):
                dve.wait_ge(s["nx_done"], g + 1)
                V.tensor_tensor(nxr[:, :], P[5][0:GT, 256:512], brow_s[0:GT, NXB, :], ALU.add).then_inc(s["nx_sum"], 1)

            def h2_norm(g):
                dve.wait_ge(s["nx_gelu"], g + 1)
                link(V.tensor_tensor(h[:, g, :], h[:, g, :], nxr[:, :], ALU.add))
                norm(h[:, g, :], xs[:, g % 2, :], "x2_ready")

            def z_evac(g):
                dve.wait_ge(s["qk1_done"], g + 1)
                for w, dst in ((0, q1), (1, kz)):
                    for c in range(DC):
                        b = (BQ1, BK1)[w] + c
                        last = V.tensor_scalar(dst[:, c, gcol(g)], bank(6, 4, GT)[:, 2 * w + c, :], bcol_s[:, b:b + 1], None, ALU.add)
                last.then_inc(s["z1_ready"], 1)

            def v_evac(g):
                dve.wait_ge(s["v1_done"], g + 1)
                if g == 0:
                    dve.wait_ge(s["vpad_zero"], 1)
                V.tensor_tensor(vpad[0:GT, g, :, 0:HD], P[7][0:GT, 0:D].rearrange("p (h m) -> p h m", m=HD),
                                brow_s[0:GT, BV1, :].rearrange("p (h m) -> p h m", m=HD), ALU.add).then_inc(s["v1_ready"], 1)

            lagged(GROUPS + 3, [(nx_evac, 2), (xa_evac, 1), (h2_norm, 2), (h1_norms, 0), (z_evac, 3), (v_evac, 3), (eo_evac, 1)])

            def min1(g):
                if g >= 2:
                    dve.wait_ge(s["q1_ready"], g - 1)
                elif g == 0:
                    dve.wait_ge(s["z1_ready"], GROUPS)
                for n, src in ((0, q1), (1, kz)):
                    last = V.tensor_scalar_min(eA[:, g % 2, n * DC * GT:(n + 1) * DC * GT].rearrange("p (c t) -> p c t", c=DC),
                                               src[:, :, gcol(g)], 0.0)
                last.then_inc(s["m1_ready"], 1)

            def elu1(g):
                dve.wait_ge(s["exp1_done"], g + 1)
                for n, src in ((0, q1), (1, kz)):
                    e = eA[:, g % 2, n * DC * GT:(n + 1) * DC * GT].rearrange("p (c t) -> p c t", c=DC)
                    last = V.scalar_tensor_tensor(src[:, :, gcol(g)], src[:, :, gcol(g)], 0.0, e, ALU.max, ALU.add)
                last.then_inc(s["q1_ready"], 1)

            def mask_scores(g):
                dve.wait_ge(s["sc_done"], g + 1)
                if g == 1:
                    dve.wait_ge(s["written"], 16)
                if g >= 2:
                    dve.wait_ge(s["av_done"], g - 1)
                causal = masks[0:GT, 128:128 + GT].unsqueeze(1).to_broadcast([GT, 4, GT])
                for r in range(4):
                    dst = S[0:GT, g % 2, r * 4 * GT:(r + 1) * 4 * GT].rearrange("p (a t) -> p a t", a=4)
                    V.tensor_tensor(dst, bank(r, 4, GT)[0:GT, :, :], causal, ALU.mult).then_inc(s["sc_ready"], 1)

            def values(g):
                dve.wait_ge(s["av_done"], g + 1)
                link(V.tensor_scalar_add(rden[:, :], bank(5, HALF), 1e-6))
                link(V.reciprocal(rden[:, :], rden[:, :]))
                if g >= 1:
                    dve.wait_ge(s["wo1_done"], g)
                V.tensor_tensor(valT[:, :, :].rearrange("p a t -> p (a t)"), bank(4, HALF), rden[:, :], ALU.mult).then_inc(s["val_ready"], 1)

            def h3_norm(g):
                dve.wait_ge(s["wo1_done"], g + 1)
                link(V.tensor_tensor(xr[:, 0, :], P[6][0:GT, 0:D], brow_s[0:GT, BO1, :], ALU.add))
                V.tensor_tensor(h[:, g, :], h[:, g, :], xr[:, 0, :], ALU.add).then_inc(s["h0_ready"], 1)
                dve.wait_ge(s["h0_ready"], 2 * GROUPS + g + 1)
                norm(h[:, g, :], x3[0:GT, g, :], "x3_ready")

            min1(0)
            elu1(0)
            min1(1)
            lagged(GROUPS + 2, [(lambda g: g + 2 < GROUPS and min1(g + 2), 0), (lambda g: g + 1 < GROUPS and elu1(g + 1), 0),
                                (values, 1), (h3_norm, 2), (mask_scores, 0)])

            logits = P[6][0:GT, 0:256].rearrange("p (g e) -> p g e", e=EXPERTS)
            iota = route[0:GT, C_IOTA:C_IOTA + EXPERTS].unsqueeze(1).to_broadcast([GT, GROUPS, EXPERTS])
            dve.wait_ge(s["lg_done"], 1)
            dve.wait_ge(s["route_in"], 32)

            def per_group(col):
                return lgm[:, col * GROUPS:(col + 1) * GROUPS].unsqueeze(2).to_broadcast([GT, GROUPS, EXPERTS])

            V.tensor_reduce(lgm[:, 0:GROUPS], logits, AX.X, ALU.max).then_inc(s["topv_ready"], 1)
            dve.wait_ge(s["topv_ready"], 1)
            link(V.tensor_tensor(big[:, :, :], logits, per_group(0), ALU.is_equal))
            link(V.tensor_tensor(big[:, :, :], big[:, :, :], iota, ALU.mult))
            link(V.tensor_reduce(lgm[:, 2 * GROUPS:3 * GROUPS], big[:, :, :], AX.X, ALU.min))
            V.tensor_tensor(onehot_b[:, :, :], iota, per_group(2), ALU.is_equal).then_inc(s["onehot_ready"], 1)
            link(V.tensor_tensor(onehot[:, :, :], iota, per_group(2), ALU.is_equal))

            def hidden(n):
                m, half = n // 2, n % 2
                dve.wait_ge(s["silu0_done"], n + 1)
                V.tensor_tensor(hidT[:, m, half * HALF:(half + 1) * HALF], zA[:, n % 2, :], bank(2 + n % 2, HALF), ALU.mult)\
                    .then_inc(s["hid_ready"], 1)

            dve.wait_ge(s["prefix_done"], 1)
            link(V.memset(before[:, 0, :], 0.0))
            for g in range(GROUPS):
                link(V.tensor_tensor(before[:, g + 1, :], before[:, g, :], P[5][:, g * EXPERTS:(g + 1) * EXPERTS], ALU.add))
            link(V.memset(rt[:, 7, :], 0.0))
            count = before[:, GROUPS, :]
            link(V.tensor_tensor_scan(rt[:, 0, :], count, rt[:, 7, :], 0.0, ALU.add, ALU.add))
            link(V.tensor_tensor(rt[:, 1, :], rt[:, 0, :], count, ALU.subtract))
            link(V.tensor_tensor(big[:, :, :], P[4][0:GT, 0:256].rearrange("p (g e) -> p g e", e=EXPERTS), before[0:GT, 0:GROUPS, :], ALU.add))
            link(V.tensor_tensor(big[:, :, :], big[:, :, :], rt[0:GT, 1, :].unsqueeze(1).to_broadcast([GT, GROUPS, EXPERTS]), ALU.add))
            link(V.tensor_tensor(big[:, :, :], big[:, :, :], onehot[:, :, :], ALU.mult))
            link(V.tensor_reduce(lgm[:, 3 * GROUPS:4 * GROUPS], big[:, :, :], AX.X, ALU.add))
            V.tensor_copy(slot_i[:, :], lgm[:, 3 * GROUPS:4 * GROUPS]).then_inc(s["slot_ready"], 1)
            dve.wait_ge(s["score_ready"], 1)
            for g in range(GROUPS):
                if g >= 2:
                    dve.wait_ge(xs_sent[g % 2], 16 * (g // 2))
                V.tensor_scalar(xs[:, g % 2, :], x3[0:GT, g, :], lgm[:, GROUPS + g:GROUPS + g + 1], None, ALU.mult).then_inc(s["xs_ready"], 1)
                if g < 4:
                    hidden(g)

            link(V.tensor_tensor(tmat[:, 0, 0:7 * EXPERTS].rearrange("p (e m) -> p e m", m=7), count[0:1, :].unsqueeze(2).to_broadcast([1, EXPERTS, 7]),
                                 route[0:1, C_128:C_128 + 7 * EXPERTS].rearrange("p (e m) -> p e m", m=7), ALU.is_gt))
            link(V.tensor_reduce(rt[0:1, 2, :], tmat[:, 0, 0:7 * EXPERTS].rearrange("p (e m) -> p e m", m=7), AX.X, ALU.add))
            link(V.tensor_tensor_scan(rt[0:1, 3, :], rt[0:1, 2, :], rt[0:1, 7, :], 0.0, ALU.add, ALU.add))
            link(V.tensor_tensor(rt[0:1, 4, :], rt[0:1, 3, :], rt[0:1, 2, :], ALU.subtract))
            link(V.tensor_scalar(rt[0:1, 5, :], rt[0:1, 4, :], float(-BLOCK), None, ALU.mult))
            link(V.tensor_tensor(rt[0:1, 5, :], rt[0:1, 5, :], rt[0:1, 1, :], ALU.add))

            def row(i):
                return rt[0:1, i, :].unsqueeze(1).to_broadcast([1, MAX_BLOCKS, EXPERTS])

            def mat(i):
                return tmat[:, i, :].rearrange("p (k e) -> p k e", e=EXPERTS)

            kk = route[0:1, C_K:C_K + MAX_BLOCKS * EXPERTS].rearrange("p (k e) -> p k e", e=EXPERTS)
            link(V.tensor_tensor(mat(0), row(3), kk, ALU.is_le))
            link(V.tensor_reduce(tfl[:, 0, :], mat(0), AX.X, ALU.add))
            V.tensor_scalar_min(table[:, 0:MAX_BLOCKS], tfl[:, 0, :], float(EXPERTS - 1))
            link(V.tensor_tensor(mat(1), row(4), kk, ALU.is_le))
            link(V.tensor_tensor(mat(1), mat(1), mat(0), ALU.subtract))
            link(V.tensor_tensor(mat(1), mat(1), row(5), ALU.mult))
            link(V.tensor_reduce(tfl[:, 1, :], mat(1), AX.X, ALU.add))
            link(V.tensor_tensor(tfl[:, 1, :], tfl[:, 1, :], route[0:1, C_128K:C_128K + MAX_BLOCKS], ALU.add))
            V.tensor_scalar_min(table[:, MAX_BLOCKS:2 * MAX_BLOCKS], tfl[:, 1, :], float(TOKENS))
            link(V.tensor_tensor(tfl[:, 0, 0:10], rt[0:1, 3, EXPERTS - 1:EXPERTS].to_broadcast([1, 10]), route[0:1, C_QUAD:C_QUAD + 10], ALU.is_gt))
            link(V.tensor_reduce(tfl[:, 1, 0:1], tfl[:, 0, 0:10], AX.X, ALU.add))
            V.tensor_copy(table[:, 2 * MAX_BLOCKS:2 * MAX_BLOCKS + 1], tfl[:, 1, 0:1]).then_inc(s["table_ready"], 1)

            for n in range(4, 2 * IC):
                hidden(n)
            for g in range(GROUPS):
                dve.wait_ge(s["sd_done"], g + 1)
                V.tensor_tensor(h[:, g, :], h[:, g, :], P[6 + g % 2][0:GT, 0:D], ALU.add).then_inc(s["h_final"], 1)

            for n in ("xwT_ready", "hw_ready", "yw_ready"):
                nc.vector.engine_nop().then_inc(s[n], 1)
            dve.wait_ge(s["table_ready"], 1)
            rounds = dve.value_load(table[0:1, 2 * MAX_BLOCKS:2 * MAX_BLOCKS + 1], min_val=1, max_val=MAX_BLOCKS // UNROLL)
            with dve.Fori(0, rounds) as r:
                for pair in range(UNROLL // 2):
                    for u in (2 * pair, 2 * pair + 1):
                        dve.wait_ge(s["xwt_done"], r * UNROLL + u + 1)
                        dve.wait_ge(s["gu_done"], 2 * r * UNROLL + 1)
                        V.tensor_copy(xwT[:, u, :, :], bank(4, DC, BLOCK)).then_inc(s["xwT_ready"], 1)
                    for u in (2 * pair, 2 * pair + 1):
                        dve.wait_ge(s["silu_done"], r * UNROLL + u + 1)
                        dve.wait_ge(s["gu_done"], 2 * (r * UNROLL + u + 1) + 1)
                        dve.wait_ge(s["dn_done"], r * UNROLL + (u if u >= 2 else 1))
                        V.tensor_tensor(hw[:, u % 2, :], sg[:, u % 2, :], P[2 + u % 2][:, :], ALU.mult).then_inc(s["hw_ready"], 1)
                    for u in (2 * pair, 2 * pair + 1):
                        dve.wait_ge(s["dn_done"], r * UNROLL + u + 2)
                        dve.wait_ge(s["written"], 16 * UNROLL * r + 16)
                        V.tensor_copy(yw[:, u, :], P[5 + u % 2][:, 0:D]).then_inc(s["yw_ready"], 1)

            for g in range(GROUPS):
                dve.wait_ge(rows_back[g], 16)
                V.tensor_tensor(h[:, g, :], h[:, g, :], back[0:GT, g, :], ALU.add).then_inc(s["out_ready"], 1)

        @block.gpsimd
        def _(pool):
            nc.gpsimd.memset(clsbuf, 0.0).then_inc(s["cls_zero"], 1)
            nc.gpsimd.memset(zrow, 0.0).then_inc(s["cls_zero"], 1)
            pool.wait_ge(s["cls_zero"], 2)
            for i in range(GI):
                pool.dma_start(clsbuf[i * POSITIONS:i * POSITIONS + 1, :], cls).then_inc(s["cls_in"], 16)
            pool.dma_start(sorted_x[TOKENS:SORTED, :], zrow).then_inc(s["written"], 16)
            pool.wait_ge(s["zeroed"], 2)

            def power(n):
                pool.wait_ge(s["var_ready"], n + 1)
                nc.gpsimd.tensor_tensor(rstd[:, :], var[:, :], mhalf[:, :], ALU.pow).then_inc(s["rstd_ready"], 1)

            for n in range(GROUPS):
                power(n)
            pool.wait_ge(s["tok_done"], GROUPS)
            nc.gpsimd.memset(pat[:, :, :], 0.0).then_inc(s["vpad_zero"], 1)
            for n in range(GROUPS, 5 * GROUPS):
                power(n)

            pool.wait_ge(s["slot_ready"], 1)
            for g in range(GROUPS):
                pool.wait_ge(s["xs_ready"], g + 1)
                if g >= 2:
                    pool.wait_ge(xs_sent[g % 2], 16 * (g // 2))
                pool.indirect_dma_start(sorted_x, bass.IndirectOffsetOnAxis(ap=slot_i[:, g:g + 1], axis=0), xs[:, g % 2, :], None)\
                    .then_inc(xs_sent[g % 2], 16)
            for i in range(2):
                pool.wait_ge(xs_sent[i], 16 * GROUPS // 2)
            nc.gpsimd.memset(slot_seen[:, :], 0.0).then_inc(s["scattered"], 16 * GROUPS)

            pool.wait_ge(s["table_ready"], 1)
            rounds = pool.value_load(table[0:1, 2 * MAX_BLOCKS:2 * MAX_BLOCKS + 1], min_val=1, max_val=MAX_BLOCKS // UNROLL)
            with pool.Fori(0, rounds) as r:
                for u in range(UNROLL):
                    at = pool.value_load(table[0:1, bass.ds(r * UNROLL + u + MAX_BLOCKS, 1)], min_val=0, max_val=TOKENS)
                    pool.wait_ge(s["yw_ready"], r * UNROLL + u + 2)
                    pool.wait_ge(s["written"], 16 * (r * UNROLL + u) + 16)
                    pool.dma_start(sorted_y[bass.ds(at, BLOCK), :], yw[:, u, :]).then_inc(s["written"], 16)
            pool.wait_ge(s["written"], 16 * UNROLL * rounds + 16)
            nc.gpsimd.tensor_tensor(slot_seen[:, :], slot_seen[:, :], slot_seen[:, :], ALU.add).then_inc(s["all_written"], 1)
            pool.wait_ge(s["all_written"], 1)
            pool.wait_ge(s["av_done"], GROUPS)
            for g in range(GROUPS):
                pool.indirect_dma_start(back[0:GT, g, :], None, sorted_y[0:TOKENS, :], bass.IndirectOffsetOnAxis(ap=slot_i[:, g:g + 1], axis=0))\
                    .then_inc(rows_back[g], 16)


_OUT = (GROUPS, GT, D)


def kernel(**inputs):
    import numpy as _np
    import concourse.bacc as _bacc
    from concourse import mybir as _mybir
    from concourse.bass_utils import run_bass_kernel_spmd as _run

    a = {k: _np.ascontiguousarray(v) for k, v in inputs.items()}

    def chunked(w):
        return w.reshape(-1, 128, w.shape[-1]).transpose(1, 0, 2)

    order = [16 * m + 2 * g + r for g in range(GROUPS) for m in range(2) for r in range(2)]
    x = a["x"][:, :, 0:80, 0:80].reshape(32, 3, 5, 16, 5, 16).transpose(0, 1, 3, 5, 2, 4)
    pt = x.reshape(32, 25, 768)[order]
    pt = _np.concatenate([_np.zeros((32, 1, 768), pt.dtype), pt], axis=1)
    pt = pt.reshape(GROUPS, GT, FC, 128).transpose(3, 0, 2, 1).reshape(128, GROUPS, FC * GT)

    wo1 = _np.zeros((HEADS, HPAD, D), _np.float32)
    wo1[:, :HD] = a["L1_attn_Wo"].reshape(HEADS, HD, D)
    heads = [[8 * (b // 2) + 2 * r + b % 2 for r in range(4)] for b in range(4)]
    wo1 = _np.stack([wo1[hs].reshape(128, D) for hs in heads], axis=1)

    def col(v):
        return v.reshape(-1, 128).T

    parity = (_np.arange(128) // HD) % 2
    bcol = _np.concatenate([
        col(a["L0_attn_bq"]), col(a["L0_attn_bk"]), col(a["L0_ffn_ln_scale"]), col(a["L0_ffn_ln_bias"]),
        col(a["L0_ffn_attn_b"]), col(a["L1_attn_bq"]), col(a["L1_attn_bk"]), col(a["L0_ffn_b2"]), col(a["L0_ffn_b1"]),
        (parity == 0)[:, None], (parity == 1)[:, None]], axis=1).astype(_np.float32)
    brow = _np.stack([a["L0_attn_bv"], a["L0_attn_bo"], a["L0_ffn_next_b"], a["L1_attn_bv"], a["L1_attn_bo"]])
    p = _np.arange(128)
    masks = _np.zeros((128, 128 + GT), _np.float32)
    masks[:, :128] = p[:, None] // IMAGES == p[None] // IMAGES
    t = _np.arange(GT)
    masks[:GT, 128:] = (t[:, None] // POSITIONS == t[None] // POSITIONS) & (t[:, None] <= t[None])
    tri = _np.ones((GT, GT + 128), _np.float32)
    tri[:, :GT] = t[:, None] < t[None]
    route = _np.zeros((128, NROUTE), _np.float32)
    route[:, C_IOTA:C_IOTA + EXPERTS] = _np.arange(EXPERTS) - 64
    route[:, C_K:C_K + MAX_BLOCKS * EXPERTS] = _np.repeat(_np.arange(MAX_BLOCKS), EXPERTS)
    route[:, C_128:C_128 + 7 * EXPERTS] = _np.tile(BLOCK * _np.arange(7), EXPERTS)
    route[:, C_QUAD:C_QUAD + 10] = UNROLL * _np.arange(10)
    route[:, C_128K:] = BLOCK * _np.arange(MAX_BLOCKS)

    def experts(gw, uw, dw):
        n = gw.shape[0]
        parts = [w.reshape(n, -1, 128, w.shape[-1]).transpose(0, 2, 1, 3).reshape(n, 128, -1) for w in (gw, uw, dw) if w is not None]
        return _np.concatenate(parts, axis=2)

    feeds = {
        "patches": pt, "cls": a["cls_tok"].reshape(1, D), "tokw": chunked(a["L0_tok_W"]),
        "w0": _np.stack([chunked(a[f"L0_attn_W{n}"].T) for n in "qkvo"], axis=1),
        "wx": _np.stack([chunked(a["L0_ffn_attn_w"].T), chunked(a["L0_ffn_next_w"].T)], axis=1),
        "w1a": _np.stack([chunked(a[f"L1_attn_W{n}"]) for n in "qkv"], axis=1), "w1o": wo1,
        "gate": chunked(a["L1_ffn_gate_w"]),
        "shared": experts(a["L1_ffn_shared_gate_w"][None], a["L1_ffn_shared_up_w"][None], a["L1_ffn_shared_down_w"][None])[0],
        "experts0": experts(a["L0_ffn_w1"], None, a["L0_ffn_w2"]),
        "experts1": experts(a["L1_ffn_routed_gate_w"], a["L1_ffn_routed_up_w"], a["L1_ffn_routed_down_w"]),
        "bcol": bcol, "brow": brow, "ident_in": _np.eye(128, dtype=_np.float32), "masks_in": masks,
        "tri_in": tri.astype(_mybir.dt.np(BF16)), "route_in": route,
    }
    nc = _bacc.Bacc("TRN2", target_bir_lowering=False, num_devices=1)
    arrays, args = {}, []
    for name, v in feeds.items():
        v = _np.ascontiguousarray(v)
        arrays[f"{name}_dram"] = v
        args.append(nc.dram_tensor(f"{name}_dram", v.shape, _mybir.dt.from_np(v.dtype), kind="ExternalInput").ap())
    args.append(nc.dram_tensor("out_dram", _OUT, F32, kind="ExternalOutput").ap())
    tower(nc, *args)
    r = _run(nc, [arrays], core_ids=[0])
    got = _np.asarray(r.results[0]["out_dram"]).reshape(IMAGES, POSITIONS, D)
    inverse = _np.argsort(order)
    return got[inverse]
```

```python
from contextlib import ExitStack

import numpy as np
import concourse.bass as bass
from concourse import mybir

F32 = mybir.dt.float32
BF16 = mybir.dt.bfloat16
I32 = mybir.dt.int32
ALU = mybir.AluOpType
ACT = mybir.ActivationFunctionType
AX = mybir.AxisListType

IMAGES, POSITIONS, D = 32, 26, 256
TOKENS = IMAGES * POSITIONS
GROUPS = 8
GT = TOKENS // GROUPS
GI = IMAGES // GROUPS
DC = D // 128
FC = 6
HIDDEN = 1024
HC = HIDDEN // 128
INNER = 512
IC = INNER // 128
EXPERTS = 32
HEADS, HD = 16, 16
HPAD = 32
EPS = 1e-5
HALF = TOKENS // 2
PT = 4 * IMAGES
PTILES = 7
BLOCK = 128
UNROLL = 4
MAX_BLOCKS = 40
SORTED = TOKENS + BLOCK

BQ0, BK0, LNS, LNB, AB, BQ1, BK1, B2, B1 = 0, 2, 4, 6, 8, 10, 12, 14, 30
EVEN, ODD = B1 + GROUPS * HC, B1 + GROUPS * HC + 1
NBCOL = ODD + 1
BV0, BO0, NXB, BV1, BO1 = range(5)
C_IOTA, C_K, C_128, C_QUAD, C_128K = 0, 32, 32 + 1280, 32 + 1280 + 224, 32 + 1280 + 224 + 10
NROUTE = C_128K + MAX_BLOCKS


def tower(nc, patches, cls, tokw, w0, wx, w1a, w1o, gate, shared, experts0, experts1, bcol, brow,
          ident_in, masks_in, tri_in, route_in, out):
    sorted_x = nc.dram_tensor("sorted_x", (SORTED, D), F32, kind="Internal").ap()
    sorted_y = nc.dram_tensor("sorted_y", (SORTED, D), F32, kind="Internal").ap()

    with ExitStack() as ctx:
        def sb(name, shape, dt=F32):
            return ctx.enter_context(nc.sbuf_tensor(name, shape, dt))

        def sem(name):
            return ctx.enter_context(nc.semaphore(name))

        ring = sb("ring", [128, 4, 4096])
        pat = sb("pat", [128, GROUPS, FC * GT])
        vpad = pat[:, :, 0:HEADS * HPAD].rearrange("p g (h m) -> p g h m", m=HPAD)
        kz = sb("kz", [128, DC, TOKENS])
        tokw_s = kz[:, :, :].rearrange("p c t -> p (c t)")[:, 0:FC * D].rearrange("p (c n) -> p c n", c=FC)
        w0_s = sb("w0_s", [128, 4, DC, D])
        wx_s = sb("wx_s", [128, 2, DC, D])
        wl1 = sb("wl1", [128, 2 * MAX_BLOCKS * EXPERTS])
        w1_s = wl1[:, 0:3 * DC * D].rearrange("p (w c n) -> p w c n", w=3, c=DC)
        w1o_s = wl1[:, 3 * DC * D:3 * DC * D + 4 * D].rearrange("p (c n) -> p c n", c=4)
        tmat = wl1[0:1, :].rearrange("p (a n) -> p a n", a=2)
        gate_s = sb("gate_s", [128, DC, EXPERTS])
        shared_s = sb("shared_s", [128, 2 * DC * INNER + IC * D])
        sgw = shared_s[:, 0:DC * INNER].rearrange("p (c n) -> p c n", c=DC)
        suw = shared_s[:, DC * INNER:2 * DC * INNER].rearrange("p (c n) -> p c n", c=DC)
        sdw = shared_s[:, 2 * DC * INNER:].rearrange("p (c n) -> p c n", c=IC)
        bcol_s = sb("bcol_s", [128, NBCOL])
        brow_s = sb("brow_s", [128, 5, D])
        ident = sb("ident", [128, 128])
        masks = sb("masks", [128, 256 + 2 * GT])
        tri = sb("tri", [GT, GT + 128], BF16)
        route = w0_s[:, :, :, :].rearrange("p w c n -> p (w c n)")[:, 0:NROUTE]
        h = sb("h", [GT, GROUPS, D])
        xA = sb("xA", [128, DC, TOKENS])
        qT = sb("qT", [128, DC, TOKENS])
        kT = sb("kT", [128, DC, TOKENS])
        q1, kE, kO = qT, kT, xA
        vrow = sb("vrow", [128, GROUPS, D])
        x3 = vrow
        oT = sb("oT", [128, DC, TOKENS])
        x3T = oT
        eA = sb("eA", [128, 2, HALF])
        fhT = sb("fhT", [128, HC, GT])
        zA = fhT[:, :, :].rearrange("p c t -> p (c t)").rearrange("p (a n) -> p a n", a=2)
        S = sb("S", [128, 2, HEADS * GT])
        hidT = S[:, :, :].rearrange("p a n -> p (a n)").rearrange("p (c n) -> p c n", c=IC)
        attA = S[:, 0, 0:2 * PT].rearrange("p (a n) -> p a n", a=2)
        clsbuf = S[0:GT, 1, 0:D]
        zrow = S[:, 1, D:2 * D]
        xr = sb("xr", [GT, 2, D])
        xr2 = sb("xr2", [GT, 2, D])
        st = sb("st", [GT, 6])
        mv = sb("mv", [GT, 2])
        var = sb("var", [GT, 1])
        rstd = sb("rstd", [GT, 1])
        slot_seen = sb("slot_seen", [1, 1])
        mhalf = sb("mhalf", [GT, 1])
        cols5 = sb("cols5", [128, 5, DC, GT])
        nT, n2T, xaT, eoT, x2T = (cols5[:, i, :, :] for i in range(5))
        flat5 = cols5[:, :, :, :].rearrange("p a c t -> p (a c t)")
        qz = flat5[:, 0:DC * GT].rearrange("p (c t) -> p c t", c=DC)
        rden = flat5[:, DC * GT:2 * DC * GT].rearrange("p (c t) -> p c t", c=DC)
        valT = flat5[:, HALF:2 * HALF].rearrange("p (a t) -> p a t", a=4)
        nxr = sb("nxr", [GT, D])
        flate = eA[:, :, :].rearrange("p a n -> p (a n)")
        big = flate[0:GT, 0:256].rearrange("p (g e) -> p g e", e=EXPERTS)
        onehot = flate[0:GT, 256:512].rearrange("p (g e) -> p g e", e=EXPERTS)
        before = flate[:, 512:512 + (GROUPS + 1) * EXPERTS].rearrange("p (g e) -> p g e", e=EXPERTS)
        onehot_b = sb("onehot_b", [GT, GROUPS, EXPERTS], BF16)
        lgm = sb("lgm", [GT, 4 * GROUPS])
        slot_i = sb("slot_i", [GT, GROUPS], I32)
        rt = sb("rt", [128, 8, EXPERTS])
        table = sb("table", [1, 2 * MAX_BLOCKS + 1], I32)
        tfl = sb("tfl", [1, 2, MAX_BLOCKS])
        xs = sb("xs", [GT, 2, D])
        xw = xA[:, :, :].rearrange("p c t -> p (c t)")[:, 0:UNROLL * D].rearrange("p (u d) -> p u d", u=UNROLL)
        xwT = kT[:, :, :].rearrange("p c t -> p (c t)")[:, 0:UNROLL * D].rearrange("p (u c t) -> p u c t", u=UNROLL, c=DC)
        sg = S[:, :, :].rearrange("p a n -> p (a n)")[:, 0:2 * INNER].rearrange("p (u n) -> p u n", u=2)
        hw = S[:, :, :].rearrange("p a n -> p (a n)")[:, 2 * INNER:4 * INNER].rearrange("p (u n) -> p u n", u=2)
        yw = qT[:, :, :].rearrange("p c t -> p (c t)")[:, 0:UNROLL * D].rearrange("p (u d) -> p u d", u=UNROLL)
        back = pat[:, :, :].rearrange("p g n -> p (g n)")[:, 0:GROUPS * D].rearrange("p (g d) -> p g d", d=D)

        P = [ctx.enter_context(nc.psum_tensor(f"P{i}", [128, 512], F32)) for i in range(8)]

        names = ("consts ident_in cls_in pat_in tokw_in w0_in wx_in w1_in gate_in shared_in bias_in brow_in route_in "
                 "zeroed tail_zero vpad_zero vec var_ready rstd_ready "
                 "tok_done h0_ready trA_done xA_ready "
                 "qk0_done z0_sum z0_ready exp0_done qk0_ready v0_done v0_ready att_done att_ready oT_done oT_ready "
                 "wo_done n_ready wo_read tr1_done nT_ready n2T_ready xa_done xaT_ready up_done gelu_done down_done eoT_ready "
                 "nx_done nx_sum nx_gelu x2_ready tr2_done x2T_ready qk1_done z1_ready v1_done v1_ready "
                 "m1_ready exp1_done q1_ready z_scan qz_ready den_done den_read qn_ready k1_ready sc_done sc_ready av_done val_ready wo1_done x3_ready tr3_done x3T_ready lg_done "
                 "onehot_ready prefix_done score_ready topv_ready slot_ready table_ready xs_ready scattered "
                 "sg_done silu0_done hid_ready sd_done h_final "
                 "xwt_done xwT_ready gu_done silu_done hw_ready dn_done yw_ready written all_written gathered out_ready stored").split()
        s = {n: sem(n) for n in names}
        ring_in = [sem(f"ring_in{i}") for i in range(4)]
        block_in = [sem(f"block_in{i}") for i in range(4)]
        window_in = [sem(f"window_in{i}") for i in range(4)]
        pat_in = [sem(f"pat_in{i}") for i in range(4)]
        xs_sent = [sem(f"xs_sent{i}") for i in range(2)]
        rows_back = [sem(f"rows_back{i}") for i in range(GROUPS)]

        def gcol(g):
            return slice(g * GT, (g + 1) * GT)

        def bank(b, *shape):
            n = int(np.prod(shape))
            if len(shape) == 1:
                return P[b][:, 0:n]
            return P[b][:, 0:n].rearrange("p (a n) -> p a n", a=shape[0])

        def ptile(i):
            n = min(PT, TOKENS - i * PT)
            return slice(i * PT, i * PT + n), n

        def lagged(steps, stages):
            for t in range(steps):
                for stage, lag in stages:
                    if 0 <= t - lag < GROUPS:
                        stage(t - lag)

        block = ctx.enter_context(nc.Block())

        @block.sync
        def _(sp):
            sp.dma_start(tokw_s[:, :, :], tokw).then_inc(s["tokw_in"], 16)
            for i in range(4):
                sp.dma_start(pat[:, 2 * i:2 * i + 2, :], patches[:, 2 * i:2 * i + 2, :]).then_inc(pat_in[i], 16)
                if i == 0:
                    sp.dma_start(clsbuf, cls).then_inc(s["cls_in"], 16)
                    sp.dma_start(ident[:, :], ident_in).then_inc(s["ident_in"], 16)
            sp.dma_start(w0_s[:, :, :, :], w0).then_inc(s["w0_in"], 16)
            sp.dma_start(bcol_s[:, :], bcol).then_inc(s["bias_in"], 16)
            sp.dma_start(brow_s[:, :, :], brow.partition_broadcast(128)).then_inc(s["brow_in"], 16)
            sp.dma_start(masks[:, :], masks_in).then_inc(s["consts"], 16)
            sp.dma_start(wx_s[:, :, :, :], wx).then_inc(s["wx_in"], 16)
            for e in range(2):
                sp.dma_start(ring[:, e, :], experts0[e]).then_inc(ring_in[e], 16)
            sp.dma_start(w1_s[:, :, :, :], w1a).then_inc(s["w1_in"], 16)
            sp.dma_start(w1o_s[:, :, :], w1o).then_inc(s["w1_in"], 16)
            for e in range(2, 4):
                sp.dma_start(ring[:, e, :], experts0[e]).then_inc(ring_in[e], 16)
            sp.dma_start(gate_s[:, :, :], gate).then_inc(s["gate_in"], 16)
            sp.dma_start(shared_s[:, :], shared).then_inc(s["shared_in"], 16)
            sp.dma_start(tri[:, :], tri_in).then_inc(s["route_in"], 16)
            for e in range(4, GROUPS):
                sp.wait_ge(s["down_done"], e - 3)
                sp.dma_start(ring[:, e - 4, :], experts0[e]).then_inc(ring_in[e - 4], 16)
            sp.wait_ge(s["wo_done"], GROUPS)
            sp.dma_start(route[:, :], route_in).then_inc(s["route_in"], 16)
            sp.wait_ge(s["table_ready"], 1)
            sp.wait_ge(s["down_done"], GROUPS)
            sp.wait_ge(s["scattered"], 16 * GROUPS)
            sp.wait_ge(s["written"], 16)
            sp.wait_ge(s["sc_done"], GROUPS)
            rounds = sp.value_load(table[0:1, 2 * MAX_BLOCKS:2 * MAX_BLOCKS + 1], min_val=1, max_val=MAX_BLOCKS // UNROLL)
            with sp.Fori(0, rounds) as r:
                for u in range(UNROLL):
                    sp.wait_ge(s["dn_done"], r * UNROLL + u + 1)
                    e = sp.value_load(table[0:1, bass.ds(r * UNROLL + u, 1)], min_val=0, max_val=EXPERTS - 1)
                    at = sp.value_load(table[0:1, bass.ds(r * UNROLL + u + MAX_BLOCKS, 1)], min_val=0, max_val=TOKENS)
                    sp.dma_start(xw[:, u, :], sorted_x[bass.ds(at, BLOCK), :]).then_inc(window_in[u], 16)
                    sp.dma_start(ring[:, u, 0:3072], experts1[bass.ds(e, 1)].rearrange("e p n -> (e p) n")).then_inc(block_in[u], 16)
            for g in range(GROUPS):
                sp.wait_ge(s["out_ready"], g + 1)
                sp.dma_start(out[g], h[:, g, :]).then_inc(s["stored"], 16)
            sp.wait_ge(s["stored"], 16 * GROUPS)

        @block.tensor
        def _(pe):
            mm = nc.tensor.matmul

            def rows(b, lhs, rhs, chunks, col=0):
                for c in range(chunks):
                    a = lhs(c)
                    last = mm(P[b][0:a.shape[1], col:col + D], a, rhs(c), start=(c == 0), stop=(c == chunks - 1))
                return last

            def tok(g):
                if g % 2 == 0:
                    pe.wait_ge(pat_in[g // 2], 16)
                if g >= 2:
                    pe.wait_ge(s["h0_ready"], g - 1)
                rows(g % 2, lambda c: pat[:, g, c * GT:(c + 1) * GT], lambda c: tokw_s[:, c, :], FC).then_inc(s["tok_done"], 1)

            def trA(g):
                if g == 0:
                    pe.wait_ge(s["ident_in"], 16)
                pe.wait_ge(s["n_ready"], g + 1)
                if g >= 2:
                    pe.wait_ge(s["xA_ready"], g - 1)
                for c in range(DC):
                    last = nc.tensor.transpose(bank(2 + g % 2, DC, GT)[:, c, :], xr[:, g % 2, c * 128:(c + 1) * 128], ident[0:GT, 0:GT])
                last.then_inc(s["trA_done"], 1)

            nc.tensor.nop().then_inc(s["dn_done"], UNROLL)
            nc.tensor.nop().then_inc(s["gu_done"], 1)
            pe.wait_ge(s["tokw_in"], 16)
            lagged(GROUPS + 2, [(trA, 2), (tok, 0)])

            pe.wait_ge(s["w0_in"], 16)
            pe.wait_ge(s["xA_ready"], GROUPS)
            pe.wait_ge(s["h0_ready"], GROUPS)
            for n in range(8):
                w, m, half = n // 4, (n // 2) % 2, n % 2
                if n >= 4:
                    pe.wait_ge(s["z0_ready"], n - 3)
                for c in range(DC):
                    last = mm(bank(n % 4, HALF), w0_s[:, w, c, m * 128:(m + 1) * 128],
                              xA[:, c, half * HALF:(half + 1) * HALF], start=(c == 0), stop=(c == DC - 1))
                last.then_inc(s["qk0_done"], 1)
            for i in range(PTILES):
                cols, n = ptile(i)
                if i >= 2:
                    pe.wait_ge(s["v0_ready"], i - 1)
                rows(4 + i % 2, lambda c: xA[:, c, cols], lambda c: w0_s[:, 2, c, :], DC).then_inc(s["v0_done"], 1)
            pe.wait_ge(s["qk0_ready"], 8)

            def att(i):
                if i >= PTILES:
                    return
                cols, n = ptile(i)
                if i >= 2:
                    pe.wait_ge(s["att_ready"], i - 1)
                for c in range(DC):
                    last = mm(P[6 + i % 2][0:n, 0:n], kT[:, c, cols], qT[:, c, cols], start=(c == 0), stop=(c == DC - 1))
                last.then_inc(s["att_done"], 1)

            def att_v(i):
                if i >= PTILES:
                    return
                cols, n = ptile(i)
                pe.wait_ge(s["att_ready"], i + 1)
                pe.wait_ge(s["v0_ready"], i + 1)
                if i >= 2:
                    pe.wait_ge(s["oT_ready"], i - 1)
                for c in range(DC):
                    last = mm(bank(i % 2, DC, PT)[:, c, 0:n], vrow[0:n, i, c * 128:(c + 1) * 128], attA[0:n, i % 2, 0:n],
                              start=True, stop=True)
                last.then_inc(s["oT_done"], 1)

            lagged(GROUPS + 1, [(att, 0), (att_v, 1)])

            def wo(g):
                if g == 0:
                    pe.wait_ge(s["oT_ready"], PTILES)
                if g >= 3:
                    pe.wait_ge(s["x2T_ready"], g - 2)
                elif g >= 1:
                    pe.wait_ge(s["wo_read"], g)
                rows(0, lambda c: oT[:, c, gcol(g)], lambda c: w0_s[:, 3, c, :], DC).then_inc(s["wo_done"], 1)

            def tr1(g):
                pe.wait_ge(s["n_ready"], GROUPS + 2 * g + 2)
                if g >= 1:
                    pe.wait_ge(s["n2T_ready"], g)
                    pe.wait_ge(s["nT_ready"], g)
                for a, src in ((0, xr), (2, xr2)):
                    for c in range(DC):
                        last = nc.tensor.transpose(bank(1, 4, GT)[:, a + c, :], src[:, g % 2, c * 128:(c + 1) * 128], ident[0:GT, 0:GT])
                last.then_inc(s["tr1_done"], 1)

            def xa(g):
                pe.wait_ge(s["n2T_ready"], g + 1)
                if g >= 1:
                    pe.wait_ge(s["xaT_ready"], g)
                for m in range(DC):
                    for c in range(DC):
                        last = mm(bank(2, DC, GT)[:, m, :], wx_s[:, 0, c, m * 128:(m + 1) * 128], n2T[:, c, :],
                                  start=(c == 0), stop=(c == DC - 1))
                last.then_inc(s["xa_done"], 1)

            def up(g):
                pe.wait_ge(ring_in[g % 4], 16 * (g // 4 + 1))
                pe.wait_ge(s["xaT_ready"], g + 1)
                w = ring[:, g % 4, 0:DC * HIDDEN].rearrange("p (c n) -> p c n", c=DC)
                for m in range(HC):
                    if g >= 1 and m % 4 == 0:
                        pe.wait_ge(s["gelu_done"], HC * (g - 1) + m + 4)
                    for c in range(DC):
                        last = mm(bank(3 + m // 4, 4, GT)[:, m % 4, :], w[:, c, m * 128:(m + 1) * 128], xaT[:, c, :],
                                  start=(c == 0), stop=(c == DC - 1))
                    if m % 4 == 3:
                        last.then_inc(s["up_done"], 1)

            def down(g):
                if g >= 1:
                    pe.wait_ge(s["nx_sum"], g)
                w = ring[:, g % 4, DC * HIDDEN:].rearrange("p (c n) -> p c n", c=HC)
                pe.wait_ge(s["gelu_done"], HC * (g + 1))
                for m in range(DC):
                    for c in range(HC):
                        last = mm(P[5][:, m * GT:(m + 1) * GT], w[:, c, m * 128:(m + 1) * 128], fhT[:, c, :],
                                  start=(c == 0), stop=(c == HC - 1))
                last.then_inc(s["down_done"], 1)

            def nx(g):
                pe.wait_ge(s["eoT_ready"], g + 1)
                rows(5, lambda c: eoT[:, c, :], lambda c: wx_s[:, 1, c, :], DC, col=256).then_inc(s["nx_done"], 1)

            def tr2(g):
                pe.wait_ge(s["x2_ready"], g + 1)
                pe.wait_ge(s["wo_read"], min(g + 3, GROUPS))
                for c in range(DC):
                    last = nc.tensor.transpose(P[0][:, 256 + c * GT:256 + (c + 1) * GT], xs[:, g % 2, c * 128:(c + 1) * 128], ident[0:GT, 0:GT])
                last.then_inc(s["tr2_done"], 1)

            def qk1(g):
                pe.wait_ge(s["x2T_ready"], g + 1)
                if g == 0:
                    pe.wait_ge(s["w1_in"], 32)
                else:
                    pe.wait_ge(s["z1_ready"], g)
                for w in range(2):
                    for m in range(DC):
                        for c in range(DC):
                            last = mm(bank(6, 4, GT)[:, 2 * w + m, :], w1_s[:, w, c, m * 128:(m + 1) * 128], x2T[:, c, :],
                                      start=(c == 0), stop=(c == DC - 1))
                last.then_inc(s["qk1_done"], 1)

            def v1(g):
                if g >= 1:
                    pe.wait_ge(s["v1_ready"], g)
                rows(7, lambda c: x2T[:, c, :], lambda c: w1_s[:, 2, c, :], DC).then_inc(s["v1_done"], 1)

            pe.wait_ge(s["wx_in"], 16)
            lagged(GROUPS + 3, [(tr1, 1), (tr2, 3), (nx, 2), (xa, 1), (wo, 0), (up, 1), (qk1, 3), (v1, 3), (down, 1)])

            def scores(g):
                pe.wait_ge(s["k1_ready"], 2 * (g + 1))
                pe.wait_ge(s["qn_ready"], g + 1)
                if g >= 1:
                    pe.wait_ge(s["sc_ready"], 4 * g)
                for c in range(DC):
                    for odd, k in ((0, kE), (1, kO)):
                        for r in range(4):
                            last = mm(bank(r, 4, GT)[0:GT, 2 * c + odd, :], k[32 * r:32 * r + 32, c, gcol(g)],
                                      q1[32 * r:32 * r + 32, c, gcol(g)], start=True, stop=True, tile_position=(32 * r, 0))
                last.then_inc(s["sc_done"], 1)

            def av(g):
                pe.wait_ge(s["sc_ready"], 4 * (g + 1))
                if g == 0:
                    pe.wait_ge(s["v1_ready"], GROUPS)
                else:
                    pe.wait_ge(s["val_ready"], g)
                for b in range(4):
                    for r in range(4):
                        head = 8 * (b // 2) + 2 * r + b % 2
                        sc = S[0:GT, g % 2, (r * 4 + b) * GT:(r * 4 + b + 1) * GT]
                        last = mm(bank(4, 4, GT)[32 * r:32 * r + 32, b, :], vpad[0:GT, g, head, :], sc, start=True, stop=True,
                                  tile_position=(0, 32 * r))
                last.then_inc(s["av_done"], 1)

            def den(g):
                pe.wait_ge(s["qz_ready"], g + 1)
                if g >= 1:
                    pe.wait_ge(s["den_read"], g)
                for c in range(DC):
                    last = mm(bank(5, DC, GT)[:, c, :], masks[:, 128 + 2 * GT:], qz[:, c, :], start=True, stop=True)
                last.then_inc(s["den_done"], 1)

            def wo1(g):
                pe.wait_ge(s["val_ready"], g + 1)
                if g >= 1:
                    pe.wait_ge(s["h0_ready"], 2 * GROUPS + g)
                rows(6, lambda c: valT[:, c, :], lambda c: w1o_s[:, c, :], 4).then_inc(s["wo1_done"], 1)

            def tr3(g):
                pe.wait_ge(s["x3_ready"], g + 1)
                if g >= 1:
                    pe.wait_ge(s["x3T_ready"], g)
                for c in range(DC):
                    last = nc.tensor.transpose(bank(7, DC, GT)[:, c, :], x3[0:GT, g, c * 128:(c + 1) * 128], ident[0:GT, 0:GT])
                last.then_inc(s["tr3_done"], 1)

            pe.wait_ge(s["zeroed"], 1)
            lagged(GROUPS + 5, [(wo1, 4), (den, 1), (av, 3), (tr3, 5), (scores, 2)])

            pe.wait_ge(s["gate_in"], 16)
            pe.wait_ge(s["h0_ready"], 3 * GROUPS)
            for g in range(GROUPS):
                pe.wait_ge(s["x3T_ready"], g + 1)
                for c in range(DC):
                    last = mm(P[6][0:GT, g * EXPERTS:(g + 1) * EXPERTS], x3T[:, c, gcol(g)], gate_s[:, c, :],
                              start=(c == 0), stop=(c == DC - 1))
            last.then_inc(s["lg_done"], 1)

            pe.wait_ge(s["shared_in"], 16)

            def shared_up(n):
                m, half = n // 2, n % 2
                if n >= 2:
                    pe.wait_ge(s["hid_ready"], n - 1)
                for b, w in ((n % 2, sgw), (2 + n % 2, suw)):
                    for c in range(DC):
                        last = mm(bank(b, HALF), w[:, c, m * 128:(m + 1) * 128], x3T[:, c, half * HALF:(half + 1) * HALF],
                                  start=(c == 0), stop=(c == DC - 1))
                last.then_inc(s["sg_done"], 1)

            for n in range(3):
                shared_up(n)
            pe.wait_ge(s["onehot_ready"], 1)
            pe.wait_ge(s["route_in"], 32)
            mm(P[4][0:GT, 0:256], tri[:, 0:GT], onehot_b[:, :, :].rearrange("p g e -> p (g e)"), start=True, stop=True)
            mm(P[5][:, 0:256], tri[:, GT:GT + 128], onehot_b[:, :, :].rearrange("p g e -> p (g e)"), start=True, stop=True)\
                .then_inc(s["prefix_done"], 1)
            for n in range(3, 2 * IC):
                shared_up(n)
            pe.wait_ge(s["hid_ready"], 2 * IC)
            for g in range(GROUPS):
                if g >= 2:
                    pe.wait_ge(s["h_final"], g - 1)
                rows(6 + g % 2, lambda c: hidT[:, c, gcol(g)], lambda c: sdw[:, c, :], IC).then_inc(s["sd_done"], 1)

            pe.wait_ge(s["h_final"], GROUPS)
            pe.wait_ge(s["slot_ready"], 1)
            rounds = pe.value_load(table[0:1, 2 * MAX_BLOCKS:2 * MAX_BLOCKS + 1], min_val=1, max_val=MAX_BLOCKS // UNROLL)
            with pe.Fori(0, rounds) as r:
                def window_t(u):
                    pe.wait_ge(window_in[u], 16 * (r + 1))
                    pe.wait_ge(s["xwT_ready"], r * UNROLL + u + 1)
                    for c in range(DC):
                        last = nc.tensor.transpose(bank((4, 7)[u % 2], DC, BLOCK)[:, c, :], xw[:, u, c * 128:(c + 1) * 128], ident[:, :])
                    last.then_inc(s["xwt_done"], 1)

                def gate_up(u):
                    gw = ring[:, u, 0:1024].rearrange("p (c n) -> p c n", c=DC)
                    uw = ring[:, u, 1024:2048].rearrange("p (c n) -> p c n", c=DC)
                    pe.wait_ge(block_in[u], 16 * (r + 1))
                    pe.wait_ge(s["xwT_ready"], r * UNROLL + u + 3)
                    pe.wait_ge(s["hw_ready"], r * UNROLL + u + 1)
                    for b, w in ((u % 2, gw), (2 + u % 2, uw)):
                        for m in range(IC):
                            for c in range(DC):
                                last = mm(bank(b, IC, BLOCK)[:, m, :], w[:, c, m * 128:(m + 1) * 128], xwT[:, u, c, :],
                                          start=(c == 0), stop=(c == DC - 1))
                        last.then_inc(s["gu_done"], 1)

                def down_rows(u):
                    dw = ring[:, u, 2048:3072].rearrange("p (c n) -> p c n", c=IC)
                    pe.wait_ge(s["hw_ready"], r * UNROLL + u + 3)
                    pe.wait_ge(s["yw_ready"], r * UNROLL + u + 1)
                    rows(5 + u % 2, lambda c: hw[:, u % 2, c * BLOCK:(c + 1) * BLOCK], lambda c: dw[:, c, :], IC)\
                        .then_inc(s["dn_done"], 1)

                for step, u in ((window_t, 0), (window_t, 1), (gate_up, 0), (gate_up, 1), (window_t, 2), (window_t, 3),
                                (down_rows, 0), (down_rows, 1), (gate_up, 2), (gate_up, 3), (down_rows, 2), (down_rows, 3)):
                    step(u)

        @block.scalar
        def _(act):
            A = nc.scalar.activation

            for g in range(GROUPS):
                act.wait_ge(s["trA_done"], g + 1)
                for c in range(DC):
                    dst = xA[:, c, :].rearrange("p (b i) -> p i b", i=IMAGES)[:, GI * g:GI * (g + 1), :]
                    src = bank(2 + g % 2, DC, GT)[:, c, :].rearrange("p (i b) -> p i b", b=POSITIONS)
                    last = A(dst, src, ACT.Copy)
                last.then_inc(s["xA_ready"], 1)
            act.wait_ge(s["bias_in"], 16)
            for n in range(8):
                act.wait_ge(s["z0_ready"], n + 1)
                A(eA[:, n % 2, :], eA[:, n % 2, :], ACT.Exp).then_inc(s["exp0_done"], 1)
            for i in range(PTILES):
                cols, n = ptile(i)
                act.wait_ge(s["oT_done"], i + 1)
                for c in range(DC):
                    dst = oT[:, c, :].rearrange("p (i b) -> p b i", b=POSITIONS)[:, 4 * i:4 * i + n // IMAGES, :]
                    src = bank(i % 2, DC, PT)[:, c, 0:n].rearrange("p (b i) -> p b i", i=IMAGES)
                    last = A(dst, src, ACT.Copy)
                last.then_inc(s["oT_ready"], 1)

            def nT_evac(g):
                act.wait_ge(s["tr1_done"], g + 1)
                if g >= 1:
                    act.wait_ge(s["xa_done"], g)
                for c in range(DC):
                    last = A(n2T[:, c, :], bank(1, 4, GT)[:, 2 + c, :], ACT.Identity, bias=bcol_s[:, LNB + c:LNB + c + 1],
                             scale=bcol_s[:, LNS + c:LNS + c + 1])
                last.then_inc(s["n2T_ready"], 1)
                if g >= 1:
                    act.wait_ge(s["xaT_ready"], g)
                for c in range(DC):
                    last = A(nT[:, c, :], bank(1, 4, GT)[:, c, :], ACT.Identity, bias=bcol_s[:, AB + c:AB + c + 1])
                last.then_inc(s["nT_ready"], 1)

            def gelu_up(g):
                if g >= 1:
                    act.wait_ge(s["down_done"], g)
                for m in range(HC):
                    if m % 4 == 0:
                        act.wait_ge(s["up_done"], 2 * g + m // 4 + 1)
                    A(fhT[:, m, :], bank(3 + m // 4, 4, GT)[:, m % 4, :], ACT.Gelu, bias=bcol_s[:, B1 + HC * g + m:B1 + HC * g + m + 1])\
                        .then_inc(s["gelu_done"], 1)

            def gelu_nx(g):
                act.wait_ge(s["nx_sum"], g + 1)
                A(nxr[:, :], nxr[:, :], ACT.Gelu).then_inc(s["nx_gelu"], 1)

            def x2_evac(g):
                act.wait_ge(s["tr2_done"], g + 1)
                if g >= 1:
                    act.wait_ge(s["v1_done"], g)
                A(x2T[:, :, :].rearrange("p c t -> p (c t)"), P[0][:, 256:256 + DC * GT], ACT.Copy).then_inc(s["x2T_ready"], 1)

            lagged(GROUPS + 3, [(nT_evac, 1), (x2_evac, 3), (gelu_nx, 2), (gelu_up, 1)])

            def exp1(g):
                act.wait_ge(s["m1_ready"], g + 1)
                A(kE[:, :, gcol(g)], kE[:, :, gcol(g)], ACT.Exp)
                A(kO[:, :, gcol(g)], kO[:, :, gcol(g)], ACT.Exp).then_inc(s["exp1_done"], 1)

            def k_evac(g):
                act.wait_ge(s["q1_ready"], g + 1)
                for dst, m in ((kE, EVEN), (kO, ODD)):
                    A(dst[:, :, gcol(g)], kz[:, :, gcol(g)], ACT.Copy, scale=bcol_s[:, m:m + 1]).then_inc(s["k1_ready"], 1)

            def val_evac(g):
                act.wait_ge(s["av_done"], g + 1)
                if g >= 1:
                    act.wait_ge(s["wo1_done"], g)
                A(valT[:, :, :].rearrange("p a t -> p (a t)"), bank(4, HALF), ACT.Copy).then_inc(s["val_ready"], 1)

            def x3_evac(g):
                act.wait_ge(s["tr3_done"], g + 1)
                A(x3T[:, :, gcol(g)], bank(7, DC, GT), ACT.Copy).then_inc(s["x3T_ready"], 1)

            exp1(0)
            lagged(GROUPS + 5, [(lambda g: g + 1 < GROUPS and exp1(g + 1), 0), (k_evac, 1), (val_evac, 3), (x3_evac, 5)])

            act.wait_ge(s["topv_ready"], 1)
            A(lgm[:, GROUPS:2 * GROUPS], lgm[:, 0:GROUPS], ACT.Sigmoid).then_inc(s["score_ready"], 1)
            for n in range(2 * IC):
                act.wait_ge(s["sg_done"], n + 1)
                if n >= 2:
                    act.wait_ge(s["hid_ready"], n - 1)
                A(zA[:, n % 2, :], bank(n % 2, HALF), ACT.Silu).then_inc(s["silu0_done"], 1)

            act.wait_ge(s["slot_ready"], 1)
            act.wait_ge(s["sd_done"], GROUPS)
            rounds = act.value_load(table[0:1, 2 * MAX_BLOCKS:2 * MAX_BLOCKS + 1], min_val=1, max_val=MAX_BLOCKS // UNROLL)
            with act.Fori(0, rounds) as r:
                for u in range(UNROLL):
                    act.wait_ge(s["gu_done"], 2 * (r * UNROLL + u) + 2)
                    act.wait_ge(s["hw_ready"], r * UNROLL + u + 1)
                    A(sg[:, u % 2, :], P[u % 2][:, :], ACT.Silu).then_inc(s["silu_done"], 1)

        @block.vector
        def _(dve):
            V = nc.vector
            chain = [0]

            def link(ins):
                chain[0] += 1
                ins.then_inc(s["vec"], 1)
                dve.wait_ge(s["vec"], chain[0])

            norms = [0]

            def norm(src, dst, done):
                link(V.bn_stats(st[:, :], src))
                link(V.bn_aggr(mv[:, :], st[:, :]))
                V.tensor_scalar_add(var[:, :], mv[:, 1:2], EPS).then_inc(s["var_ready"], 1)
                norms[0] += 1
                dve.wait_ge(s["rstd_ready"], norms[0])
                V.tensor_scalar(dst, src, mv[:, 0:1], rstd[:, :], ALU.subtract, ALU.mult).then_inc(s[done], 1)

            V.memset(mhalf[:, :], -0.5).then_inc(s["zeroed"], 1)

            dve.wait_ge(s["cls_in"], 16)
            for g in range(GROUPS):
                dve.wait_ge(s["tok_done"], g + 1)
                V.tensor_tensor(h[:, g, :], P[g % 2][0:GT, 0:D], clsbuf, ALU.add).then_inc(s["h0_ready"], 1)
                dve.wait_ge(s["h0_ready"], g + 1)
                if g >= 2:
                    dve.wait_ge(s["trA_done"], g - 1)
                norm(h[:, g, :], xr[:, g % 2, :], "n_ready")

            dve.wait_ge(s["bias_in"], 16)
            for n in range(9):
                if n < 8:
                    b = (BQ0, BK0)[n // 4] + (n // 2) % 2
                    dve.wait_ge(s["qk0_done"], n + 1)
                    if n >= 2:
                        dve.wait_ge(s["qk0_ready"], n - 1)
                    V.tensor_scalar(zA[:, n % 2, :], bank(n % 4, HALF), bcol_s[:, b:b + 1], None, ALU.add).then_inc(s["z0_sum"], 1)
                    dve.wait_ge(s["z0_sum"], n + 1)
                    V.tensor_scalar_min(eA[:, n % 2, :], zA[:, n % 2, :], 0.0).then_inc(s["z0_ready"], 1)
                if n == 0:
                    continue
                n -= 1
                w, m, half = n // 4, (n // 2) % 2, n % 2
                dve.wait_ge(s["exp0_done"], n + 1)
                V.scalar_tensor_tensor((qT, kT)[w][:, m, half * HALF:(half + 1) * HALF], zA[:, n % 2, :], 0.0, eA[:, n % 2, :],
                                       ALU.max, ALU.add).then_inc(s["qk0_ready"], 1)
            dve.wait_ge(s["brow_in"], 16)
            for i in range(PTILES):
                cols, n = ptile(i)
                dve.wait_ge(s["v0_done"], i + 1)
                V.tensor_tensor(vrow[0:n, i, :], P[4 + i % 2][0:n, 0:D], brow_s[0:n, BV0, :], ALU.add).then_inc(s["v0_ready"], 1)
            dve.wait_ge(s["consts"], 16)
            for i in range(PTILES):
                cols, n = ptile(i)
                dve.wait_ge(s["att_done"], i + 1)
                if i >= 2:
                    dve.wait_ge(s["oT_done"], i - 1)
                V.tensor_tensor(attA[0:n, i % 2, 0:n], P[6 + i % 2][0:n, 0:n], masks[0:n, 0:n], ALU.mult).then_inc(s["att_ready"], 1)

            def h1_norms(g):
                dve.wait_ge(s["wo_done"], g + 1)
                V.tensor_tensor(xr2[:, g % 2, :], P[0][0:GT, 0:D], brow_s[0:GT, BO0, :], ALU.add).then_inc(s["wo_read"], 1)
                dve.wait_ge(s["wo_read"], g + 1)
                V.tensor_tensor(h[:, g, :], h[:, g, :], xr2[:, g % 2, :], ALU.add).then_inc(s["h0_ready"], 1)
                dve.wait_ge(s["h0_ready"], GROUPS + g + 1)
                norm(h[:, g, :], xr[:, g % 2, :], "n_ready")
                dve.wait_ge(s["n_ready"], GROUPS + 2 * g + 1)
                norm(xr[:, g % 2, :], xr2[:, g % 2, :], "n_ready")

            def xa_evac(g):
                dve.wait_ge(s["xa_done"], g + 1)
                dve.wait_ge(s["nT_ready"], g + 1)
                if g >= 1:
                    dve.wait_ge(s["up_done"], 2 * g)
                V.tensor_tensor(xaT[:, :, :], bank(2, DC, GT), nT[:, :, :], ALU.add).then_inc(s["xaT_ready"], 1)

            def eo_evac(g):
                dve.wait_ge(s["down_done"], g + 1)
                if g >= 1:
                    dve.wait_ge(s["nx_done"], g)
                for c in range(DC):
                    last = V.tensor_scalar(eoT[:, c, :], P[5][:, c * GT:(c + 1) * GT], bcol_s[:, B2 + DC * g + c:B2 + DC * g + c + 1], None, ALU.add)
                last.then_inc(s["eoT_ready"], 1)

            def nx_evac(g):
                dve.wait_ge(s["nx_done"], g + 1)
                V.tensor_tensor(nxr[:, :], P[5][0:GT, 256:512], brow_s[0:GT, NXB, :], ALU.add).then_inc(s["nx_sum"], 1)

            def h2_norm(g):
                dve.wait_ge(s["nx_gelu"], g + 1)
                link(V.tensor_tensor(h[:, g, :], h[:, g, :], nxr[:, :], ALU.add))
                norm(h[:, g, :], xs[:, g % 2, :], "x2_ready")

            def z_evac(g):
                dve.wait_ge(s["qk1_done"], g + 1)
                for w, dst in ((0, q1), (1, kz)):
                    for c in range(DC):
                        b = (BQ1, BK1)[w] + c
                        last = V.tensor_scalar(dst[:, c, gcol(g)], bank(6, 4, GT)[:, 2 * w + c, :], bcol_s[:, b:b + 1], None, ALU.add)
                last.then_inc(s["z1_ready"], 1)
                dve.wait_ge(s["z1_ready"], g + 1)
                V.tensor_scalar_min(kE[:, :, gcol(g)], q1[:, :, gcol(g)], 0.0)
                V.tensor_scalar_min(kO[:, :, gcol(g)], kz[:, :, gcol(g)], 0.0).then_inc(s["m1_ready"], 1)

            def v_evac(g):
                dve.wait_ge(s["v1_done"], g + 1)
                if g == 0:
                    dve.wait_ge(s["vpad_zero"], 1)
                V.tensor_tensor(vpad[0:GT, g, :, 0:HD], P[7][0:GT, 0:D].rearrange("p (h m) -> p h m", m=HD),
                                brow_s[0:GT, BV1, :].rearrange("p (h m) -> p h m", m=HD), ALU.add).then_inc(s["v1_ready"], 1)

            lagged(GROUPS + 3, [(nx_evac, 2), (xa_evac, 1), (h2_norm, 2), (h1_norms, 0), (z_evac, 3), (v_evac, 3), (eo_evac, 1)])

            def elu1(g):
                dve.wait_ge(s["exp1_done"], g + 1)
                for e, src in ((kE, q1), (kO, kz)):
                    last = V.scalar_tensor_tensor(src[:, :, gcol(g)], src[:, :, gcol(g)], 0.0, e[:, :, gcol(g)], ALU.max, ALU.add)
                last.then_inc(s["q1_ready"], 1)
                dve.wait_ge(s["q1_ready"], g + 1)
                if g >= 1:
                    dve.wait_ge(s["den_done"], g)
                for c in range(DC):
                    last = V.tensor_tensor_scan(qz[:, c, :], masks[:, 128 + GT:128 + 2 * GT], kz[:, c, gcol(g)], 0.0, ALU.mult, ALU.add)
                last.then_inc(s["z_scan"], 1)
                dve.wait_ge(s["z_scan"], g + 1)
                V.tensor_tensor(qz[:, :, :], qz[:, :, :], q1[:, :, gcol(g)], ALU.mult).then_inc(s["qz_ready"], 1)

            def norm_q(g):
                dve.wait_ge(s["den_done"], g + 1)
                V.tensor_scalar_add(rden[:, :, :], bank(5, DC, GT), 1e-6).then_inc(s["den_read"], 1)
                dve.wait_ge(s["den_read"], g + 1)
                link(V.reciprocal(rden[:, :, :], rden[:, :, :]))
                V.tensor_tensor(q1[:, :, gcol(g)], q1[:, :, gcol(g)], rden[:, :, :], ALU.mult).then_inc(s["qn_ready"], 1)

            def mask_scores(g):
                dve.wait_ge(s["sc_done"], g + 1)
                if g == 1:
                    dve.wait_ge(s["written"], 16)
                if g >= 2:
                    dve.wait_ge(s["av_done"], g - 1)
                causal = masks[0:GT, 128:128 + GT].unsqueeze(1).to_broadcast([GT, 4, GT])
                for r in range(4):
                    dst = S[0:GT, g % 2, r * 4 * GT:(r + 1) * 4 * GT].rearrange("p (a t) -> p a t", a=4)
                    V.tensor_tensor(dst, bank(r, 4, GT)[0:GT, :, :], causal, ALU.mult).then_inc(s["sc_ready"], 1)

            def h3_norm(g):
                dve.wait_ge(s["wo1_done"], g + 1)
                link(V.tensor_tensor(xr[:, 0, :], P[6][0:GT, 0:D], brow_s[0:GT, BO1, :], ALU.add))
                V.tensor_tensor(h[:, g, :], h[:, g, :], xr[:, 0, :], ALU.add).then_inc(s["h0_ready"], 1)
                dve.wait_ge(s["h0_ready"], 2 * GROUPS + g + 1)
                norm(h[:, g, :], x3[0:GT, g, :], "x3_ready")

            lagged(GROUPS + 4, [(mask_scores, 3), (elu1, 0), (norm_q, 1), (h3_norm, 4)])

            logits = P[6][0:GT, 0:256].rearrange("p (g e) -> p g e", e=EXPERTS)
            iota = route[0:GT, C_IOTA:C_IOTA + EXPERTS].unsqueeze(1).to_broadcast([GT, GROUPS, EXPERTS])
            dve.wait_ge(s["lg_done"], 1)
            dve.wait_ge(s["route_in"], 32)

            def per_group(col):
                return lgm[:, col * GROUPS:(col + 1) * GROUPS].unsqueeze(2).to_broadcast([GT, GROUPS, EXPERTS])

            V.tensor_reduce(lgm[:, 0:GROUPS], logits, AX.X, ALU.max).then_inc(s["topv_ready"], 1)
            dve.wait_ge(s["topv_ready"], 1)
            link(V.tensor_tensor(big[:, :, :], logits, per_group(0), ALU.is_equal))
            link(V.tensor_tensor(big[:, :, :], big[:, :, :], iota, ALU.mult))
            link(V.tensor_reduce(lgm[:, 2 * GROUPS:3 * GROUPS], big[:, :, :], AX.X, ALU.min))
            V.tensor_tensor(onehot_b[:, :, :], iota, per_group(2), ALU.is_equal).then_inc(s["onehot_ready"], 1)
            link(V.tensor_tensor(onehot[:, :, :], iota, per_group(2), ALU.is_equal))

            def hidden(n):
                m, half = n // 2, n % 2
                dve.wait_ge(s["silu0_done"], n + 1)
                V.tensor_tensor(hidT[:, m, half * HALF:(half + 1) * HALF], zA[:, n % 2, :], bank(2 + n % 2, HALF), ALU.mult)\
                    .then_inc(s["hid_ready"], 1)

            hidden(0)
            hidden(1)
            dve.wait_ge(s["prefix_done"], 1)
            link(V.memset(before[:, 0, :], 0.0))
            for g in range(GROUPS):
                link(V.tensor_tensor(before[:, g + 1, :], before[:, g, :], P[5][:, g * EXPERTS:(g + 1) * EXPERTS], ALU.add))
            hidden(2)
            link(V.memset(rt[:, 7, :], 0.0))
            count = before[:, GROUPS, :]
            link(V.tensor_tensor_scan(rt[:, 0, :], count, rt[:, 7, :], 0.0, ALU.add, ALU.add))
            link(V.tensor_tensor(rt[:, 1, :], rt[:, 0, :], count, ALU.subtract))
            link(V.tensor_tensor(big[:, :, :], P[4][0:GT, 0:256].rearrange("p (g e) -> p g e", e=EXPERTS), before[0:GT, 0:GROUPS, :], ALU.add))
            link(V.tensor_tensor(big[:, :, :], big[:, :, :], rt[0:GT, 1, :].unsqueeze(1).to_broadcast([GT, GROUPS, EXPERTS]), ALU.add))
            link(V.tensor_tensor(big[:, :, :], big[:, :, :], onehot[:, :, :], ALU.mult))
            link(V.tensor_reduce(lgm[:, 3 * GROUPS:4 * GROUPS], big[:, :, :], AX.X, ALU.add))
            V.tensor_copy(slot_i[:, :], lgm[:, 3 * GROUPS:4 * GROUPS]).then_inc(s["slot_ready"], 1)
            dve.wait_ge(s["score_ready"], 1)
            for g in range(GROUPS):
                if g >= 2:
                    dve.wait_ge(xs_sent[g % 2], 16 * (g // 2))
                V.tensor_scalar(xs[:, g % 2, :], x3[0:GT, g, :], lgm[:, GROUPS + g:GROUPS + g + 1], None, ALU.mult).then_inc(s["xs_ready"], 1)
                if g % 4 == 3:
                    hidden(3 + g // 4)

            link(V.tensor_tensor(tmat[:, 0, 0:7 * EXPERTS].rearrange("p (e m) -> p e m", m=7), count[0:1, :].unsqueeze(2).to_broadcast([1, EXPERTS, 7]),
                                 route[0:1, C_128:C_128 + 7 * EXPERTS].rearrange("p (e m) -> p e m", m=7), ALU.is_gt))
            link(V.tensor_reduce(rt[0:1, 2, :], tmat[:, 0, 0:7 * EXPERTS].rearrange("p (e m) -> p e m", m=7), AX.X, ALU.add))
            link(V.tensor_tensor_scan(rt[0:1, 3, :], rt[0:1, 2, :], rt[0:1, 7, :], 0.0, ALU.add, ALU.add))
            link(V.tensor_tensor(rt[0:1, 4, :], rt[0:1, 3, :], rt[0:1, 2, :], ALU.subtract))
            link(V.tensor_scalar(rt[0:1, 5, :], rt[0:1, 4, :], float(-BLOCK), None, ALU.mult))
            link(V.tensor_tensor(rt[0:1, 5, :], rt[0:1, 5, :], rt[0:1, 1, :], ALU.add))

            hidden(5)

            def row(i):
                return rt[0:1, i, :].unsqueeze(1).to_broadcast([1, MAX_BLOCKS, EXPERTS])

            def mat(i):
                return tmat[:, i, :].rearrange("p (k e) -> p k e", e=EXPERTS)

            kk = route[0:1, C_K:C_K + MAX_BLOCKS * EXPERTS].rearrange("p (k e) -> p k e", e=EXPERTS)
            link(V.tensor_tensor(mat(0), row(3), kk, ALU.is_le))
            link(V.tensor_reduce(tfl[:, 0, :], mat(0), AX.X, ALU.add))
            V.tensor_scalar_min(table[:, 0:MAX_BLOCKS], tfl[:, 0, :], float(EXPERTS - 1))
            hidden(6)
            link(V.tensor_tensor(mat(1), row(4), kk, ALU.is_le))
            link(V.tensor_tensor(mat(1), mat(1), mat(0), ALU.subtract))
            link(V.tensor_tensor(mat(1), mat(1), row(5), ALU.mult))
            link(V.tensor_reduce(tfl[:, 1, :], mat(1), AX.X, ALU.add))
            link(V.tensor_tensor(tfl[:, 1, :], tfl[:, 1, :], route[0:1, C_128K:C_128K + MAX_BLOCKS], ALU.add))
            V.tensor_scalar_min(table[:, MAX_BLOCKS:2 * MAX_BLOCKS], tfl[:, 1, :], float(TOKENS))
            link(V.tensor_tensor(tfl[:, 0, 0:10], rt[0:1, 3, EXPERTS - 1:EXPERTS].to_broadcast([1, 10]), route[0:1, C_QUAD:C_QUAD + 10], ALU.is_gt))
            link(V.tensor_reduce(tfl[:, 1, 0:1], tfl[:, 0, 0:10], AX.X, ALU.add))
            V.tensor_copy(table[:, 2 * MAX_BLOCKS:2 * MAX_BLOCKS + 1], tfl[:, 1, 0:1]).then_inc(s["table_ready"], 1)

            hidden(7)
            for g in range(GROUPS):
                dve.wait_ge(s["sd_done"], g + 1)
                V.tensor_tensor(h[:, g, :], h[:, g, :], P[6 + g % 2][0:GT, 0:D], ALU.add).then_inc(s["h_final"], 1)

            for n in ("xwT_ready", "hw_ready", "yw_ready"):
                nc.vector.engine_nop().then_inc(s[n], 2)
            dve.wait_ge(s["table_ready"], 1)
            rounds = dve.value_load(table[0:1, 2 * MAX_BLOCKS:2 * MAX_BLOCKS + 1], min_val=1, max_val=MAX_BLOCKS // UNROLL)
            with dve.Fori(0, rounds) as r:
                def window_cols(u):
                    dve.wait_ge(s["xwt_done"], r * UNROLL + u + 1)
                    dve.wait_ge(s["gu_done"], 2 * r * UNROLL + 1)
                    V.tensor_copy(xwT[:, u, :, :], bank((4, 7)[u % 2], DC, BLOCK)).then_inc(s["xwT_ready"], 1)

                def hidden_cols(u):
                    dve.wait_ge(s["silu_done"], r * UNROLL + u + 1)
                    dve.wait_ge(s["gu_done"], 2 * (r * UNROLL + u + 1) + 1)
                    dve.wait_ge(s["dn_done"], r * UNROLL + u + UNROLL - 1)
                    V.tensor_tensor(hw[:, u % 2, :], sg[:, u % 2, :], P[2 + u % 2][:, :], ALU.mult).then_inc(s["hw_ready"], 1)

                def rows_out(u):
                    dve.wait_ge(s["dn_done"], r * UNROLL + u + UNROLL + 1)
                    dve.wait_ge(s["written"], 16 * UNROLL * r + 16)
                    V.tensor_copy(yw[:, u, :], P[5 + u % 2][:, 0:D]).then_inc(s["yw_ready"], 1)

                for step, u in ((window_cols, 0), (window_cols, 1), (hidden_cols, 0), (hidden_cols, 1), (window_cols, 2),
                                (window_cols, 3), (rows_out, 0), (rows_out, 1), (hidden_cols, 2), (hidden_cols, 3), (rows_out, 2),
                                (rows_out, 3)):
                    step(u)

            for g in range(GROUPS):
                dve.wait_ge(rows_back[g], 16)
                V.tensor_tensor(h[:, g, :], h[:, g, :], back[0:GT, g, :], ALU.add).then_inc(s["out_ready"], 1)

        @block.gpsimd
        def _(pool):
            nc.gpsimd.memset(zrow, 0.0).then_inc(s["tail_zero"], 1)
            pool.wait_ge(s["tail_zero"], 1)
            pool.dma_start(sorted_x[TOKENS:SORTED, :], zrow).then_inc(s["written"], 16)
            pool.wait_ge(s["zeroed"], 1)

            def power(n):
                pool.wait_ge(s["var_ready"], n + 1)
                nc.gpsimd.tensor_tensor(rstd[:, :], var[:, :], mhalf[:, :], ALU.pow).then_inc(s["rstd_ready"], 1)

            for n in range(GROUPS):
                power(n)
            pool.wait_ge(s["tok_done"], GROUPS)
            nc.gpsimd.memset(pat[:, :, :], 0.0).then_inc(s["vpad_zero"], 1)
            for n in range(GROUPS, 5 * GROUPS):
                power(n)

            pool.wait_ge(s["slot_ready"], 1)
            for g in range(GROUPS):
                pool.wait_ge(s["xs_ready"], g + 1)
                if g >= 2:
                    pool.wait_ge(xs_sent[g % 2], 16 * (g // 2))
                pool.indirect_dma_start(sorted_x, bass.IndirectOffsetOnAxis(ap=slot_i[:, g:g + 1], axis=0), xs[:, g % 2, :], None)\
                    .then_inc(xs_sent[g % 2], 16)
            for i in range(2):
                pool.wait_ge(xs_sent[i], 16 * GROUPS // 2)
            nc.gpsimd.memset(slot_seen[:, :], 0.0).then_inc(s["scattered"], 16 * GROUPS)

            pool.wait_ge(s["table_ready"], 1)
            rounds = pool.value_load(table[0:1, 2 * MAX_BLOCKS:2 * MAX_BLOCKS + 1], min_val=1, max_val=MAX_BLOCKS // UNROLL)
            with pool.Fori(0, rounds) as r:
                for u in range(UNROLL):
                    at = pool.value_load(table[0:1, bass.ds(r * UNROLL + u + MAX_BLOCKS, 1)], min_val=0, max_val=TOKENS)
                    pool.wait_ge(s["yw_ready"], r * UNROLL + u + 3)
                    pool.wait_ge(s["written"], 16 * (r * UNROLL + u) + 16)
                    pool.dma_start(sorted_y[bass.ds(at, BLOCK), :], yw[:, u, :]).then_inc(s["written"], 16)
            pool.wait_ge(s["written"], 16 * UNROLL * rounds + 16)
            nc.gpsimd.tensor_tensor(slot_seen[:, :], slot_seen[:, :], slot_seen[:, :], ALU.add).then_inc(s["all_written"], 1)
            pool.wait_ge(s["all_written"], 1)
            pool.wait_ge(s["av_done"], GROUPS)
            for g in range(GROUPS):
                pool.indirect_dma_start(back[0:GT, g, :], None, sorted_y[0:TOKENS, :], bass.IndirectOffsetOnAxis(ap=slot_i[:, g:g + 1], axis=0))\
                    .then_inc(rows_back[g], 16)


_OUT = (GROUPS, GT, D)


def kernel(**inputs):
    import numpy as _np
    import concourse.bacc as _bacc
    from concourse import mybir as _mybir
    from concourse.bass_utils import run_bass_kernel_spmd as _run

    a = {k: _np.ascontiguousarray(v) for k, v in inputs.items()}

    def chunked(w):
        return w.reshape(-1, 128, w.shape[-1]).transpose(1, 0, 2)

    order = [16 * m + 2 * g + r for g in range(GROUPS) for m in range(2) for r in range(2)]
    x = a["x"][:, :, 0:80, 0:80].reshape(32, 3, 5, 16, 5, 16).transpose(0, 1, 3, 5, 2, 4)
    pt = x.reshape(32, 25, 768)[order]
    pt = _np.concatenate([_np.zeros((32, 1, 768), pt.dtype), pt], axis=1)
    pt = pt.reshape(GROUPS, GT, FC, 128).transpose(3, 0, 2, 1).reshape(128, GROUPS, FC * GT)

    cls = _np.zeros((GI, POSITIONS, D), _np.float32)
    cls[:, 0] = a["cls_tok"].reshape(1, D)
    cls = cls.reshape(GT, D)

    wo1 = _np.zeros((HEADS, HPAD, D), _np.float32)
    wo1[:, :HD] = a["L1_attn_Wo"].reshape(HEADS, HD, D)
    heads = [[8 * (b // 2) + 2 * r + b % 2 for r in range(4)] for b in range(4)]
    wo1 = _np.stack([wo1[hs].reshape(128, D) for hs in heads], axis=1)

    def col(v):
        return v.reshape(-1, 128).T

    parity = (_np.arange(128) // HD) % 2
    bcol = _np.concatenate([
        col(a["L0_attn_bq"]), col(a["L0_attn_bk"]), col(a["L0_ffn_ln_scale"]), col(a["L0_ffn_ln_bias"]),
        col(a["L0_ffn_attn_b"]), col(a["L1_attn_bq"]), col(a["L1_attn_bk"]), col(a["L0_ffn_b2"]), col(a["L0_ffn_b1"]),
        (parity == 0)[:, None], (parity == 1)[:, None]], axis=1).astype(_np.float32)
    brow = _np.stack([a["L0_attn_bv"], a["L0_attn_bo"], a["L0_ffn_next_b"], a["L1_attn_bv"], a["L1_attn_bo"]])
    p = _np.arange(128)
    masks = _np.zeros((128, 256 + 2 * GT), _np.float32)
    masks[:, 128 + 2 * GT:] = p[:, None] // HD == p[None] // HD
    masks[:, :128] = p[:, None] // IMAGES == p[None] // IMAGES
    t = _np.arange(GT)
    masks[:, 128 + GT:128 + 2 * GT] = t % POSITIONS != 0
    masks[:GT, 128:128 + GT] = (t[:, None] // POSITIONS == t[None] // POSITIONS) & (t[:, None] <= t[None])
    tri = _np.ones((GT, GT + 128), _np.float32)
    tri[:, :GT] = t[:, None] < t[None]
    route = _np.zeros((128, NROUTE), _np.float32)
    route[:, C_IOTA:C_IOTA + EXPERTS] = _np.arange(EXPERTS) - 64
    route[:, C_K:C_K + MAX_BLOCKS * EXPERTS] = _np.repeat(_np.arange(MAX_BLOCKS), EXPERTS)
    route[:, C_128:C_128 + 7 * EXPERTS] = _np.tile(BLOCK * _np.arange(7), EXPERTS)
    route[:, C_QUAD:C_QUAD + 10] = UNROLL * _np.arange(10)
    route[:, C_128K:] = BLOCK * _np.arange(MAX_BLOCKS)

    def experts(gw, uw, dw):
        n = gw.shape[0]
        parts = [w.reshape(n, -1, 128, w.shape[-1]).transpose(0, 2, 1, 3).reshape(n, 128, -1) for w in (gw, uw, dw) if w is not None]
        return _np.concatenate(parts, axis=2)

    feeds = {
        "patches": pt, "cls": cls, "tokw": chunked(a["L0_tok_W"]),
        "w0": _np.stack([chunked(a[f"L0_attn_W{n}"].T) for n in "qkvo"], axis=1),
        "wx": _np.stack([chunked(a["L0_ffn_attn_w"].T), chunked(a["L0_ffn_next_w"].T)], axis=1),
        "w1a": _np.stack([chunked(a[f"L1_attn_W{n}"]) for n in "qkv"], axis=1), "w1o": wo1,
        "gate": chunked(a["L1_ffn_gate_w"]),
        "shared": experts(a["L1_ffn_shared_gate_w"][None], a["L1_ffn_shared_up_w"][None], a["L1_ffn_shared_down_w"][None])[0],
        "experts0": experts(a["L0_ffn_w1"], None, a["L0_ffn_w2"]),
        "experts1": experts(a["L1_ffn_routed_gate_w"], a["L1_ffn_routed_up_w"], a["L1_ffn_routed_down_w"]),
        "bcol": bcol, "brow": brow, "ident_in": _np.eye(128, dtype=_np.float32), "masks_in": masks,
        "tri_in": tri.astype(_mybir.dt.np(BF16)), "route_in": route,
    }
    nc = _bacc.Bacc("TRN2", target_bir_lowering=False, num_devices=1)
    arrays, args = {}, []
    for name, v in feeds.items():
        v = _np.ascontiguousarray(v)
        arrays[f"{name}_dram"] = v
        args.append(nc.dram_tensor(f"{name}_dram", v.shape, _mybir.dt.from_np(v.dtype), kind="ExternalInput").ap())
    args.append(nc.dram_tensor("out_dram", _OUT, F32, kind="ExternalOutput").ap())
    tower(nc, *args)
    r = _run(nc, [arrays], core_ids=[0])
    got = _np.asarray(r.results[0]["out_dram"]).reshape(IMAGES, POSITIONS, D)
    inverse = _np.argsort(order)
    return got[inverse]
```

```python
from contextlib import ExitStack

import numpy as np
import concourse.bass as bass
from concourse import mybir

F32 = mybir.dt.float32
BF16 = mybir.dt.bfloat16
I32 = mybir.dt.int32
ALU = mybir.AluOpType
ACT = mybir.ActivationFunctionType
AX = mybir.AxisListType

IMAGES, POSITIONS, D = 32, 26, 256
TOKENS = IMAGES * POSITIONS
GROUPS = 8
GT = TOKENS // GROUPS
GI = IMAGES // GROUPS
DC = D // 128
FC = 6
HIDDEN = 1024
HC = HIDDEN // 128
INNER = 512
IC = INNER // 128
EXPERTS = 32
HEADS, HD = 16, 16
HPAD = 32
EPS = 1e-5
HALF = TOKENS // 2
PT = 4 * IMAGES
PTILES = 7
BLOCK = 128
UNROLL = 4
MAX_BLOCKS = 40
STEPS = -(-TOKENS // BLOCK)
SORTED = TOKENS + BLOCK
XROW = D + 2

BQ0, BK0, LNS, LNB, AB, BQ1, BK1, B2, B1 = 0, 2, 4, 6, 8, 10, 12, 14, 30
EVEN, ODD = B1 + GROUPS * HC, B1 + GROUPS * HC + 1
NBCOL = ODD + 1
BV0, BO0, NXB, BV1, BO1 = range(5)
NROUND = MAX_BLOCKS // UNROLL
C_IOTA = 0
C_K = C_IOTA + EXPERTS
C_STEP = C_K + 2
C_ROUND = C_STEP + EXPERTS * STEPS
C_ID = C_ROUND + NROUND
C_SPILL = C_ID + GROUPS
NROUTE = C_SPILL + 2


def tower(nc, patches, cls, tokw, w0, wx, w1a, w1o, gate, shared, experts0, experts1, bcol, brow,
          ident_in, masks_in, tri_in, route_in, out):
    sorted_x = nc.dram_tensor("sorted_x", (SORTED, XROW), F32, kind="Internal").ap()

    with ExitStack() as ctx:
        def sb(name, shape, dt=F32):
            return ctx.enter_context(nc.sbuf_tensor(name, shape, dt))

        def sem(name):
            return ctx.enter_context(nc.semaphore(name))

        ring = sb("ring", [128, 4, 4096])
        pat = sb("pat", [128, GROUPS, FC * GT])
        vpad = pat[:, :, 0:HEADS * HPAD].rearrange("p g (h m) -> p g h m", m=HPAD)
        kz = sb("kz", [128, DC, TOKENS])
        tokw_s = kz[:, :, :].rearrange("p c t -> p (c t)")[:, 0:FC * D].rearrange("p (c n) -> p c n", c=FC)
        w0_s = sb("w0_s", [128, 4, DC, D])
        wx_s = sb("wx_s", [128, 2, DC, D])
        wl1 = sb("wl1", [128, 3 * DC * D + 4 * D])
        w1_s = wl1[:, 0:3 * DC * D].rearrange("p (w c n) -> p w c n", w=3, c=DC)
        w1o_s = wl1[:, 3 * DC * D:3 * DC * D + 4 * D].rearrange("p (c n) -> p c n", c=4)
        steps = wl1[:, 0:EXPERTS * STEPS].rearrange("p (e m) -> p e m", m=STEPS)
        gate_s = sb("gate_s", [128, DC, EXPERTS])
        shared_s = sb("shared_s", [128, 2 * DC * INNER + IC * D])
        sgw = shared_s[:, 0:DC * INNER].rearrange("p (c n) -> p c n", c=DC)
        suw = shared_s[:, DC * INNER:2 * DC * INNER].rearrange("p (c n) -> p c n", c=DC)
        sdw = shared_s[:, 2 * DC * INNER:].rearrange("p (c n) -> p c n", c=IC)
        bcol_s = sb("bcol_s", [128, NBCOL])
        brow_s = sb("brow_s", [128, 5, D])
        ident = sb("ident", [128, 128])
        masks = sb("masks", [128, 256 + 2 * GT])
        tri = sb("tri", [GT, GT + 128], BF16)
        route = w0_s[:, :, :, :].rearrange("p w c n -> p (w c n)")[:, 0:NROUTE]
        h = sb("h", [GT, GROUPS, D])
        xA = sb("xA", [128, DC, TOKENS])
        qT = sb("qT", [128, DC, TOKENS])
        kT = sb("kT", [128, DC, TOKENS])
        q1, kE, kO = qT, kT, xA
        vrow = sb("vrow", [128, GROUPS, XROW])
        x3 = vrow[:, :, 0:D]
        oT = sb("oT", [128, DC, TOKENS])
        x3T = oT
        eA = kz[:, :, :].rearrange("p c t -> p (c t)")[:, 0:2 * HALF].rearrange("p (a n) -> p a n", a=2)
        fhT = sb("fhT", [128, HC, GT])
        zA = fhT[:, :, :].rearrange("p c t -> p (c t)").rearrange("p (a n) -> p a n", a=2)
        S = sb("S", [128, 2, HEADS * GT])
        hidT = S[:, :, :].rearrange("p a n -> p (a n)").rearrange("p (c n) -> p c n", c=IC)
        attA = S[:, 0, 0:2 * PT].rearrange("p (a n) -> p a n", a=2)
        clsbuf = S[0:GT, 1, 0:D]
        zrow = S[0:BLOCK, 1, D:D + XROW]
        xr = sb("xr", [GT, 2, D])
        xr2 = sb("xr2", [GT, 2, D])
        st = sb("st", [GT, 6])
        mv = sb("mv", [GT, 2])
        var = sb("var", [GT, 1])
        rstd = sb("rstd", [GT, 1])
        slot_seen = sb("slot_seen", [1, 1])
        mhalf = sb("mhalf", [GT, 1])
        cols5 = sb("cols5", [128, 5, DC, GT])
        nT, n2T, xaT, eoT, x2T = (cols5[:, i, :, :] for i in range(5))
        flat5 = cols5[:, :, :, :].rearrange("p a c t -> p (a c t)")
        qz = flat5[:, 0:DC * GT].rearrange("p (c t) -> p c t", c=DC)
        rden = flat5[:, DC * GT:2 * DC * GT].rearrange("p (c t) -> p c t", c=DC)
        valT = flat5[:, HALF:2 * HALF].rearrange("p (a t) -> p a t", a=4)
        nxr = sb("nxr", [GT, D])
        flate = eA[:, :, :].rearrange("p a n -> p (a n)")
        big = flate[0:GT, 0:256].rearrange("p (g e) -> p g e", e=EXPERTS)
        onehot = flate[0:GT, 256:512].rearrange("p (g e) -> p g e", e=EXPERTS)
        onehot_b = sb("onehot_b", [GT, GROUPS, EXPERTS], BF16)
        lgm = sb("lgm", [GT, 6 * GROUPS])
        slot_i = sb("slot_i", [GT, GROUPS], I32)
        rt = sb("rt", [128, 8, EXPERTS])
        table = sb("table", [1, 2 * MAX_BLOCKS + 2], I32)
        tcol = sb("tcol", [128, 2])
        tfl = sb("tfl", [1, NROUND + 1])
        x2 = sb("x2", [GT, 2, D])
        xw = xA[:, :, :].rearrange("p c t -> p (c t)")[:, 0:UNROLL * XROW].rearrange("p (u d) -> p u d", u=UNROLL)
        xwT = kT[:, :, :].rearrange("p c t -> p (c t)")[:, 0:UNROLL * DC * BLOCK].rearrange("p (u c t) -> p u c t", u=UNROLL, c=DC)
        blk = S[:, :, :].rearrange("p a n -> p (a n)")
        sg, hw = (blk[:, i * INNER:(i + 2) * INNER].rearrange("p (u n) -> p u n", u=2) for i in (0, 2))
        yw = qT[:, :, :].rearrange("p c t -> p (c t)")[:, 0:UNROLL * D].rearrange("p (u d) -> p u d", u=UNROLL)
        own = sb("own", [128, 3])
        mine, where, kcol = own[:, 0:1], own[:, 1:2], own[:, 2:3]
        target = sb("target", [128, UNROLL], I32)
        spill = sb("spill", [128, 2])
        idb = vrow[0:GT, :, D:XROW]

        P = [ctx.enter_context(nc.psum_tensor(f"P{i}", [128, 512], F32)) for i in range(8)]

        names = ("consts ident_in cls_in pat_in tokw_in w0_in wx_in w1_in gate_in shared_in bias_in brow_in route_in "
                 "zeroed tail_zero vpad_zero vec var_ready rstd_ready "
                 "tok_done h0_ready trA_done xA_ready "
                 "qk0_done z0_sum z0_ready exp0_done qk0_ready v0_done v0_ready att_done att_ready oT_done oT_ready "
                 "wo_done n_ready wo_read tr1_done nT_ready n2T_ready xa_done xaT_ready up_done gelu_done down_done eoT_ready "
                 "nx_done nx_sum nx_gelu x2_ready tr2_done x2T_ready qk1_done z1_ready v1_done v1_ready "
                 "m1_ready exp1_done q1_ready z_scan qz_ready den_done den_read qn_ready k1_ready sc_done sc_ready av_done val_ready wo1_done x3_ready tr3_done x3T_ready lg_done "
                 "onehot_ready prefix_done score_ready topv_ready slot_ready blocks_ready table_done table_ready xs_scaled xs_ready scattered "
                 "sg_done silu0_done hid_ready sd_done ids_done h_final "
                 "xwt_done xwT_ready gu_done silu_done hw_ready dn_done turn yw_ready written stored").split()
        s = {n: sem(n) for n in names}
        ring_in = [sem(f"ring_in{i}") for i in range(4)]
        block_in = [sem(f"block_in{i}") for i in range(4)]
        window_in = [sem(f"window_in{i}") for i in range(4)]
        pat_in = [sem(f"pat_in{i}") for i in range(4)]
        xs_sent = [sem(f"xs_sent{i}") for i in range(GROUPS)]

        def gcol(g):
            return slice(g * GT, (g + 1) * GT)

        def bank(b, *shape):
            n = int(np.prod(shape))
            if len(shape) == 1:
                return P[b][:, 0:n]
            return P[b][:, 0:n].rearrange("p (a n) -> p a n", a=shape[0])

        def ptile(i):
            n = min(PT, TOKENS - i * PT)
            return slice(i * PT, i * PT + n), n

        def lagged(steps, stages):
            for t in range(steps):
                for stage, lag in stages:
                    if 0 <= t - lag < GROUPS:
                        stage(t - lag)

        def all_rounds(engine):
            return engine.value_load(table[0:1, 2 * MAX_BLOCKS:2 * MAX_BLOCKS + 1], min_val=2, max_val=MAX_BLOCKS // UNROLL)

        def more_rounds(engine):
            return engine.value_load(table[0:1, 2 * MAX_BLOCKS + 1:2 * MAX_BLOCKS + 2], min_val=1, max_val=MAX_BLOCKS // UNROLL - 1)

        block = ctx.enter_context(nc.Block())

        @block.sync
        def _(sp):
            sp.dma_start(tokw_s[:, :, :], tokw).then_inc(s["tokw_in"], 16)
            for i in range(4):
                sp.dma_start(pat[:, 2 * i:2 * i + 2, :], patches[:, 2 * i:2 * i + 2, :]).then_inc(pat_in[i], 16)
                if i == 0:
                    sp.dma_start(clsbuf, cls).then_inc(s["cls_in"], 16)
                    sp.dma_start(ident[:, :], ident_in).then_inc(s["ident_in"], 16)
            sp.dma_start(w0_s[:, :, :, :], w0).then_inc(s["w0_in"], 16)
            sp.dma_start(bcol_s[:, :], bcol).then_inc(s["bias_in"], 16)
            sp.dma_start(brow_s[:, :, :], brow.partition_broadcast(128)).then_inc(s["brow_in"], 16)
            sp.dma_start(masks[:, :], masks_in).then_inc(s["consts"], 16)
            sp.dma_start(wx_s[:, :, :, :], wx).then_inc(s["wx_in"], 16)
            for e in range(2):
                sp.dma_start(ring[:, e, :], experts0[e]).then_inc(ring_in[e], 16)
            sp.dma_start(w1_s[:, :, :, :], w1a).then_inc(s["w1_in"], 16)
            sp.dma_start(w1o_s[:, :, :], w1o).then_inc(s["w1_in"], 16)
            for e in range(2, 4):
                sp.dma_start(ring[:, e, :], experts0[e]).then_inc(ring_in[e], 16)
            sp.dma_start(gate_s[:, :, :], gate).then_inc(s["gate_in"], 16)
            sp.dma_start(shared_s[:, :], shared).then_inc(s["shared_in"], 16)
            sp.dma_start(tri[:, :], tri_in).then_inc(s["route_in"], 16)
            for e in range(4, GROUPS):
                sp.wait_ge(s["down_done"], e - 3)
                sp.dma_start(ring[:, e - 4, :], experts0[e]).then_inc(ring_in[e - 4], 16)
            sp.wait_ge(s["wo_done"], GROUPS)
            sp.dma_start(route[:, :], route_in).then_inc(s["route_in"], 16)
            sp.wait_ge(s["table_ready"], 1)
            sp.wait_ge(s["down_done"], GROUPS)

            def weights(k, slot):
                e = sp.value_load(table[0:1, bass.ds(k, 1)], min_val=0, max_val=EXPERTS - 1)
                sp.dma_start(ring[:, slot, 0:3072], experts1[bass.ds(e, 1)].rearrange("e p n -> (e p) n")).then_inc(block_in[slot], 16)

            def window(k, slot):
                at = sp.value_load(table[0:1, bass.ds(k + MAX_BLOCKS, 1)], min_val=0, max_val=TOKENS)
                sp.dma_start(xw[:, slot, :], sorted_x[bass.ds(at, BLOCK), :]).then_inc(window_in[slot], 16)

            weights(0, 0)
            weights(1, 1)
            sp.wait_ge(s["scattered"], 16 * GROUPS)
            sp.wait_ge(s["written"], 16 * UNROLL)
            sp.wait_ge(s["sc_done"], GROUPS)
            for u in range(UNROLL):
                window(u, u)
            weights(2, 2)
            weights(3, 3)
            more = more_rounds(sp)
            with sp.Fori(0, more) as r:
                for u in range(UNROLL):
                    sp.wait_ge(s["ids_done"], 3 * (r * UNROLL + u + 1 + UNROLL))
                    sp.wait_ge(s["dn_done"], r * UNROLL + u + 1 + UNROLL)
                    window(r * UNROLL + u + UNROLL, u)
                    weights(r * UNROLL + u + UNROLL, u)

        @block.tensor
        def _(pe):
            mm = nc.tensor.matmul

            def rows(b, lhs, rhs, chunks, col=0):
                for c in range(chunks):
                    a = lhs(c)
                    last = mm(P[b][0:a.shape[1], col:col + D], a, rhs(c), start=(c == 0), stop=(c == chunks - 1))
                return last

            def tok(g):
                if g % 2 == 0:
                    pe.wait_ge(pat_in[g // 2], 16)
                if g >= 2:
                    pe.wait_ge(s["h0_ready"], g - 1)
                rows(g % 2, lambda c: pat[:, g, c * GT:(c + 1) * GT], lambda c: tokw_s[:, c, :], FC).then_inc(s["tok_done"], 1)

            def trA(g):
                if g == 0:
                    pe.wait_ge(s["ident_in"], 16)
                pe.wait_ge(s["n_ready"], g + 1)
                if g >= 2:
                    pe.wait_ge(s["xA_ready"], g - 1)
                for c in range(DC):
                    last = nc.tensor.transpose(bank(2 + g % 2, DC, GT)[:, c, :], xr[:, g % 2, c * 128:(c + 1) * 128], ident[0:GT, 0:GT])
                last.then_inc(s["trA_done"], 1)

            nc.tensor.nop().then_inc(s["dn_done"], UNROLL)
            nc.tensor.nop().then_inc(s["gu_done"], 1)
            pe.wait_ge(s["tokw_in"], 16)
            lagged(GROUPS + 2, [(trA, 2), (tok, 0)])

            pe.wait_ge(s["w0_in"], 16)
            pe.wait_ge(s["xA_ready"], GROUPS)
            pe.wait_ge(s["h0_ready"], GROUPS)
            for n in range(8):
                w, m, half = n // 4, (n // 2) % 2, n % 2
                if n >= 4:
                    pe.wait_ge(s["z0_ready"], n - 3)
                for c in range(DC):
                    last = mm(bank(n % 4, HALF), w0_s[:, w, c, m * 128:(m + 1) * 128],
                              xA[:, c, half * HALF:(half + 1) * HALF], start=(c == 0), stop=(c == DC - 1))
                last.then_inc(s["qk0_done"], 1)
            for i in range(PTILES):
                cols, n = ptile(i)
                if i >= 2:
                    pe.wait_ge(s["v0_ready"], i - 1)
                rows(4 + i % 2, lambda c: xA[:, c, cols], lambda c: w0_s[:, 2, c, :], DC).then_inc(s["v0_done"], 1)
            pe.wait_ge(s["qk0_ready"], 8)

            def att(i):
                if i >= PTILES:
                    return
                cols, n = ptile(i)
                if i >= 2:
                    pe.wait_ge(s["att_ready"], i - 1)
                for c in range(DC):
                    last = mm(P[6 + i % 2][0:n, 0:n], kT[:, c, cols], qT[:, c, cols], start=(c == 0), stop=(c == DC - 1))
                last.then_inc(s["att_done"], 1)

            def att_v(i):
                if i >= PTILES:
                    return
                cols, n = ptile(i)
                pe.wait_ge(s["att_ready"], i + 1)
                pe.wait_ge(s["v0_ready"], i + 1)
                if i >= 2:
                    pe.wait_ge(s["oT_ready"], i - 1)
                for c in range(DC):
                    last = mm(bank(i % 2, DC, PT)[:, c, 0:n], vrow[0:n, i, c * 128:(c + 1) * 128], attA[0:n, i % 2, 0:n],
                              start=True, stop=True)
                last.then_inc(s["oT_done"], 1)

            lagged(GROUPS + 1, [(att, 0), (att_v, 1)])

            def wo(g):
                if g == 0:
                    pe.wait_ge(s["oT_ready"], PTILES)
                if g >= 3:
                    pe.wait_ge(s["x2T_ready"], g - 2)
                elif g >= 1:
                    pe.wait_ge(s["wo_read"], g)
                rows(0, lambda c: oT[:, c, gcol(g)], lambda c: w0_s[:, 3, c, :], DC).then_inc(s["wo_done"], 1)

            def tr1(g):
                pe.wait_ge(s["n_ready"], GROUPS + 2 * g + 2)
                if g >= 1:
                    pe.wait_ge(s["n2T_ready"], g)
                    pe.wait_ge(s["nT_ready"], g)
                for a, src in ((0, xr), (2, xr2)):
                    for c in range(DC):
                        last = nc.tensor.transpose(bank(1, 4, GT)[:, a + c, :], src[:, g % 2, c * 128:(c + 1) * 128], ident[0:GT, 0:GT])
                last.then_inc(s["tr1_done"], 1)

            def xa(g):
                pe.wait_ge(s["n2T_ready"], g + 1)
                if g >= 1:
                    pe.wait_ge(s["xaT_ready"], g)
                for m in range(DC):
                    for c in range(DC):
                        last = mm(bank(2, DC, GT)[:, m, :], wx_s[:, 0, c, m * 128:(m + 1) * 128], n2T[:, c, :],
                                  start=(c == 0), stop=(c == DC - 1))
                last.then_inc(s["xa_done"], 1)

            def up(g):
                pe.wait_ge(ring_in[g % 4], 16 * (g // 4 + 1))
                pe.wait_ge(s["xaT_ready"], g + 1)
                w = ring[:, g % 4, 0:DC * HIDDEN].rearrange("p (c n) -> p c n", c=DC)
                for m in range(HC):
                    if g >= 1 and m % 4 == 0:
                        pe.wait_ge(s["gelu_done"], HC * (g - 1) + m + 4)
                    for c in range(DC):
                        last = mm(bank(3 + m // 4, 4, GT)[:, m % 4, :], w[:, c, m * 128:(m + 1) * 128], xaT[:, c, :],
                                  start=(c == 0), stop=(c == DC - 1))
                    if m % 4 == 3:
                        last.then_inc(s["up_done"], 1)

            def down(g):
                if g >= 1:
                    pe.wait_ge(s["nx_sum"], g)
                w = ring[:, g % 4, DC * HIDDEN:].rearrange("p (c n) -> p c n", c=HC)
                pe.wait_ge(s["gelu_done"], HC * (g + 1))
                for m in range(DC):
                    for c in range(HC):
                        last = mm(P[5][:, m * GT:(m + 1) * GT], w[:, c, m * 128:(m + 1) * 128], fhT[:, c, :],
                                  start=(c == 0), stop=(c == HC - 1))
                last.then_inc(s["down_done"], 1)

            def nx(g):
                pe.wait_ge(s["eoT_ready"], g + 1)
                rows(5, lambda c: eoT[:, c, :], lambda c: wx_s[:, 1, c, :], DC, col=256).then_inc(s["nx_done"], 1)

            def tr2(g):
                pe.wait_ge(s["x2_ready"], g + 1)
                pe.wait_ge(s["wo_read"], min(g + 3, GROUPS))
                for c in range(DC):
                    last = nc.tensor.transpose(P[0][:, 256 + c * GT:256 + (c + 1) * GT], x2[:, g % 2, c * 128:(c + 1) * 128], ident[0:GT, 0:GT])
                last.then_inc(s["tr2_done"], 1)

            def qk1(g):
                pe.wait_ge(s["x2T_ready"], g + 1)
                if g == 0:
                    pe.wait_ge(s["w1_in"], 32)
                else:
                    pe.wait_ge(s["z1_ready"], g)
                for w in range(2):
                    for m in range(DC):
                        for c in range(DC):
                            last = mm(bank(6, 4, GT)[:, 2 * w + m, :], w1_s[:, w, c, m * 128:(m + 1) * 128], x2T[:, c, :],
                                      start=(c == 0), stop=(c == DC - 1))
                last.then_inc(s["qk1_done"], 1)

            def v1(g):
                if g >= 1:
                    pe.wait_ge(s["v1_ready"], g)
                rows(7, lambda c: x2T[:, c, :], lambda c: w1_s[:, 2, c, :], DC).then_inc(s["v1_done"], 1)

            pe.wait_ge(s["wx_in"], 16)
            lagged(GROUPS + 3, [(tr1, 1), (tr2, 3), (nx, 2), (xa, 1), (wo, 0), (up, 1), (qk1, 3), (v1, 3), (down, 1)])

            def scores(g):
                pe.wait_ge(s["k1_ready"], 2 * (g + 1))
                pe.wait_ge(s["qn_ready"], g + 1)
                if g >= 1:
                    pe.wait_ge(s["sc_ready"], 4 * g)
                for c in range(DC):
                    for odd, k in ((0, kE), (1, kO)):
                        for r in range(4):
                            last = mm(bank(r, 4, GT)[0:GT, 2 * c + odd, :], k[32 * r:32 * r + 32, c, gcol(g)],
                                      q1[32 * r:32 * r + 32, c, gcol(g)], start=True, stop=True, tile_position=(32 * r, 0))
                last.then_inc(s["sc_done"], 1)

            def av(g):
                pe.wait_ge(s["sc_ready"], 4 * (g + 1))
                if g == 0:
                    pe.wait_ge(s["v1_ready"], GROUPS)
                else:
                    pe.wait_ge(s["val_ready"], g)
                for b in range(4):
                    for r in range(4):
                        head = 8 * (b // 2) + 2 * r + b % 2
                        sc = S[0:GT, g % 2, (r * 4 + b) * GT:(r * 4 + b + 1) * GT]
                        last = mm(bank(4, 4, GT)[32 * r:32 * r + 32, b, :], vpad[0:GT, g, head, :], sc, start=True, stop=True,
                                  tile_position=(0, 32 * r))
                last.then_inc(s["av_done"], 1)

            def den(g):
                pe.wait_ge(s["qz_ready"], g + 1)
                if g >= 1:
                    pe.wait_ge(s["den_read"], g)
                for c in range(DC):
                    last = mm(bank(5, DC, GT)[:, c, :], masks[:, 128 + 2 * GT:], qz[:, c, :], start=True, stop=True)
                last.then_inc(s["den_done"], 1)

            def wo1(g):
                pe.wait_ge(s["val_ready"], g + 1)
                if g >= 1:
                    pe.wait_ge(s["h0_ready"], 2 * GROUPS + g)
                rows(6, lambda c: valT[:, c, :], lambda c: w1o_s[:, c, :], 4).then_inc(s["wo1_done"], 1)

            def tr3(g):
                pe.wait_ge(s["x3_ready"], g + 1)
                if g >= 1:
                    pe.wait_ge(s["x3T_ready"], g)
                for c in range(DC):
                    last = nc.tensor.transpose(bank(7, DC, GT)[:, c, :], vrow[0:GT, g, c * 128:(c + 1) * 128], ident[0:GT, 0:GT])
                last.then_inc(s["tr3_done"], 1)

            def logits(g):
                if g == 0:
                    pe.wait_ge(s["gate_in"], 16)
                    pe.wait_ge(s["den_read"], GROUPS)
                pe.wait_ge(s["x3T_ready"], g + 1)
                for c in range(DC):
                    last = mm(P[5][0:GT, g * EXPERTS:(g + 1) * EXPERTS], x3T[:, c, gcol(g)], gate_s[:, c, :],
                              start=(c == 0), stop=(c == DC - 1))
                last.then_inc(s["lg_done"], 1)

            def logits_so_far(g):
                for j in range(GROUPS):
                    if j == g >= 5 or j <= g == 4:
                        logits(j)

            def shared_up(n):
                m, half = n // 2, n % 2
                if n == 0:
                    pe.wait_ge(s["shared_in"], 16)
                if n >= 2:
                    pe.wait_ge(s["hid_ready"], n - 1)
                for b, w in ((n % 2, sgw), (2 + n % 2, suw)):
                    for c in range(DC):
                        last = mm(bank(b, HALF), w[:, c, m * 128:(m + 1) * 128], x3T[:, c, half * HALF:(half + 1) * HALF],
                                  start=(c == 0), stop=(c == DC - 1))
                last.then_inc(s["sg_done"], 1)

            def shared_first(g):
                if g == GROUPS - 1:
                    shared_up(0)

            pe.wait_ge(s["zeroed"], 1)
            lagged(GROUPS + 6, [(wo1, 4), (den, 1), (av, 3), (shared_first, 5), (tr3, 5), (logits_so_far, 6), (scores, 2)])

            shared_up(1)
            pe.wait_ge(s["onehot_ready"], 1)
            pe.wait_ge(s["route_in"], 32)
            flat_hot = onehot_b[:, :, :].rearrange("p g e -> p (g e)")
            mm(P[4][0:GT, 0:256], tri[:, 0:GT], flat_hot, start=True, stop=False)
            for g in range(GROUPS - 1):
                rest = GROUPS - 1 - g
                mm(P[4][0:GT, (g + 1) * EXPERTS:256].rearrange("p (g e) -> p g e", e=EXPERTS), tri[:, GT:2 * GT],
                   onehot_b[:, g, :].unsqueeze(1).to_broadcast([GT, rest, EXPERTS]), start=False, stop=(rest == 1))
            for g in range(GROUPS):
                last = mm(P[5][:, 256:256 + EXPERTS], tri[:, GT:GT + 128], onehot_b[:, g, :], start=(g == 0), stop=(g == GROUPS - 1))
            last.then_inc(s["prefix_done"], 1)
            for n in range(2, 6):
                shared_up(n)
            pe.wait_ge(s["blocks_ready"], 1)
            for i in range(2):
                last = mm(P[5][0:1, 288 + i * MAX_BLOCKS:288 + (i + 1) * MAX_BLOCKS], tcol[0:MAX_BLOCKS, i:i + 1],
                          ident[0:MAX_BLOCKS, 0:MAX_BLOCKS], start=True, stop=True)
            last.then_inc(s["table_done"], 1)
            for n in range(6, 2 * IC):
                shared_up(n)

            def window_t(r, v):
                k, u, visit = r * UNROLL + v, v % UNROLL, r + v // UNROLL
                pe.wait_ge(window_in[u], 16 * (visit + 1))
                pe.wait_ge(s["xwT_ready"], k + 1)
                for c in range(DC):
                    last = nc.tensor.transpose(bank((4, 7)[u % 2], DC, BLOCK)[:, c, :], xw[:, u, c * 128:(c + 1) * 128], ident[:, :])
                last.then_inc(s["xwt_done"], 1)

            def gate_up(r, v):
                k, u, visit = r * UNROLL + v, v % UNROLL, r + v // UNROLL
                gw = ring[:, u, 0:1024].rearrange("p (c n) -> p c n", c=DC)
                uw = ring[:, u, 1024:2048].rearrange("p (c n) -> p c n", c=DC)
                pe.wait_ge(block_in[u], 16 * (visit + 1))
                pe.wait_ge(s["xwT_ready"], k + 3)
                pe.wait_ge(s["hw_ready"], k + 1)
                for b, w in ((u % 2, gw), (2 + u % 2, uw)):
                    for m in range(IC):
                        for c in range(DC):
                            last = mm(bank(b, IC, BLOCK)[:, m, :], w[:, c, m * 128:(m + 1) * 128], xwT[:, u, c, :],
                                      start=(c == 0), stop=(c == DC - 1))
                    last.then_inc(s["gu_done"], 1)

            def down_rows(r, v):
                k, u = r * UNROLL + v, v
                dw = ring[:, u, 2048:3072].rearrange("p (c n) -> p c n", c=IC)
                pe.wait_ge(s["hw_ready"], k + 3)
                pe.wait_ge(s["yw_ready"], k + 1)
                rows(5 + u % 2, lambda c: hw[:, u % 2, c * BLOCK:(c + 1) * BLOCK], lambda c: dw[:, c, :], IC)\
                    .then_inc(s["dn_done"], 1)

            pe.wait_ge(s["table_ready"], 1)
            more = more_rounds(pe)
            pe.wait_ge(s["hid_ready"], 2 * IC)
            for g in range(GROUPS):
                if g >= 2:
                    pe.wait_ge(s["h_final"], g - 1)
                rows(6 + g % 2, lambda c: hidT[:, c, gcol(g)], lambda c: sdw[:, c, :], IC).then_inc(s["sd_done"], 1)
                if g == GROUPS - 2:
                    window_t(0, 0)
            gate_up(0, 0)
            pe.wait_ge(s["h_final"], GROUPS)
            window_t(0, 1)
            with pe.Fori(0, more) as r:
                for u in range(UNROLL):
                    window_t(r, u + 2)
                    gate_up(r, u + 1)
                    down_rows(r, u)
            for u in range(UNROLL):
                if u + 2 < UNROLL:
                    window_t(more, u + 2)
                if u + 1 < UNROLL:
                    gate_up(more, u + 1)
                down_rows(more, u)

        @block.scalar
        def _(act):
            A = nc.scalar.activation

            for g in range(GROUPS):
                act.wait_ge(s["trA_done"], g + 1)
                for c in range(DC):
                    dst = xA[:, c, :].rearrange("p (b i) -> p i b", i=IMAGES)[:, GI * g:GI * (g + 1), :]
                    src = bank(2 + g % 2, DC, GT)[:, c, :].rearrange("p (i b) -> p i b", b=POSITIONS)
                    last = A(dst, src, ACT.Copy)
                last.then_inc(s["xA_ready"], 1)
            act.wait_ge(s["bias_in"], 16)
            for n in range(8):
                act.wait_ge(s["z0_ready"], n + 1)
                A(eA[:, n % 2, :], eA[:, n % 2, :], ACT.Exp).then_inc(s["exp0_done"], 1)
            for i in range(PTILES):
                cols, n = ptile(i)
                act.wait_ge(s["oT_done"], i + 1)
                for c in range(DC):
                    dst = oT[:, c, :].rearrange("p (i b) -> p b i", b=POSITIONS)[:, 4 * i:4 * i + n // IMAGES, :]
                    src = bank(i % 2, DC, PT)[:, c, 0:n].rearrange("p (b i) -> p b i", i=IMAGES)
                    last = A(dst, src, ACT.Copy)
                last.then_inc(s["oT_ready"], 1)

            def nT_evac(g):
                act.wait_ge(s["tr1_done"], g + 1)
                if g >= 1:
                    act.wait_ge(s["xa_done"], g)
                for c in range(DC):
                    last = A(n2T[:, c, :], bank(1, 4, GT)[:, 2 + c, :], ACT.Identity, bias=bcol_s[:, LNB + c:LNB + c + 1],
                             scale=bcol_s[:, LNS + c:LNS + c + 1])
                last.then_inc(s["n2T_ready"], 1)
                if g >= 1:
                    act.wait_ge(s["xaT_ready"], g)
                for c in range(DC):
                    last = A(nT[:, c, :], bank(1, 4, GT)[:, c, :], ACT.Identity, bias=bcol_s[:, AB + c:AB + c + 1])
                last.then_inc(s["nT_ready"], 1)

            def gelu_up(g):
                if g >= 1:
                    act.wait_ge(s["down_done"], g)
                for m in range(HC):
                    if m % 4 == 0:
                        act.wait_ge(s["up_done"], 2 * g + m // 4 + 1)
                    A(fhT[:, m, :], bank(3 + m // 4, 4, GT)[:, m % 4, :], ACT.Gelu, bias=bcol_s[:, B1 + HC * g + m:B1 + HC * g + m + 1])\
                        .then_inc(s["gelu_done"], 1)

            def gelu_nx(g):
                act.wait_ge(s["nx_sum"], g + 1)
                A(nxr[:, :], nxr[:, :], ACT.Gelu).then_inc(s["nx_gelu"], 1)

            def x2_evac(g):
                act.wait_ge(s["tr2_done"], g + 1)
                if g >= 1:
                    act.wait_ge(s["v1_done"], g)
                A(x2T[:, :, :].rearrange("p c t -> p (c t)"), P[0][:, 256:256 + DC * GT], ACT.Copy).then_inc(s["x2T_ready"], 1)

            lagged(GROUPS + 3, [(nT_evac, 1), (x2_evac, 3), (gelu_nx, 2), (gelu_up, 1)])

            def exp1(g):
                act.wait_ge(s["m1_ready"], g + 1)
                A(kE[:, :, gcol(g)], kE[:, :, gcol(g)], ACT.Exp)
                A(kO[:, :, gcol(g)], kO[:, :, gcol(g)], ACT.Exp).then_inc(s["exp1_done"], 1)

            def k_evac(g):
                act.wait_ge(s["q1_ready"], g + 1)
                for dst, m in ((kE, EVEN), (kO, ODD)):
                    A(dst[:, :, gcol(g)], kz[:, :, gcol(g)], ACT.Copy, scale=bcol_s[:, m:m + 1]).then_inc(s["k1_ready"], 1)

            def val_evac(g):
                act.wait_ge(s["av_done"], g + 1)
                if g >= 1:
                    act.wait_ge(s["wo1_done"], g)
                A(valT[:, :, :].rearrange("p a t -> p (a t)"), bank(4, HALF), ACT.Copy).then_inc(s["val_ready"], 1)

            def x3_evac(g):
                act.wait_ge(s["tr3_done"], g + 1)
                A(x3T[:, :, gcol(g)], bank(7, DC, GT), ACT.Copy).then_inc(s["x3T_ready"], 1)

            exp1(0)
            lagged(GROUPS + 5, [(lambda g: g + 1 < GROUPS and exp1(g + 1), 0), (k_evac, 1), (val_evac, 3), (x3_evac, 5)])

            for n in range(2 * IC):
                if n == 1:
                    act.wait_ge(s["topv_ready"], 1)
                    A(lgm[:, GROUPS:2 * GROUPS], lgm[:, 0:GROUPS], ACT.Sigmoid).then_inc(s["score_ready"], 1)
                act.wait_ge(s["sg_done"], n + 1)
                if n >= 2:
                    act.wait_ge(s["hid_ready"], n - 1)
                A(zA[:, n % 2, :], bank(n % 2, HALF), ACT.Silu).then_inc(s["silu0_done"], 1)

            act.wait_ge(s["table_ready"], 1)
            act.wait_ge(s["sd_done"], GROUPS)
            rounds = all_rounds(act)
            for g in range(GROUPS):
                act.wait_ge(s["h_final"], g + 1)
                act.dma_start(out[gcol(g), :], h[:, g, :]).then_inc(s["stored"], 16)
            with act.Fori(0, rounds) as r:
                for u in range(UNROLL):
                    act.wait_ge(s["gu_done"], 2 * (r * UNROLL + u) + 2)
                    act.wait_ge(s["hw_ready"], r * UNROLL + u + 1)
                    A(sg[:, u % 2, :], P[u % 2][:, :], ACT.Silu).then_inc(s["silu_done"], 1)

        @block.vector
        def _(dve):
            V = nc.vector
            chain = [0]

            def link(ins):
                chain[0] += 1
                ins.then_inc(s["vec"], 1)
                dve.wait_ge(s["vec"], chain[0])

            norms = [0]

            def norm(src, dst, done):
                link(V.bn_stats(st[:, :], src))
                link(V.bn_aggr(mv[:, :], st[:, :]))
                V.tensor_scalar_add(var[:, :], mv[:, 1:2], EPS).then_inc(s["var_ready"], 1)
                norms[0] += 1
                dve.wait_ge(s["rstd_ready"], norms[0])
                V.tensor_scalar(dst, src, mv[:, 0:1], rstd[:, :], ALU.subtract, ALU.mult).then_inc(s[done], 1)

            V.memset(mhalf[:, :], -0.5).then_inc(s["zeroed"], 1)

            dve.wait_ge(s["cls_in"], 16)
            for g in range(GROUPS):
                dve.wait_ge(s["tok_done"], g + 1)
                V.tensor_tensor(h[:, g, :], P[g % 2][0:GT, 0:D], clsbuf, ALU.add).then_inc(s["h0_ready"], 1)
                dve.wait_ge(s["h0_ready"], g + 1)
                if g >= 2:
                    dve.wait_ge(s["trA_done"], g - 1)
                norm(h[:, g, :], xr[:, g % 2, :], "n_ready")

            dve.wait_ge(s["bias_in"], 16)
            for n in range(9):
                if n < 8:
                    b = (BQ0, BK0)[n // 4] + (n // 2) % 2
                    dve.wait_ge(s["qk0_done"], n + 1)
                    if n >= 2:
                        dve.wait_ge(s["qk0_ready"], n - 1)
                    V.tensor_scalar(zA[:, n % 2, :], bank(n % 4, HALF), bcol_s[:, b:b + 1], None, ALU.add).then_inc(s["z0_sum"], 1)
                    dve.wait_ge(s["z0_sum"], n + 1)
                    V.tensor_scalar_min(eA[:, n % 2, :], zA[:, n % 2, :], 0.0).then_inc(s["z0_ready"], 1)
                if n == 0:
                    continue
                n -= 1
                w, m, half = n // 4, (n // 2) % 2, n % 2
                dve.wait_ge(s["exp0_done"], n + 1)
                V.scalar_tensor_tensor((qT, kT)[w][:, m, half * HALF:(half + 1) * HALF], zA[:, n % 2, :], 0.0, eA[:, n % 2, :],
                                       ALU.max, ALU.add).then_inc(s["qk0_ready"], 1)
            dve.wait_ge(s["brow_in"], 16)
            for i in range(PTILES):
                cols, n = ptile(i)
                dve.wait_ge(s["v0_done"], i + 1)
                V.tensor_tensor(vrow[0:n, i, 0:D], P[4 + i % 2][0:n, 0:D], brow_s[0:n, BV0, :], ALU.add).then_inc(s["v0_ready"], 1)
            dve.wait_ge(s["consts"], 16)
            for i in range(PTILES):
                cols, n = ptile(i)
                dve.wait_ge(s["att_done"], i + 1)
                if i >= 2:
                    dve.wait_ge(s["oT_done"], i - 1)
                V.tensor_tensor(attA[0:n, i % 2, 0:n], P[6 + i % 2][0:n, 0:n], masks[0:n, 0:n], ALU.mult).then_inc(s["att_ready"], 1)

            def h1_norms(g):
                dve.wait_ge(s["wo_done"], g + 1)
                V.tensor_tensor(xr2[:, g % 2, :], P[0][0:GT, 0:D], brow_s[0:GT, BO0, :], ALU.add).then_inc(s["wo_read"], 1)
                dve.wait_ge(s["wo_read"], g + 1)
                V.tensor_tensor(h[:, g, :], h[:, g, :], xr2[:, g % 2, :], ALU.add).then_inc(s["h0_ready"], 1)
                dve.wait_ge(s["h0_ready"], GROUPS + g + 1)
                norm(h[:, g, :], xr[:, g % 2, :], "n_ready")
                dve.wait_ge(s["n_ready"], GROUPS + 2 * g + 1)
                norm(xr[:, g % 2, :], xr2[:, g % 2, :], "n_ready")

            def xa_evac(g):
                dve.wait_ge(s["xa_done"], g + 1)
                dve.wait_ge(s["nT_ready"], g + 1)
                if g >= 1:
                    dve.wait_ge(s["up_done"], 2 * g)
                V.tensor_tensor(xaT[:, :, :], bank(2, DC, GT), nT[:, :, :], ALU.add).then_inc(s["xaT_ready"], 1)

            def eo_evac(g):
                dve.wait_ge(s["down_done"], g + 1)
                if g >= 1:
                    dve.wait_ge(s["nx_done"], g)
                for c in range(DC):
                    last = V.tensor_scalar(eoT[:, c, :], P[5][:, c * GT:(c + 1) * GT], bcol_s[:, B2 + DC * g + c:B2 + DC * g + c + 1], None, ALU.add)
                last.then_inc(s["eoT_ready"], 1)

            def nx_evac(g):
                dve.wait_ge(s["nx_done"], g + 1)
                V.tensor_tensor(nxr[:, :], P[5][0:GT, 256:512], brow_s[0:GT, NXB, :], ALU.add).then_inc(s["nx_sum"], 1)

            def h2_norm(g):
                dve.wait_ge(s["nx_gelu"], g + 1)
                link(V.tensor_tensor(h[:, g, :], h[:, g, :], nxr[:, :], ALU.add))
                norm(h[:, g, :], x2[:, g % 2, :], "x2_ready")

            def z_evac(g):
                dve.wait_ge(s["qk1_done"], g + 1)
                for w, dst in ((0, q1), (1, kz)):
                    for c in range(DC):
                        b = (BQ1, BK1)[w] + c
                        last = V.tensor_scalar(dst[:, c, gcol(g)], bank(6, 4, GT)[:, 2 * w + c, :], bcol_s[:, b:b + 1], None, ALU.add)
                last.then_inc(s["z1_ready"], 1)
                dve.wait_ge(s["z1_ready"], g + 1)
                V.tensor_scalar_min(kE[:, :, gcol(g)], q1[:, :, gcol(g)], 0.0)
                V.tensor_scalar_min(kO[:, :, gcol(g)], kz[:, :, gcol(g)], 0.0).then_inc(s["m1_ready"], 1)

            def v_evac(g):
                dve.wait_ge(s["v1_done"], g + 1)
                if g == 0:
                    dve.wait_ge(s["vpad_zero"], 1)
                V.tensor_tensor(vpad[0:GT, g, :, 0:HD], P[7][0:GT, 0:D].rearrange("p (h m) -> p h m", m=HD),
                                brow_s[0:GT, BV1, :].rearrange("p (h m) -> p h m", m=HD), ALU.add).then_inc(s["v1_ready"], 1)

            lagged(GROUPS + 3, [(nx_evac, 2), (xa_evac, 1), (h2_norm, 2), (h1_norms, 0), (z_evac, 3), (v_evac, 3), (eo_evac, 1)])

            def elu1(g):
                dve.wait_ge(s["exp1_done"], g + 1)
                for e, src in ((kE, q1), (kO, kz)):
                    last = V.scalar_tensor_tensor(src[:, :, gcol(g)], src[:, :, gcol(g)], 0.0, e[:, :, gcol(g)], ALU.max, ALU.add)
                last.then_inc(s["q1_ready"], 1)
                dve.wait_ge(s["q1_ready"], g + 1)
                if g >= 1:
                    dve.wait_ge(s["den_done"], g)
                for c in range(DC):
                    last = V.tensor_tensor_scan(qz[:, c, :], masks[:, 128 + GT:128 + 2 * GT], kz[:, c, gcol(g)], 0.0, ALU.mult, ALU.add)
                last.then_inc(s["z_scan"], 1)
                dve.wait_ge(s["z_scan"], g + 1)
                V.tensor_tensor(qz[:, :, :], qz[:, :, :], q1[:, :, gcol(g)], ALU.mult).then_inc(s["qz_ready"], 1)

            def norm_q(g):
                dve.wait_ge(s["den_done"], g + 1)
                V.tensor_scalar_add(rden[:, :, :], bank(5, DC, GT), 1e-6).then_inc(s["den_read"], 1)
                dve.wait_ge(s["den_read"], g + 1)
                link(V.reciprocal(rden[:, :, :], rden[:, :, :]))
                V.tensor_tensor(q1[:, :, gcol(g)], q1[:, :, gcol(g)], rden[:, :, :], ALU.mult).then_inc(s["qn_ready"], 1)

            def mask_scores(g):
                dve.wait_ge(s["sc_done"], g + 1)
                if g == 1:
                    dve.wait_ge(s["written"], 16 * UNROLL)
                if g >= 2:
                    dve.wait_ge(s["av_done"], g - 1)
                causal = masks[0:GT, 128:128 + GT].unsqueeze(1).to_broadcast([GT, 4, GT])
                for r in range(4):
                    dst = S[0:GT, g % 2, r * 4 * GT:(r + 1) * 4 * GT].rearrange("p (a t) -> p a t", a=4)
                    V.tensor_tensor(dst, bank(r, 4, GT)[0:GT, :, :], causal, ALU.mult).then_inc(s["sc_ready"], 1)

            def h3_norm(g):
                dve.wait_ge(s["wo1_done"], g + 1)
                link(V.tensor_tensor(xr[:, 0, :], P[6][0:GT, 0:D], brow_s[0:GT, BO1, :], ALU.add))
                V.tensor_tensor(h[:, g, :], h[:, g, :], xr[:, 0, :], ALU.add).then_inc(s["h0_ready"], 1)
                dve.wait_ge(s["h0_ready"], 2 * GROUPS + g + 1)
                norm(h[:, g, :], x3[0:GT, g, :], "x3_ready")

            lagged(GROUPS + 4, [(mask_scores, 3), (elu1, 0), (norm_q, 1), (h3_norm, 4)])

            logits = P[5][0:GT, 0:256].rearrange("p (g e) -> p g e", e=EXPERTS)
            iota = route[0:GT, C_IOTA:C_IOTA + EXPERTS].unsqueeze(1).to_broadcast([GT, GROUPS, EXPERTS])
            dve.wait_ge(s["lg_done"], GROUPS)
            dve.wait_ge(s["route_in"], 32)
            V.memset(kcol, 0.0)
            V.tensor_copy(spill[:, :], route[:, C_SPILL:C_SPILL + 2]).then_inc(s["ids_done"], 3 * UNROLL)

            def per_group(col):
                return lgm[:, col * GROUPS:(col + 1) * GROUPS].unsqueeze(2).to_broadcast([GT, GROUPS, EXPERTS])

            V.tensor_reduce(lgm[:, 0:GROUPS], logits, AX.X, ALU.max).then_inc(s["topv_ready"], 1)
            dve.wait_ge(s["topv_ready"], 1)
            link(V.tensor_tensor(big[:, :, :], logits, per_group(0), ALU.is_equal))
            link(V.tensor_tensor(big[:, :, :], big[:, :, :], iota, ALU.mult))
            link(V.tensor_reduce(lgm[:, 2 * GROUPS:3 * GROUPS], big[:, :, :], AX.X, ALU.min))
            V.tensor_tensor(onehot_b[:, :, :], iota, per_group(2), ALU.is_equal).then_inc(s["onehot_ready"], 1)
            link(V.tensor_tensor(onehot[:, :, :], iota, per_group(2), ALU.is_equal))

            def hidden(n):
                m, half = n // 2, n % 2
                dve.wait_ge(s["silu0_done"], n + 1)
                V.tensor_tensor(hidT[:, m, half * HALF:(half + 1) * HALF], zA[:, n % 2, :], bank(2 + n % 2, HALF), ALU.mult)\
                    .then_inc(s["hid_ready"], 1)

            hidden(0)
            dve.wait_ge(s["score_ready"], 1)
            for g in range(GROUPS):
                last = V.tensor_scalar(x3[0:GT, g, :], x3[0:GT, g, :], lgm[:, GROUPS + g:GROUPS + g + 1], None, ALU.mult)
            last.then_inc(s["xs_scaled"], 1)
            link(V.memset(rt[:, 7, :], 0.0))
            hidden(1)
            dve.wait_ge(s["prefix_done"], 1)
            count = rt[:, 6, :]
            link(V.tensor_copy(count, P[5][:, 256:256 + EXPERTS]))
            link(V.tensor_tensor_scan(rt[:, 0, :], count, rt[:, 7, :], 0.0, ALU.add, ALU.add))
            link(V.tensor_tensor(rt[:, 1, :], rt[:, 0, :], count, ALU.subtract))
            link(V.tensor_tensor(big[:, :, :], P[4][0:GT, 0:256].rearrange("p (g e) -> p g e", e=EXPERTS), onehot[:, :, :], ALU.mult))
            rank, first, slot = (lgm[:, i * GROUPS:(i + 1) * GROUPS] for i in (3, 4, 5))
            link(V.tensor_reduce(rank, big[:, :, :], AX.X, ALU.add))

            def of_expert(dst, row):
                link(V.tensor_tensor(big[:, :, :], onehot[:, :, :], rt[0:GT, row, :].unsqueeze(1).to_broadcast([GT, GROUPS, EXPERTS]), ALU.mult))
                link(V.tensor_reduce(dst, big[:, :, :], AX.X, ALU.add))

            of_expert(first, 1)
            link(V.tensor_tensor(slot, rank, first, ALU.add))
            V.tensor_copy(slot_i[:, :], slot).then_inc(s["slot_ready"], 1)
            hidden(2)
            link(V.tensor_tensor(steps, count.unsqueeze(2).to_broadcast([128, EXPERTS, STEPS]),
                                 route[:, C_STEP:C_STEP + EXPERTS * STEPS].rearrange("p (e m) -> p e m", m=STEPS), ALU.is_gt))
            link(V.tensor_reduce(rt[:, 2, :], steps, AX.X, ALU.add))
            link(V.tensor_tensor_scan(rt[:, 3, :], rt[:, 2, :], rt[:, 7, :], 0.0, ALU.add, ALU.add))
            link(V.tensor_tensor(rt[:, 4, :], rt[:, 3, :], rt[:, 2, :], ALU.subtract))
            of_expert(first, 4)
            upto = steps[0:GT, 0:GROUPS, :]
            link(V.tensor_tensor(upto, rank.unsqueeze(2).to_broadcast([GT, GROUPS, STEPS]),
                                 route[0:GT, C_STEP:C_STEP + GROUPS * STEPS].rearrange("p (e m) -> p e m", m=STEPS), ALU.is_ge))
            link(V.tensor_reduce(slot, upto, AX.X, ALU.add))
            V.tensor_copy(idb[:, :, 0], route[0:GT, C_ID:C_ID + GROUPS])
            V.scalar_tensor_tensor(idb[:, :, 1], slot, -1.0, first, ALU.add, ALU.add).then_inc(s["xs_ready"], 1)

            hidden(3)
            at_k, rows_k = route[:, C_K:C_K + 1], route[:, C_K + 1:C_K + 2]
            link(V.tensor_scalar(rt[:, 5, :], rt[:, 4, :], float(-BLOCK), None, ALU.mult))
            link(V.tensor_tensor(rt[:, 5, :], rt[:, 5, :], rt[:, 1, :], ALU.add))
            link(V.tensor_scalar(rt[:, 0, :], rt[:, 3, :], at_k, None, ALU.is_le))
            link(V.tensor_reduce(own[:, 0:1], rt[:, 0, :], AX.X, ALU.add))
            V.tensor_scalar_min(tcol[:, 0:1], own[:, 0:1], float(EXPERTS - 1))
            link(V.tensor_scalar(rt[:, 4, :], rt[:, 4, :], at_k, None, ALU.is_le))
            link(V.tensor_tensor(rt[:, 4, :], rt[:, 4, :], rt[:, 0, :], ALU.subtract))
            link(V.tensor_tensor(rt[:, 4, :], rt[:, 4, :], rt[:, 5, :], ALU.mult))
            link(V.tensor_reduce(own[:, 1:2], rt[:, 4, :], AX.X, ALU.add))
            link(V.tensor_scalar(own[:, 1:2], own[:, 1:2], rows_k, None, ALU.add))
            V.tensor_scalar_min(tcol[:, 1:2], own[:, 1:2], float(TOKENS)).then_inc(s["blocks_ready"], 1)
            hidden(4)
            link(V.tensor_tensor(tfl[:, 0:NROUND], rt[0:1, 3, EXPERTS - 1:EXPERTS].to_broadcast([1, NROUND]), route[0:1, C_ROUND:C_ROUND + NROUND], ALU.is_gt))
            link(V.tensor_reduce(tfl[:, NROUND:NROUND + 1], tfl[:, 0:NROUND], AX.X, ALU.add))
            V.tensor_copy(table[:, 2 * MAX_BLOCKS:2 * MAX_BLOCKS + 1], tfl[:, NROUND:NROUND + 1])
            V.tensor_scalar_add(table[:, 2 * MAX_BLOCKS + 1:2 * MAX_BLOCKS + 2], tfl[:, NROUND:NROUND + 1], -1.0)
            dve.wait_ge(s["table_done"], 1)
            V.tensor_copy(table[:, 0:2 * MAX_BLOCKS], P[5][0:1, 288:288 + 2 * MAX_BLOCKS]).then_inc(s["table_ready"], 1)

            hidden(5)
            hidden(6)
            hidden(7)
            for n in ("xwT_ready", "hw_ready", "yw_ready"):
                nc.vector.engine_nop().then_inc(s[n], 2)
            more = more_rounds(dve)
            def window_cols(r, v):
                k, u = r * UNROLL + v, v % UNROLL
                dve.wait_ge(s["xwt_done"], k + 1)
                V.tensor_copy(xwT[:, u, :, :], bank((4, 7)[u % 2], DC, BLOCK)).then_inc(s["xwT_ready"], 1)

            def targets(r, u):
                k = r * UNROLL + u
                dve.wait_ge(window_in[u], 16 * (r + 1))
                dve.wait_ge(s["written"], 16 * (k + 1))
                dve.wait_ge(s["ids_done"], 3 * (k + UNROLL))
                V.tensor_tensor(mine, xw[:, u, D + 1:XROW], kcol, ALU.is_equal)
                V.tensor_scalar(where, xw[:, u, D:D + 1], spill[:, 0:1], None, ALU.add).then_inc(s["ids_done"], 1)
                dve.wait_ge(s["ids_done"], 3 * (k + UNROLL) + 1)
                V.scalar_tensor_tensor(target[:, u:u + 1], where, mine, spill[:, 1:2], ALU.mult, ALU.add).then_inc(s["ids_done"], 1)
                V.tensor_scalar_add(kcol, kcol, 1.0).then_inc(s["ids_done"], 1)

            def hidden_cols(r, v):
                k, u = r * UNROLL + v, v % UNROLL
                dve.wait_ge(s["silu_done"], k + 1)
                dve.wait_ge(s["gu_done"], 2 * (k + 1) + 1)
                dve.wait_ge(s["dn_done"], k + UNROLL - 1)
                V.tensor_tensor(hw[:, u % 2, :], sg[:, u % 2, :], P[2 + u % 2][:, :], ALU.mult).then_inc(s["hw_ready"], 1)

            def rows_out(r, u):
                k = r * UNROLL + u
                dve.wait_ge(s["dn_done"], k + UNROLL + 1)
                dve.wait_ge(s["written"], 16 * (k + 1))
                V.tensor_copy(yw[:, u, :], P[5 + u % 2][:, 0:D]).then_inc(s["yw_ready"], 1)

            for g in range(GROUPS):
                dve.wait_ge(s["sd_done"], g + 1)
                V.tensor_tensor(h[:, g, :], h[:, g, :], P[6 + g % 2][0:GT, 0:D], ALU.add).then_inc(s["h_final"], 1)
                if g == GROUPS - 2:
                    window_cols(0, 0)
            window_cols(0, 1)
            hidden_cols(0, 0)
            with dve.Fori(0, more) as r:
                for u in range(UNROLL):
                    window_cols(r, u + 2)
                    targets(r, u)
                    hidden_cols(r, u + 1)
                    rows_out(r, u)
            for u in range(UNROLL):
                if u + 2 < UNROLL:
                    window_cols(more, u + 2)
                targets(more, u)
                if u + 1 < UNROLL:
                    hidden_cols(more, u + 1)
                rows_out(more, u)

        @block.gpsimd
        def _(pool):
            nc.gpsimd.memset(zrow, 0.0).then_inc(s["tail_zero"], 1)
            pool.wait_ge(s["tail_zero"], 1)
            for j in range(2):
                part = slice(j * BLOCK // 2, (j + 1) * BLOCK // 2)
                pool.dma_start(sorted_x[TOKENS:SORTED, :][part, :], zrow[part, :]).then_inc(s["written"], 16)
                pool.dma_start(out[TOKENS:SORTED, :][part, :], zrow[part, 0:D]).then_inc(s["written"], 16)
            pool.wait_ge(s["zeroed"], 1)

            def power(n):
                pool.wait_ge(s["var_ready"], n + 1)
                nc.gpsimd.tensor_tensor(rstd[:, :], var[:, :], mhalf[:, :], ALU.pow).then_inc(s["rstd_ready"], 1)

            for n in range(GROUPS):
                power(n)
            pool.wait_ge(s["tok_done"], GROUPS)
            nc.gpsimd.memset(pat[:, :, :], 0.0).then_inc(s["vpad_zero"], 1)
            for n in range(GROUPS, 5 * GROUPS):
                power(n)

            pool.wait_ge(s["slot_ready"], 1)
            for g in range(GROUPS):
                pool.wait_ge(s["xs_ready"], 1)
                pool.indirect_dma_start(sorted_x, bass.IndirectOffsetOnAxis(ap=slot_i[:, g:g + 1], axis=0), vrow[0:GT, g, :], None)\
                    .then_inc(xs_sent[g], 16)
            for g in range(GROUPS):
                pool.wait_ge(xs_sent[g], 16)
            nc.gpsimd.memset(slot_seen[:, :], 0.0).then_inc(s["scattered"], 16 * GROUPS)

            pool.wait_ge(s["stored"], 16 * GROUPS)
            pool.wait_ge(s["table_ready"], 1)
            rounds = all_rounds(pool)
            nc.gpsimd.engine_nop().then_inc(s["turn"], 1)
            with pool.Fori(0, rounds) as r:
                for u in range(UNROLL):
                    pool.wait_ge(s["yw_ready"], r * UNROLL + u + 3)
                    pool.wait_ge(s["written"], 16 * (r * UNROLL + u + UNROLL))
                    pool.wait_ge(s["turn"], r * UNROLL + u + 1)
                    nc.gpsimd.tensor_tensor(slot_seen[:, :], slot_seen[:, :], slot_seen[:, :], ALU.add).then_inc(s["turn"], 1)
                    pool.indirect_dma_start(out, bass.IndirectOffsetOnAxis(ap=target[:, u:u + 1], axis=0),
                                            yw[:, u, :], None, compute_op=ALU.add).then_inc(s["written"], 16)
            pool.wait_ge(s["written"], 16 * UNROLL * (rounds + 1))
            pool.wait_ge(s["turn"], UNROLL * rounds + 1)
            nc.gpsimd.tensor_tensor(slot_seen[:, :], slot_seen[:, :], slot_seen[:, :], ALU.add).then_inc(s["turn"], 1)


_OUT = (SORTED, D)


def kernel(**inputs):
    import numpy as _np
    import concourse.bacc as _bacc
    from concourse import mybir as _mybir
    from concourse.bass_utils import run_bass_kernel_spmd as _run

    a = {k: _np.ascontiguousarray(v) for k, v in inputs.items()}

    def chunked(w):
        return w.reshape(-1, 128, w.shape[-1]).transpose(1, 0, 2)

    order = [16 * m + 2 * g + r for g in range(GROUPS) for m in range(2) for r in range(2)]
    x = a["x"][:, :, 0:80, 0:80].reshape(32, 3, 5, 16, 5, 16).transpose(0, 1, 3, 5, 2, 4)
    pt = x.reshape(32, 25, 768)[order]
    pt = _np.concatenate([_np.zeros((32, 1, 768), pt.dtype), pt], axis=1)
    pt = pt.reshape(GROUPS, GT, FC, 128).transpose(3, 0, 2, 1).reshape(128, GROUPS, FC * GT)

    cls = _np.zeros((GI, POSITIONS, D), _np.float32)
    cls[:, 0] = a["cls_tok"].reshape(1, D)
    cls = cls.reshape(GT, D)

    wo1 = _np.zeros((HEADS, HPAD, D), _np.float32)
    wo1[:, :HD] = a["L1_attn_Wo"].reshape(HEADS, HD, D)
    heads = [[8 * (b // 2) + 2 * r + b % 2 for r in range(4)] for b in range(4)]
    wo1 = _np.stack([wo1[hs].reshape(128, D) for hs in heads], axis=1)

    def col(v):
        return v.reshape(-1, 128).T

    parity = (_np.arange(128) // HD) % 2
    bcol = _np.concatenate([
        col(a["L0_attn_bq"]), col(a["L0_attn_bk"]), col(a["L0_ffn_ln_scale"]), col(a["L0_ffn_ln_bias"]),
        col(a["L0_ffn_attn_b"]), col(a["L1_attn_bq"]), col(a["L1_attn_bk"]), col(a["L0_ffn_b2"]), col(a["L0_ffn_b1"]),
        (parity == 0)[:, None], (parity == 1)[:, None]], axis=1).astype(_np.float32)
    brow = _np.stack([a["L0_attn_bv"], a["L0_attn_bo"], a["L0_ffn_next_b"], a["L1_attn_bv"], a["L1_attn_bo"]])
    p = _np.arange(128)
    masks = _np.zeros((128, 256 + 2 * GT), _np.float32)
    masks[:, 128 + 2 * GT:] = p[:, None] // HD == p[None] // HD
    masks[:, :128] = p[:, None] // IMAGES == p[None] // IMAGES
    t = _np.arange(GT)
    masks[:, 128 + GT:128 + 2 * GT] = t % POSITIONS != 0
    masks[:GT, 128:128 + GT] = (t[:, None] // POSITIONS == t[None] // POSITIONS) & (t[:, None] <= t[None])
    tri = _np.ones((GT, GT + 128), _np.float32)
    tri[:, :GT] = t[:, None] < t[None]
    route = _np.zeros((128, NROUTE), _np.float32)
    route[:, C_IOTA:C_IOTA + EXPERTS] = _np.arange(EXPERTS) - 64
    route[:, C_K] = p
    route[:, C_K + 1] = BLOCK * p
    route[:, C_STEP:C_STEP + EXPERTS * STEPS] = _np.tile(BLOCK * _np.arange(STEPS), EXPERTS)
    route[:, C_ROUND:C_ROUND + NROUND] = UNROLL * _np.arange(NROUND)
    route[:GT, C_ID:C_ID + GROUPS] = GT * _np.arange(GROUPS)[None] + t[:, None]
    spill = TOKENS + p
    route[:, C_SPILL] = -spill
    route[:, C_SPILL + 1] = spill

    def experts(gw, uw, dw):
        n = gw.shape[0]
        parts = [w.reshape(n, -1, 128, w.shape[-1]).transpose(0, 2, 1, 3).reshape(n, 128, -1) for w in (gw, uw, dw) if w is not None]
        return _np.concatenate(parts, axis=2)

    feeds = {
        "patches": pt, "cls": cls, "tokw": chunked(a["L0_tok_W"]),
        "w0": _np.stack([chunked(a[f"L0_attn_W{n}"].T) for n in "qkvo"], axis=1),
        "wx": _np.stack([chunked(a["L0_ffn_attn_w"].T), chunked(a["L0_ffn_next_w"].T)], axis=1),
        "w1a": _np.stack([chunked(a[f"L1_attn_W{n}"]) for n in "qkv"], axis=1), "w1o": wo1,
        "gate": chunked(a["L1_ffn_gate_w"]),
        "shared": experts(a["L1_ffn_shared_gate_w"][None], a["L1_ffn_shared_up_w"][None], a["L1_ffn_shared_down_w"][None])[0],
        "experts0": experts(a["L0_ffn_w1"], None, a["L0_ffn_w2"]),
        "experts1": experts(a["L1_ffn_routed_gate_w"], a["L1_ffn_routed_up_w"], a["L1_ffn_routed_down_w"]),
        "bcol": bcol, "brow": brow, "ident_in": _np.eye(128, dtype=_np.float32), "masks_in": masks,
        "tri_in": tri.astype(_mybir.dt.np(BF16)), "route_in": route,
    }
    nc = _bacc.Bacc("TRN2", target_bir_lowering=False, num_devices=1)
    arrays, args = {}, []
    for name, v in feeds.items():
        v = _np.ascontiguousarray(v)
        arrays[f"{name}_dram"] = v
        args.append(nc.dram_tensor(f"{name}_dram", v.shape, _mybir.dt.from_np(v.dtype), kind="ExternalInput").ap())
    args.append(nc.dram_tensor("out_dram", _OUT, F32, kind="ExternalOutput").ap())
    tower(nc, *args)
    r = _run(nc, [arrays], core_ids=[0])
    got = _np.asarray(r.results[0]["out_dram"])[:TOKENS].reshape(IMAGES, POSITIONS, D)
    inverse = _np.argsort(order)
    return got[inverse]
```
